# Optimizing a Trainium2 kernel written in Bass

```python
import numpy as np
import jax
import jax.numpy as jnp

def _softmax(x, axis=-1):
    return jax.nn.softmax(x, axis=axis)

def _gelu(x):
    return jax.nn.gelu(x, approximate=True)

def _silu(x):
    return jax.nn.silu(x)

def _sigmoid(x):
    return jax.nn.sigmoid(x)

def _layernorm(x, axis=-1, eps=1e-05):
    m = jnp.mean(x, axis=axis, keepdims=True)
    v = jnp.var(x, axis=axis, keepdims=True)
    return (x - m) / jnp.sqrt(v + eps)

def _scatter_add(tgt, idx, src, axis=0):
    return tgt.at[idx].add(src)

def _segment_sum(src, seg, n):
    return jax.ops.segment_sum(src, seg, n)
kernel_name = 'mk_adaln_attn_ffn_d2_seqx_r4_74af43'

def setup_inputs(seed: int=0):
    np.random.seed(seed)
    _w = jnp.asarray

    def _rec_inputs():
        import jax
        import jax.numpy as jnp
        _rk = jax.random.key(seed)
        x = -0.000125 + 0.9999 * jax.random.normal(jax.random.fold_in(_rk, 1), (4, 512, 512), jnp.float32)
        _lenS = 512 - jax.random.randint(jax.random.fold_in(_rk, 7), (4,), 0, max(1, 512 // 4) + 1, jnp.int32)
        _lenS2 = 512 - jax.random.randint(jax.random.fold_in(_rk, 8), (4,), 0, max(1, 512 // 4) + 1, jnp.int32)
        fside_BxSxS_0 = -1.52775e-05 + 0.999936 * jax.random.normal(jax.random.fold_in(_rk, 11), (4, 512, 512), jnp.float32)
        cond_512 = -5.03954e-05 + 1.00559 * jax.random.normal(jax.random.fold_in(_rk, 12), (4, 128), jnp.float32)
        return (x, fside_BxSxS_0, cond_512)
    x, fside_BxSxS_0, cond_512 = _rec_inputs()

    def _L0_cond_setup():
        import jax, jax.numpy as jnp
        from jax import lax
        import numpy as np
        B, T, C, TD = (8, 512, 512, 128)

        def _bi_wkv(r, k, v, w, u, time_emb):
            tf = jax.nn.sigmoid(jnp.sum(time_emb, axis=-1))[:, None, None]
            decay = jnp.exp(-jnp.exp(w.astype(jnp.float32)))[None, :] * (0.5 + 0.5 * tf[:, :, 0])
            kf = k.astype(jnp.float32)
            vf = v.astype(jnp.float32)
            ek = jnp.exp(jnp.minimum(kf, 30.0))
            ekv = ek * vf

            def step(carry, x):
                a, b = carry
                ekv_t, ek_t = x
                a = a * decay + ekv_t
                b = b * decay + ek_t
                return ((a, b), (a, b))
            ekv_t = jnp.swapaxes(ekv, 0, 1)
            ek_t = jnp.swapaxes(ek, 0, 1)
            init = (jnp.zeros_like(decay), jnp.zeros_like(decay))
            _, (nf, df) = lax.scan(step, init, (ekv_t, ek_t))
            _, (nb, db) = lax.scan(step, init, (ekv_t, ek_t), reverse=True)
            nf = jnp.swapaxes(nf, 0, 1)
            df = jnp.swapaxes(df, 0, 1)
            nb = jnp.swapaxes(nb, 0, 1)
            db = jnp.swapaxes(db, 0, 1)
            euk = jnp.exp(jnp.minimum(u.astype(jnp.float32)[None, None, :] + kf, 30.0))
            num = nf + nb - ekv + euk * vf
            den = df + db - ek + euk
            base = jax.nn.sigmoid(r.astype(jnp.float32)) * (num / jnp.maximum(den, 1e-08))
            out = base * (0.8 + 0.2 * tf)
            return out.astype(r.dtype)
        key = jax.random.key(seed)
        ks = jax.random.split(key, 6)
        return {'r': jax.random.normal(ks[0], (B, T, C), dtype=jnp.float32), 'k': jax.random.normal(ks[1], (B, T, C), dtype=jnp.float32), 'v': jax.random.normal(ks[2], (B, T, C), dtype=jnp.float32), 'w': jax.random.normal(ks[3], (C,), dtype=jnp.float32), 'u': jax.random.normal(ks[4], (C,), dtype=jnp.float32), 'time_emb': jax.random.normal(ks[5], (B, TD), dtype=jnp.float32)}
    _L0_cond_all = _L0_cond_setup()
    _L0_cond_in = {k: v for k, v in _L0_cond_all.items() if k in ('w', 'u')}
    del _L0_cond_all

    def _L0_attn_setup():
        import jax, jax.numpy as jnp
        import numpy as np
        D_MODEL = 512
        D_STATE = 128
        D_CONV = 4
        EXPAND = 2
        HEADDIM = 64
        NGROUPS = 1
        CHUNK = 64
        D_INNER = EXPAND * D_MODEL
        NHEADS = D_INNER // HEADDIM
        HG = NHEADS // NGROUPS
        CONV_DIM = D_INNER + 2 * NGROUPS * D_STATE
        D_IN_PROJ = 2 * D_INNER + 2 * NGROUPS * D_STATE + NHEADS
        BATCH = 2
        SEQLEN = 512
        EPS = 1e-05

        def _mamba2(u, in_proj_w, conv_w, conv_b, dt_bias, A_log, D_skip, norm_w, out_proj_w):
            b, l, _ = u.shape
            nc = l // CHUNK
            zxbcdt = u @ in_proj_w.T
            z = zxbcdt[..., :D_INNER]
            xBC = zxbcdt[..., D_INNER:D_INNER + CONV_DIM]
            dt = jax.nn.softplus(zxbcdt[..., D_INNER + CONV_DIM:] + dt_bias)
            xp = jnp.pad(xBC, ((0, 0), (D_CONV - 1, 0), (0, 0)))
            conv = conv_b + sum((conv_w[:, k] * xp[:, k:k + l, :] for k in range(D_CONV)))
            xBC = jax.nn.silu(conv)
            x = xBC[..., :D_INNER].reshape(b, l, NHEADS, HEADDIM)
            Bm = xBC[..., D_INNER:D_INNER + NGROUPS * D_STATE].reshape(b, l, NGROUPS, D_STATE)
            Cm = xBC[..., D_INNER + NGROUPS * D_STATE:].reshape(b, l, NGROUPS, D_STATE)
            A = -jnp.exp(A_log)
            xc = x.reshape(b, nc, CHUNK, NGROUPS, HG, HEADDIM)
            dtc = dt.reshape(b, nc, CHUNK, NGROUPS, HG)
            Bc = Bm.reshape(b, nc, CHUNK, NGROUPS, D_STATE)
            Cc = Cm.reshape(b, nc, CHUNK, NGROUPS, D_STATE)
            dA = jnp.transpose(dtc * A.reshape(NGROUPS, HG), (0, 3, 4, 1, 2))
            dA_cs = jnp.cumsum(dA, axis=-1)
            seg = dA_cs[..., :, None] - dA_cs[..., None, :]
            tri = jnp.tril(jnp.ones((CHUNK, CHUNK), bool))
            Lmat = jnp.where(tri, jnp.exp(seg), 0.0)
            xdt = xc * dtc[..., None]
            CB = jnp.einsum('bclgn,bcsgn->bcgls', Cc, Bc)
            Y_diag = jnp.einsum('bcgls,bgHcls,bcsgHp->bclgHp', CB, Lmat, xdt)
            decay_states = jnp.exp(dA_cs[..., -1:] - dA_cs)
            states = jnp.einsum('bcsgn,bgHcs,bcsgHp->bcgHpn', Bc, decay_states, xdt)
            chunk_decay = jnp.exp(dA_cs[..., -1])

            def step(carry, inp):
                st, dec = inp
                return (carry * dec[..., None, None] + st, carry)
            _, prev = jax.lax.scan(step, jnp.zeros_like(states[:, 0]), (jnp.moveaxis(states, 1, 0), jnp.moveaxis(chunk_decay, -1, 0)))
            prev = jnp.moveaxis(prev, 0, 1)
            Y_off = jnp.einsum('bclgn,bcgHpn,bgHcl->bclgHp', Cc, prev, jnp.exp(dA_cs))
            y = (Y_diag + Y_off).reshape(b, l, NHEADS, HEADDIM) + x * D_skip[None, None, :, None]
            y = y.reshape(b, l, D_INNER)
            y = y * jax.nn.silu(z)
            yg = y.reshape(b, l, NGROUPS, D_INNER // NGROUPS)
            yg = yg * jax.lax.rsqrt(jnp.mean(yg * yg, axis=-1, keepdims=True) + EPS)
            y = yg.reshape(b, l, D_INNER) * norm_w
            return y @ out_proj_w.T
        ks = jax.random.split(jax.random.key(seed), 8)
        u = jax.random.normal(ks[0], (BATCH, SEQLEN, D_MODEL), jnp.float32)
        in_proj_w = jax.random.normal(ks[1], (D_IN_PROJ, D_MODEL), jnp.float32) * D_MODEL ** (-0.5)
        conv_w = jax.random.normal(ks[2], (CONV_DIM, D_CONV), jnp.float32) * D_CONV ** (-0.5)
        conv_b = jax.random.normal(ks[3], (CONV_DIM,), jnp.float32) * 0.1
        dt = jnp.exp(jax.random.uniform(ks[4], (NHEADS,), jnp.float32) * (np.float32(np.log(0.1)) - np.float32(np.log(0.001))) + np.float32(np.log(0.001)))
        dt = jnp.clip(dt, 0.0001, None)
        dt_bias = dt + jnp.log(-jnp.expm1(-dt))
        A_log = jnp.log(jax.random.uniform(ks[5], (NHEADS,), jnp.float32, minval=1.0, maxval=16.0))
        D_skip = jnp.ones((NHEADS,), jnp.float32)
        norm_w = jnp.ones((D_INNER,), jnp.float32)
        out_proj_w = jax.random.normal(ks[6], (D_MODEL, D_INNER), jnp.float32) * D_INNER ** (-0.5)
        return dict(u=u, in_proj_w=in_proj_w, conv_w=conv_w, conv_b=conv_b, dt_bias=dt_bias, A_log=A_log, D_skip=D_skip, norm_w=norm_w, out_proj_w=out_proj_w)
    _L0_attn_all = _L0_attn_setup()
    _L0_attn_in = {k: v for k, v in _L0_attn_all.items() if k in ('in_proj_w', 'conv_w', 'conv_b', 'dt_bias', 'A_log', 'D_skip', 'norm_w', 'out_proj_w')}
    del _L0_attn_all

    def _L0_cond2_setup():
        import jax, jax.numpy as jnp
        from jax import lax
        import numpy as np
        B, T, C, TD = (8, 512, 512, 128)

        def _bi_wkv(r, k, v, w, u, time_emb):
            tf = jax.nn.sigmoid(jnp.sum(time_emb, axis=-1))[:, None, None]
            decay = jnp.exp(-jnp.exp(w.astype(jnp.float32)))[None, :] * (0.5 + 0.5 * tf[:, :, 0])
            kf = k.astype(jnp.float32)
            vf = v.astype(jnp.float32)
            ek = jnp.exp(jnp.minimum(kf, 30.0))
            ekv = ek * vf

            def step(carry, x):
                a, b = carry
                ekv_t, ek_t = x
                a = a * decay + ekv_t
                b = b * decay + ek_t
                return ((a, b), (a, b))
            ekv_t = jnp.swapaxes(ekv, 0, 1)
            ek_t = jnp.swapaxes(ek, 0, 1)
            init = (jnp.zeros_like(decay), jnp.zeros_like(decay))
            _, (nf, df) = lax.scan(step, init, (ekv_t, ek_t))
            _, (nb, db) = lax.scan(step, init, (ekv_t, ek_t), reverse=True)
            nf = jnp.swapaxes(nf, 0, 1)
            df = jnp.swapaxes(df, 0, 1)
            nb = jnp.swapaxes(nb, 0, 1)
            db = jnp.swapaxes(db, 0, 1)
            euk = jnp.exp(jnp.minimum(u.astype(jnp.float32)[None, None, :] + kf, 30.0))
            num = nf + nb - ekv + euk * vf
            den = df + db - ek + euk
            base = jax.nn.sigmoid(r.astype(jnp.float32)) * (num / jnp.maximum(den, 1e-08))
            out = base * (0.8 + 0.2 * tf)
            return out.astype(r.dtype)
        key = jax.random.key(seed)
        ks = jax.random.split(key, 6)
        return {'r': jax.random.normal(ks[0], (B, T, C), dtype=jnp.float32), 'k': jax.random.normal(ks[1], (B, T, C), dtype=jnp.float32), 'v': jax.random.normal(ks[2], (B, T, C), dtype=jnp.float32), 'w': jax.random.normal(ks[3], (C,), dtype=jnp.float32), 'u': jax.random.normal(ks[4], (C,), dtype=jnp.float32), 'time_emb': jax.random.normal(ks[5], (B, TD), dtype=jnp.float32)}
    _L0_cond2_all = _L0_cond2_setup()
    _L0_cond2_in = {k: v for k, v in _L0_cond2_all.items() if k in ('w', 'u')}
    del _L0_cond2_all

    def _L0_ffn_setup():
        import jax, jax.numpy as jnp
        import numpy as np
        NUM_EXPERTS = 8
        TOP_K = 2
        key = jax.random.key(seed)
        ks = jax.random.split(key, 7)
        B, S, H, I, E = (4, 512, 512, 512, NUM_EXPERTS)
        sc = 0.02
        return {'hidden_states': jax.random.normal(ks[0], (B, S, H), dtype=jnp.float32), 'gate_w': jax.random.normal(ks[1], (E, H), dtype=jnp.float32) * sc, 'gate_b': jax.random.normal(ks[2], (E,), dtype=jnp.float32) * sc, 'w1': jax.random.normal(ks[3], (E, 2 * I, H), dtype=jnp.float32) * sc, 'b1': jax.random.normal(ks[4], (E, 2 * I), dtype=jnp.float32) * sc, 'w2': jax.random.normal(ks[5], (E, H, I), dtype=jnp.float32) * sc, 'b2': jax.random.normal(ks[6], (E, H), dtype=jnp.float32) * sc}
    _L0_ffn_all = _L0_ffn_setup()
    _L0_ffn_in = {k: v for k, v in _L0_ffn_all.items() if k in ('gate_w', 'gate_b', 'w1', 'b1', 'w2', 'b2')}
    del _L0_ffn_all

    def _L1_cond_setup():
        import jax, jax.numpy as jnp
        from jax import lax
        import numpy as np
        B, T, C, TD = (8, 512, 512, 128)

        def _bi_wkv(r, k, v, w, u, time_emb):
            tf = jax.nn.sigmoid(jnp.sum(time_emb, axis=-1))[:, None, None]
            decay = jnp.exp(-jnp.exp(w.astype(jnp.float32)))[None, :] * (0.5 + 0.5 * tf[:, :, 0])
            kf = k.astype(jnp.float32)
            vf = v.astype(jnp.float32)
            ek = jnp.exp(jnp.minimum(kf, 30.0))
            ekv = ek * vf

            def step(carry, x):
                a, b = carry
                ekv_t, ek_t = x
                a = a * decay + ekv_t
                b = b * decay + ek_t
                return ((a, b), (a, b))
            ekv_t = jnp.swapaxes(ekv, 0, 1)
            ek_t = jnp.swapaxes(ek, 0, 1)
            init = (jnp.zeros_like(decay), jnp.zeros_like(decay))
            _, (nf, df) = lax.scan(step, init, (ekv_t, ek_t))
            _, (nb, db) = lax.scan(step, init, (ekv_t, ek_t), reverse=True)
            nf = jnp.swapaxes(nf, 0, 1)
            df = jnp.swapaxes(df, 0, 1)
            nb = jnp.swapaxes(nb, 0, 1)
            db = jnp.swapaxes(db, 0, 1)
            euk = jnp.exp(jnp.minimum(u.astype(jnp.float32)[None, None, :] + kf, 30.0))
            num = nf + nb - ekv + euk * vf
            den = df + db - ek + euk
            base = jax.nn.sigmoid(r.astype(jnp.float32)) * (num / jnp.maximum(den, 1e-08))
            out = base * (0.8 + 0.2 * tf)
            return out.astype(r.dtype)
        key = jax.random.key(seed)
        ks = jax.random.split(key, 6)
        return {'r': jax.random.normal(ks[0], (B, T, C), dtype=jnp.float32), 'k': jax.random.normal(ks[1], (B, T, C), dtype=jnp.float32), 'v': jax.random.normal(ks[2], (B, T, C), dtype=jnp.float32), 'w': jax.random.normal(ks[3], (C,), dtype=jnp.float32), 'u': jax.random.normal(ks[4], (C,), dtype=jnp.float32), 'time_emb': jax.random.normal(ks[5], (B, TD), dtype=jnp.float32)}
    _L1_cond_all = _L1_cond_setup()
    _L1_cond_in = {k: v for k, v in _L1_cond_all.items() if k in ('w', 'u')}
    del _L1_cond_all

    def _L1_attn_setup():
        import jax, jax.numpy as jnp
        import numpy as np
        B, SQ, HIDDEN = (2, 512, 512)
        HEADS, GROUPS, KVC = (16, 4, 128)
        HPG = HEADS // GROUPS
        LAYER_INDEX = 1
        SCALE = KVC ** (-0.5)
        key = jax.random.key(seed)
        k1, k2, k3, k4 = jax.random.split(key, 4)
        return {'x': jax.random.normal(k1, (B, SQ, HIDDEN), jnp.float32), 'w_q': jax.random.normal(k2, (HIDDEN, HEADS * KVC), jnp.float32) * 0.02, 'w_kv': jax.random.normal(k3, (HIDDEN, 2 * GROUPS * KVC), jnp.float32) * 0.02, 'w_dense': jax.random.normal(k4, (HEADS * KVC, HIDDEN), jnp.float32) * 0.02}
    _L1_attn_all = _L1_attn_setup()
    _L1_attn_in = {k: v for k, v in _L1_attn_all.items() if k in ('w_q', 'w_kv', 'w_dense')}
    del _L1_attn_all

    def _L1_cond2_setup():
        import jax, jax.numpy as jnp
        from jax import lax
        import numpy as np
        B, T, C, TD = (8, 512, 512, 128)

        def _bi_wkv(r, k, v, w, u, time_emb):
            tf = jax.nn.sigmoid(jnp.sum(time_emb, axis=-1))[:, None, None]
            decay = jnp.exp(-jnp.exp(w.astype(jnp.float32)))[None, :] * (0.5 + 0.5 * tf[:, :, 0])
            kf = k.astype(jnp.float32)
            vf = v.astype(jnp.float32)
            ek = jnp.exp(jnp.minimum(kf, 30.0))
            ekv = ek * vf

            def step(carry, x):
                a, b = carry
                ekv_t, ek_t = x
                a = a * decay + ekv_t
                b = b * decay + ek_t
                return ((a, b), (a, b))
            ekv_t = jnp.swapaxes(ekv, 0, 1)
            ek_t = jnp.swapaxes(ek, 0, 1)
            init = (jnp.zeros_like(decay), jnp.zeros_like(decay))
            _, (nf, df) = lax.scan(step, init, (ekv_t, ek_t))
            _, (nb, db) = lax.scan(step, init, (ekv_t, ek_t), reverse=True)
            nf = jnp.swapaxes(nf, 0, 1)
            df = jnp.swapaxes(df, 0, 1)
            nb = jnp.swapaxes(nb, 0, 1)
            db = jnp.swapaxes(db, 0, 1)
            euk = jnp.exp(jnp.minimum(u.astype(jnp.float32)[None, None, :] + kf, 30.0))
            num = nf + nb - ekv + euk * vf
            den = df + db - ek + euk
            base = jax.nn.sigmoid(r.astype(jnp.float32)) * (num / jnp.maximum(den, 1e-08))
            out = base * (0.8 + 0.2 * tf)
            return out.astype(r.dtype)
        key = jax.random.key(seed)
        ks = jax.random.split(key, 6)
        return {'r': jax.random.normal(ks[0], (B, T, C), dtype=jnp.float32), 'k': jax.random.normal(ks[1], (B, T, C), dtype=jnp.float32), 'v': jax.random.normal(ks[2], (B, T, C), dtype=jnp.float32), 'w': jax.random.normal(ks[3], (C,), dtype=jnp.float32), 'u': jax.random.normal(ks[4], (C,), dtype=jnp.float32), 'time_emb': jax.random.normal(ks[5], (B, TD), dtype=jnp.float32)}
    _L1_cond2_all = _L1_cond2_setup()
    _L1_cond2_in = {k: v for k, v in _L1_cond2_all.items() if k in ('w', 'u')}
    del _L1_cond2_all

    def _L1_ffn_setup():
        import jax, jax.numpy as jnp
        import numpy as np
        HIDDEN = 512
        INTER = 1408
        B, S = (2, 512)

        def _ternary(key, shape):
            return jax.random.randint(key, shape, -1, 2).astype(jnp.float32)
        key = jax.random.key(seed)
        ks = jax.random.split(key, 7)
        x = jax.random.normal(ks[0], (B, S, HIDDEN), dtype=jnp.float32)
        gate_w = _ternary(ks[1], (INTER, HIDDEN))
        up_w = _ternary(ks[2], (INTER, HIDDEN))
        down_w = _ternary(ks[3], (HIDDEN, INTER))
        gate_s = jax.random.uniform(ks[4], (INTER,), minval=0.01, maxval=0.1, dtype=jnp.float32)
        up_s = jax.random.uniform(ks[5], (INTER,), minval=0.01, maxval=0.1, dtype=jnp.float32)
        down_s = jax.random.uniform(ks[6], (HIDDEN,), minval=0.01, maxval=0.1, dtype=jnp.float32)
        return {'x': x, 'gate_w': gate_w, 'up_w': up_w, 'down_w': down_w, 'gate_s': gate_s, 'up_s': up_s, 'down_s': down_s}
    _L1_ffn_all = _L1_ffn_setup()
    _L1_ffn_in = {k: v for k, v in _L1_ffn_all.items() if k in ('gate_w', 'up_w', 'down_w', 'gate_s', 'up_s', 'down_s')}
    del _L1_ffn_all
    return {'x': x, 'fside_BxSxS_0': fside_BxSxS_0, 'cond_512': cond_512, 'L0_cond_w': _L0_cond_in['w'], 'L0_cond_u': _L0_cond_in['u'], 'L0_attn_in_proj_w': _L0_attn_in['in_proj_w'], 'L0_attn_conv_w': _L0_attn_in['conv_w'], 'L0_attn_conv_b': _L0_attn_in['conv_b'], 'L0_attn_dt_bias': _L0_attn_in['dt_bias'], 'L0_attn_A_log': _L0_attn_in['A_log'], 'L0_attn_D_skip': _L0_attn_in['D_skip'], 'L0_attn_norm_w': _L0_attn_in['norm_w'], 'L0_attn_out_proj_w': _L0_attn_in['out_proj_w'], 'L0_cond2_w': _L0_cond2_in['w'], 'L0_cond2_u': _L0_cond2_in['u'], 'L0_ffn_gate_w': _L0_ffn_in['gate_w'], 'L0_ffn_gate_b': _L0_ffn_in['gate_b'], 'L0_ffn_w1': _L0_ffn_in['w1'], 'L0_ffn_b1': _L0_ffn_in['b1'], 'L0_ffn_w2': _L0_ffn_in['w2'], 'L0_ffn_b2': _L0_ffn_in['b2'], 'L1_cond_w': _L1_cond_in['w'], 'L1_cond_u': _L1_cond_in['u'], 'L1_attn_w_q': _L1_attn_in['w_q'], 'L1_attn_w_kv': _L1_attn_in['w_kv'], 'L1_attn_w_dense': _L1_attn_in['w_dense'], 'L1_cond2_w': _L1_cond2_in['w'], 'L1_cond2_u': _L1_cond2_in['u'], 'L1_ffn_gate_w': _L1_ffn_in['gate_w'], 'L1_ffn_up_w': _L1_ffn_in['up_w'], 'L1_ffn_down_w': _L1_ffn_in['down_w'], 'L1_ffn_gate_s': _L1_ffn_in['gate_s'], 'L1_ffn_up_s': _L1_ffn_in['up_s'], 'L1_ffn_down_s': _L1_ffn_in['down_s']}

def reference(x, fside_BxSxS_0, cond_512, L0_cond_w, L0_cond_u, L0_attn_in_proj_w, L0_attn_conv_w, L0_attn_conv_b, L0_attn_dt_bias, L0_attn_A_log, L0_attn_D_skip, L0_attn_norm_w, L0_attn_out_proj_w, L0_cond2_w, L0_cond2_u, L0_ffn_gate_w, L0_ffn_gate_b, L0_ffn_w1, L0_ffn_b1, L0_ffn_w2, L0_ffn_b2, L1_cond_w, L1_cond_u, L1_attn_w_q, L1_attn_w_kv, L1_attn_w_dense, L1_cond2_w, L1_cond2_u, L1_ffn_gate_w, L1_ffn_up_w, L1_ffn_down_w, L1_ffn_gate_s, L1_ffn_up_s, L1_ffn_down_s):
    import jax
    import jax.numpy as jnp

    def _L0_cond_ref(r, k, v, w, u, time_emb):
        import jax, jax.numpy as jnp
        from jax import lax
        import numpy as np
        B, T, C, TD = (8, 512, 512, 128)

        def _bi_wkv(r, k, v, w, u, time_emb):
            tf = jax.nn.sigmoid(jnp.sum(time_emb, axis=-1))[:, None, None]
            decay = jnp.exp(-jnp.exp(w.astype(jnp.float32)))[None, :] * (0.5 + 0.5 * tf[:, :, 0])
            kf = k.astype(jnp.float32)
            vf = v.astype(jnp.float32)
            ek = jnp.exp(jnp.minimum(kf, 30.0))
            ekv = ek * vf

            def step(carry, x):
                a, b = carry
                ekv_t, ek_t = x
                a = a * decay + ekv_t
                b = b * decay + ek_t
                return ((a, b), (a, b))
            ekv_t = jnp.swapaxes(ekv, 0, 1)
            ek_t = jnp.swapaxes(ek, 0, 1)
            init = (jnp.zeros_like(decay), jnp.zeros_like(decay))
            _, (nf, df) = lax.scan(step, init, (ekv_t, ek_t))
            _, (nb, db) = lax.scan(step, init, (ekv_t, ek_t), reverse=True)
            nf = jnp.swapaxes(nf, 0, 1)
            df = jnp.swapaxes(df, 0, 1)
            nb = jnp.swapaxes(nb, 0, 1)
            db = jnp.swapaxes(db, 0, 1)
            euk = jnp.exp(jnp.minimum(u.astype(jnp.float32)[None, None, :] + kf, 30.0))
            num = nf + nb - ekv + euk * vf
            den = df + db - ek + euk
            base = jax.nn.sigmoid(r.astype(jnp.float32)) * (num / jnp.maximum(den, 1e-08))
            out = base * (0.8 + 0.2 * tf)
            return out.astype(r.dtype)
        return _bi_wkv(r, k, v, w, u, time_emb)

    def _L0_attn_ref(u, in_proj_w, conv_w, conv_b, dt_bias, A_log, D_skip, norm_w, out_proj_w):
        import jax, jax.numpy as jnp
        import numpy as np
        D_MODEL = 512
        D_STATE = 128
        D_CONV = 4
        EXPAND = 2
        HEADDIM = 64
        NGROUPS = 1
        CHUNK = 64
        D_INNER = EXPAND * D_MODEL
        NHEADS = D_INNER // HEADDIM
        HG = NHEADS // NGROUPS
        CONV_DIM = D_INNER + 2 * NGROUPS * D_STATE
        D_IN_PROJ = 2 * D_INNER + 2 * NGROUPS * D_STATE + NHEADS
        BATCH = 2
        SEQLEN = 512
        EPS = 1e-05

        def _mamba2(u, in_proj_w, conv_w, conv_b, dt_bias, A_log, D_skip, norm_w, out_proj_w):
            b, l, _ = u.shape
            nc = l // CHUNK
            zxbcdt = u @ in_proj_w.T
            z = zxbcdt[..., :D_INNER]
            xBC = zxbcdt[..., D_INNER:D_INNER + CONV_DIM]
            dt = jax.nn.softplus(zxbcdt[..., D_INNER + CONV_DIM:] + dt_bias)
            xp = jnp.pad(xBC, ((0, 0), (D_CONV - 1, 0), (0, 0)))
            conv = conv_b + sum((conv_w[:, k] * xp[:, k:k + l, :] for k in range(D_CONV)))
            xBC = jax.nn.silu(conv)
            x = xBC[..., :D_INNER].reshape(b, l, NHEADS, HEADDIM)
            Bm = xBC[..., D_INNER:D_INNER + NGROUPS * D_STATE].reshape(b, l, NGROUPS, D_STATE)
            Cm = xBC[..., D_INNER + NGROUPS * D_STATE:].reshape(b, l, NGROUPS, D_STATE)
            A = -jnp.exp(A_log)
            xc = x.reshape(b, nc, CHUNK, NGROUPS, HG, HEADDIM)
            dtc = dt.reshape(b, nc, CHUNK, NGROUPS, HG)
            Bc = Bm.reshape(b, nc, CHUNK, NGROUPS, D_STATE)
            Cc = Cm.reshape(b, nc, CHUNK, NGROUPS, D_STATE)
            dA = jnp.transpose(dtc * A.reshape(NGROUPS, HG), (0, 3, 4, 1, 2))
            dA_cs = jnp.cumsum(dA, axis=-1)
            seg = dA_cs[..., :, None] - dA_cs[..., None, :]
            tri = jnp.tril(jnp.ones((CHUNK, CHUNK), bool))
            Lmat = jnp.where(tri, jnp.exp(seg), 0.0)
            xdt = xc * dtc[..., None]
            CB = jnp.einsum('bclgn,bcsgn->bcgls', Cc, Bc)
            Y_diag = jnp.einsum('bcgls,bgHcls,bcsgHp->bclgHp', CB, Lmat, xdt)
            decay_states = jnp.exp(dA_cs[..., -1:] - dA_cs)
            states = jnp.einsum('bcsgn,bgHcs,bcsgHp->bcgHpn', Bc, decay_states, xdt)
            chunk_decay = jnp.exp(dA_cs[..., -1])

            def step(carry, inp):
                st, dec = inp
                return (carry * dec[..., None, None] + st, carry)
            _, prev = jax.lax.scan(step, jnp.zeros_like(states[:, 0]), (jnp.moveaxis(states, 1, 0), jnp.moveaxis(chunk_decay, -1, 0)))
            prev = jnp.moveaxis(prev, 0, 1)
            Y_off = jnp.einsum('bclgn,bcgHpn,bgHcl->bclgHp', Cc, prev, jnp.exp(dA_cs))
            y = (Y_diag + Y_off).reshape(b, l, NHEADS, HEADDIM) + x * D_skip[None, None, :, None]
            y = y.reshape(b, l, D_INNER)
            y = y * jax.nn.silu(z)
            yg = y.reshape(b, l, NGROUPS, D_INNER // NGROUPS)
            yg = yg * jax.lax.rsqrt(jnp.mean(yg * yg, axis=-1, keepdims=True) + EPS)
            y = yg.reshape(b, l, D_INNER) * norm_w
            return y @ out_proj_w.T
        return _mamba2(u, in_proj_w, conv_w, conv_b, dt_bias, A_log, D_skip, norm_w, out_proj_w)

    def _L0_cond2_ref(r, k, v, w, u, time_emb):
        import jax, jax.numpy as jnp
        from jax import lax
        import numpy as np
        B, T, C, TD = (8, 512, 512, 128)

        def _bi_wkv(r, k, v, w, u, time_emb):
            tf = jax.nn.sigmoid(jnp.sum(time_emb, axis=-1))[:, None, None]
            decay = jnp.exp(-jnp.exp(w.astype(jnp.float32)))[None, :] * (0.5 + 0.5 * tf[:, :, 0])
            kf = k.astype(jnp.float32)
            vf = v.astype(jnp.float32)
            ek = jnp.exp(jnp.minimum(kf, 30.0))
            ekv = ek * vf

            def step(carry, x):
                a, b = carry
                ekv_t, ek_t = x
                a = a * decay + ekv_t
                b = b * decay + ek_t
                return ((a, b), (a, b))
            ekv_t = jnp.swapaxes(ekv, 0, 1)
            ek_t = jnp.swapaxes(ek, 0, 1)
            init = (jnp.zeros_like(decay), jnp.zeros_like(decay))
            _, (nf, df) = lax.scan(step, init, (ekv_t, ek_t))
            _, (nb, db) = lax.scan(step, init, (ekv_t, ek_t), reverse=True)
            nf = jnp.swapaxes(nf, 0, 1)
            df = jnp.swapaxes(df, 0, 1)
            nb = jnp.swapaxes(nb, 0, 1)
            db = jnp.swapaxes(db, 0, 1)
            euk = jnp.exp(jnp.minimum(u.astype(jnp.float32)[None, None, :] + kf, 30.0))
            num = nf + nb - ekv + euk * vf
            den = df + db - ek + euk
            base = jax.nn.sigmoid(r.astype(jnp.float32)) * (num / jnp.maximum(den, 1e-08))
            out = base * (0.8 + 0.2 * tf)
            return out.astype(r.dtype)
        return _bi_wkv(r, k, v, w, u, time_emb)

    def _L0_ffn_ref(hidden_states, gate_w, gate_b, w1, b1, w2, b2):
        import jax, jax.numpy as jnp
        import numpy as np
        NUM_EXPERTS = 8
        TOP_K = 2
        B, S, H = hidden_states.shape
        x = hidden_states.reshape(-1, H)
        logits = x @ gate_w.T + gate_b
        top_vals, top_idx = jax.lax.top_k(logits, TOP_K)
        routing = jax.nn.softmax(top_vals.astype(jnp.float32), axis=-1).astype(x.dtype)
        out = jnp.zeros_like(x)
        E = w1.shape[0]
        for e in range(E):
            h = x @ w1[e].T + b1[e]
            x_glu = h[:, 0::2]
            x_lin = h[:, 1::2]
            y = x_glu * jax.nn.sigmoid(1.702 * x_glu) * (x_lin + 1.0)
            ye = y @ w2[e].T + b2[e]
            we = jnp.sum(routing * (top_idx == e), axis=-1)
            out = out + ye * we[:, None]
        return out.reshape(B, S, H)

    def _L1_cond_ref(r, k, v, w, u, time_emb):
        import jax, jax.numpy as jnp
        from jax import lax
        import numpy as np
        B, T, C, TD = (8, 512, 512, 128)

        def _bi_wkv(r, k, v, w, u, time_emb):
            tf = jax.nn.sigmoid(jnp.sum(time_emb, axis=-1))[:, None, None]
            decay = jnp.exp(-jnp.exp(w.astype(jnp.float32)))[None, :] * (0.5 + 0.5 * tf[:, :, 0])
            kf = k.astype(jnp.float32)
            vf = v.astype(jnp.float32)
            ek = jnp.exp(jnp.minimum(kf, 30.0))
            ekv = ek * vf

            def step(carry, x):
                a, b = carry
                ekv_t, ek_t = x
                a = a * decay + ekv_t
                b = b * decay + ek_t
                return ((a, b), (a, b))
            ekv_t = jnp.swapaxes(ekv, 0, 1)
            ek_t = jnp.swapaxes(ek, 0, 1)
            init = (jnp.zeros_like(decay), jnp.zeros_like(decay))
            _, (nf, df) = lax.scan(step, init, (ekv_t, ek_t))
            _, (nb, db) = lax.scan(step, init, (ekv_t, ek_t), reverse=True)
            nf = jnp.swapaxes(nf, 0, 1)
            df = jnp.swapaxes(df, 0, 1)
            nb = jnp.swapaxes(nb, 0, 1)
            db = jnp.swapaxes(db, 0, 1)
            euk = jnp.exp(jnp.minimum(u.astype(jnp.float32)[None, None, :] + kf, 30.0))
            num = nf + nb - ekv + euk * vf
            den = df + db - ek + euk
            base = jax.nn.sigmoid(r.astype(jnp.float32)) * (num / jnp.maximum(den, 1e-08))
            out = base * (0.8 + 0.2 * tf)
            return out.astype(r.dtype)
        return _bi_wkv(r, k, v, w, u, time_emb)

    def _L1_attn_ref(x, w_q, w_kv, w_dense):
        import jax, jax.numpy as jnp
        import numpy as np
        B, SQ, HIDDEN = (2, 512, 512)
        HEADS, GROUPS, KVC = (16, 4, 128)
        HPG = HEADS // GROUPS
        LAYER_INDEX = 1
        SCALE = KVC ** (-0.5)
        b, sq, _ = x.shape
        sk = sq
        q = jnp.einsum('bsh,he->bse', x, w_q).reshape(b, sq, GROUPS, HPG, KVC)
        kv = jnp.einsum('bsh,he->bse', x, w_kv)
        k, v = jnp.split(kv, 2, axis=-1)
        k = k.reshape(b, sk, GROUPS, KVC)
        v = v.reshape(b, sk, GROUPS, KVC)
        scores = jnp.einsum('bqgpd,bkgd->bgqpk', q, k) * (SCALE / LAYER_INDEX)
        scores = scores.astype(jnp.float32) * LAYER_INDEX
        causal = jnp.arange(sq)[:, None] >= jnp.arange(sk)[None, :]
        scores = jnp.where(causal[None, None, :, None, :], scores, -jnp.inf)
        probs = jax.nn.softmax(scores, axis=-1).astype(x.dtype)
        ctx = jnp.einsum('bgqpk,bkgd->bqgpd', probs, v).reshape(b, sq, HEADS * KVC)
        return jnp.einsum('bse,eh->bsh', ctx, w_dense)

    def _L1_cond2_ref(r, k, v, w, u, time_emb):
        import jax, jax.numpy as jnp
        from jax import lax
        import numpy as np
        B, T, C, TD = (8, 512, 512, 128)

        def _bi_wkv(r, k, v, w, u, time_emb):
            tf = jax.nn.sigmoid(jnp.sum(time_emb, axis=-1))[:, None, None]
            decay = jnp.exp(-jnp.exp(w.astype(jnp.float32)))[None, :] * (0.5 + 0.5 * tf[:, :, 0])
            kf = k.astype(jnp.float32)
            vf = v.astype(jnp.float32)
            ek = jnp.exp(jnp.minimum(kf, 30.0))
            ekv = ek * vf

            def step(carry, x):
                a, b = carry
                ekv_t, ek_t = x
                a = a * decay + ekv_t
                b = b * decay + ek_t
                return ((a, b), (a, b))
            ekv_t = jnp.swapaxes(ekv, 0, 1)
            ek_t = jnp.swapaxes(ek, 0, 1)
            init = (jnp.zeros_like(decay), jnp.zeros_like(decay))
            _, (nf, df) = lax.scan(step, init, (ekv_t, ek_t))
            _, (nb, db) = lax.scan(step, init, (ekv_t, ek_t), reverse=True)
            nf = jnp.swapaxes(nf, 0, 1)
            df = jnp.swapaxes(df, 0, 1)
            nb = jnp.swapaxes(nb, 0, 1)
            db = jnp.swapaxes(db, 0, 1)
            euk = jnp.exp(jnp.minimum(u.astype(jnp.float32)[None, None, :] + kf, 30.0))
            num = nf + nb - ekv + euk * vf
            den = df + db - ek + euk
            base = jax.nn.sigmoid(r.astype(jnp.float32)) * (num / jnp.maximum(den, 1e-08))
            out = base * (0.8 + 0.2 * tf)
            return out.astype(r.dtype)
        return _bi_wkv(r, k, v, w, u, time_emb)

    def _L1_ffn_ref(x, gate_w, up_w, down_w, gate_s, up_s, down_s):
        import jax, jax.numpy as jnp
        import numpy as np
        HIDDEN = 512
        INTER = 1408
        B, S = (2, 512)

        def _ternary(key, shape):
            return jax.random.randint(key, shape, -1, 2).astype(jnp.float32)
        b, s, h = x.shape
        xf = x.reshape(b * s, h)
        g = jnp.einsum('th,ih->ti', xf, gate_w) * gate_s
        u = jnp.einsum('th,ih->ti', xf, up_w) * up_s
        hdn = jax.nn.silu(g) * u
        out = jnp.einsum('ti,hi->th', hdn, down_w) * down_s
        return out.reshape(b, s, -1)
    x = x + _L0_attn_ref(_L0_cond_ref(x, fside_BxSxS_0, fside_BxSxS_0, L0_cond_w, L0_cond_u, cond_512), L0_attn_in_proj_w, L0_attn_conv_w, L0_attn_conv_b, L0_attn_dt_bias, L0_attn_A_log, L0_attn_D_skip, L0_attn_norm_w, L0_attn_out_proj_w)
    x = x + _L0_ffn_ref(_L0_cond2_ref(x, fside_BxSxS_0, fside_BxSxS_0, L0_cond2_w, L0_cond2_u, cond_512), L0_ffn_gate_w, L0_ffn_gate_b, L0_ffn_w1, L0_ffn_b1, L0_ffn_w2, L0_ffn_b2)
    x = x + _L1_attn_ref(_L1_cond_ref(x, fside_BxSxS_0, fside_BxSxS_0, L1_cond_w, L1_cond_u, cond_512), L1_attn_w_q, L1_attn_w_kv, L1_attn_w_dense)
    x = x + _L1_ffn_ref(_L1_cond2_ref(x, fside_BxSxS_0, fside_BxSxS_0, L1_cond2_w, L1_cond2_u, cond_512), L1_ffn_gate_w, L1_ffn_up_w, L1_ffn_down_w, L1_ffn_gate_s, L1_ffn_up_s, L1_ffn_down_s)
    return x

_drawn_inputs = setup_inputs


def setup_inputs(seed=0):
    import zlib

    import numpy as np

    out = dict(_drawn_inputs(seed))
    spreads = {'L0_attn_D_skip': (1.0, 0.2), 'L0_attn_norm_w': (1.0, 0.2)}
    factors = {'L0_cond2_w': 3.151,
     'L0_cond2_u': 6.558,
     'L0_ffn_gate_b': 8.0,
     'L0_ffn_b1': 22.262,
     'L0_ffn_b2': 5.871,
     'L1_cond_u': 6.356,
     'L1_attn_w_q': 64.0}
    for name, (base, spread) in spreads.items():
        noise = np.random.default_rng([zlib.crc32(name.encode()), seed]).standard_normal(out[name].shape)
        drawn = base * np.exp(spread * noise) if base else spread * noise
        out[name] = jnp.asarray(drawn.astype(out[name].dtype))
    for name, factor in factors.items():
        out[name] = (out[name] * factor).astype(out[name].dtype)
    return out
```

```python
from contextlib import ExitStack

import numpy as np
import concourse.bass as bass
from concourse import mybir

F32, F32R, BF16, I32 = mybir.dt.float32, mybir.dt.float32r, mybir.dt.bfloat16, mybir.dt.int32
ALU, ACT, AX = mybir.AluOpType, mybir.ActivationFunctionType, mybir.AxisListType

P = 128
BATCH, T, C = 4, 512, 512
KC = C // P
TB = T // P
N_GATES = 4
TILES = BATCH * KC
EXP30 = float(np.exp(np.float32(30.0)))
HEADS_M, HD, D_IN = 16, 64, 1024
XC = D_IN // P
N_CONV = XC + 2
IN_COLS = 2 * D_IN + 2 * P + HEADS_M
DT_COL = 2 * D_IN + 2 * P
PAIRS = HEADS_M // 2
EPS = 1e-5
E, I_MOE = 8, 512
HALF = 2
MOE_UP, MOE_DN = KC * 512, 2 * C
MOE_W = MOE_UP + MOE_DN
GROUPS, HPG, DH = 4, 4, 128
SCALE = DH ** -0.5
A_Q, A_K, A_V, A_D = 0, KC * 512, KC * 512 + C, KC * 512 + 2 * C
ATT_W = A_D + HPG * C
FS = 11
FFN_UP, FFN_W = KC * 256, KC * 256 + C
NEG = -1e30

COLS = {}
_at = 0
for _name, _n in (("u", 16), ("w", 16), ("conv_w", 4 * N_CONV), ("conv_b", N_CONV), ("norm_w", XC), ("d_skip", XC),
                  ("b1_glu", 32), ("b1_lin", 32), ("gate_s", FS), ("up_s", FS), ("down_s", KC)):
    COLS[_name] = _at
    _at += _n
N_COLS = _at
N_ROWS = 2 * HEADS_M + E
G_PRE, G_MAMBA, G_MOE = 4, 8, 4
G_STEPS = 14


def network(nc, xT, fT, condT, cols_d, rows_d, w_in_d, w_out_d, moe_d, gw_d, b2_d, att_d, ffn_d, outT):
    g_dram = nc.dram_tensor("gates", (N_GATES * TILES, P, T), F32, kind="Internal").ap()
    x_view = xT.rearrange("(k p) n -> p k n", p=P)
    o_view = outT.rearrange("(k p) n -> p k n", p=P)
    ctx = ExitStack()
    with ctx:
        def sem(name):
            return ctx.enter_context(nc.semaphore(name))

        def sb(name, shape, dt=F32, stack=ctx):
            return stack.enter_context(nc.sbuf_tensor(name, shape, dt))

        XT = sb("XT", [P, KC, BATCH * T])
        cols = sb("cols", [P, N_COLS])
        rows = sb("rows", [P, N_ROWS])
        u_all = sb("u_all", [P, N_GATES * TILES])
        decay = sb("decay", [P, N_GATES * TILES])
        oscale = sb("oscale", [P, N_GATES * TILES])
        ident = sb("ident", [P, P])
        ident_b = sb("ident_b", [P, P], BF16)
        ones = sb("ones", [P, P])
        sel_h = sb("sel_h", [64, HEADS_M], F32R)
        causal_b = sb("causal_b", [P, P], BF16)
        bgs = sb("bgs", [P, 4 * E])
        gsh = sb("gsh", [P, FS])
        ush = sb("ush", [P, FS])
        bias_e = sb("bias_e", [P, 8])
        f_sc = sb("f_sc", [P, 2])
        nmx = sb("nmx", [P, 2, TB])
        rsum = sb("rsum", [P, 2, TB])
        rinv = sb("rinv", [P, 2, TB])
        g_v = sb("g_v", [P, 2, T])
        bank = [ctx.enter_context(nc.psum_tensor(f"bank{i}", [P, 512], F32)) for i in range(8)]

        def col(name, i):
            return cols[:, COLS[name] + i:COLS[name] + i + 1]

        with ExitStack() as s:
            condT_s = sb("condT_s", [P, BATCH], F32, s)
            tf = sb("tf", [P, BATCH], F32, s)
            fac = sb("fac", [P, BATCH], F32, s)
            osc = sb("osc", [P, BATCH], F32, s)
            dec0 = sb("dec0", [P, 16], F32, s)
        gs_ = ctx.enter_context(ExitStack())
        g_ek = sb("g_ek", [P, 2, T], F32, gs_)
        g_eu = sb("g_eu", [P, 2, T], F32, gs_)
        g_e = sb("g_e", [P, T], F32, gs_)
        g_f = sb("g_f", [P, T], F32, gs_)
        g_r = sb("g_r", [P, T], F32, gs_)
        with ExitStack() as s:
            w_in = sb("w_in", [P, KC, IN_COLS], F32, s)
            w_out = sb("w_out", [P, XC, C], F32, s)
            um = sb("um", [P, KC, T], F32, s)
            txm = sb("txm", [P, KC, T], F32, s)
            tri = sb("tri", [P, P], F32, s)
            neg4 = sb("neg4", [P, TB, P], BF16, s)
            sel_p = sb("sel_p", [64, PAIRS, P], F32R, s)
            xa = sb("xa", [P, XC, T], F32, s)
            bT = sb("bT", [P, T], F32, s)
            cT = sb("cT", [P, T], F32, s)
            b_tok = sb("b_tok", [P, TB, P], F32, s)
            cb = sb("cb", [P, TB, P], F32, s)
            xdt = sb("xdt", [P, TB, D_IN], F32, s)
            xdt2 = sb("xdt2", [P, D_IN], F32, s)
            state = sb("state", [P, TB - 1, D_IN], F32, s)
            csT = sb("csT", [64, T], F32R, s)
            lm = sb("lm", [P, 2, T], F32, s)
            e2 = sb("e2", [P, T], F32, s)
            tz = sb("tz", [P, T], F32, s)
            sq = sb("sq", [P, T], F32, s)
            ssum = sb("ssum", [P, T], F32, s)
            NB = TB * HEADS_M
            d_x, d_a, d_e, d_s, d_p, d_q, dt_t, d_A, csn, w2, w2e, dts, cdec = (
                sb(f"dt{i}", [P, NB], F32, s) for i in range(13))
            a_neg = sb("a_neg", [P, HEADS_M], F32, s)
            eps_c = sb("eps_c", [P, 1], F32, s)
        acc = [lm[:, 0, :], lm[:, 1, :]]
        cth = [e2[:, :], tz[:, :]]
        with ExitStack() as s:
            u_hi = sb("u_hi", [P, KC, BATCH * T], F32R, s)
            u_lo = sb("u_lo", [P, KC, BATCH * T], F32R, s)
            we_t = sb("we_t", [64, BATCH * T], F32R, s)
            with ExitStack() as s2:
                mw_hi = sb("mw_hi", [P, 2, MOE_W], F32R, s2)
                mw_lo = sb("mw_lo", [P, 2, MOE_W], F32R, s2)
                m_stage = sb("m_stage", [P, MOE_W // 2], F32, s2)
                b2_s = sb("b2_s", [64, C], F32, s2)
                gw = sb("gw", [P, KC, E], F32, s2)
                sel_e = sb("sel_e", [64, P], F32R, s2)
                lg, ex, gt, eq, pre, wx, rst = (sb(f"rt{i}", [P, TB, E], F32, s2) for i in range(7))
                mx8 = sb("mx8", [P, TB, 8], F32, s2)
                r4 = sb("r4", [P, 2, TB], F32, s2)
                with ExitStack() as s3:
                    uf1 = sb("uf1", [P, KC, T], F32, s3)
                    tx1 = sb("tx1", [P, KC, T], F32, s3)
                with ExitStack() as s3:
                    my_hi = sb("my_hi", [P, 2, 2, T], F32R, s3)
                    my_lo = sb("my_lo", [P, 2, 2, T], F32R, s3)
                    m_t = sb("m_t", [P, 2, T], F32, s3)
                    m_y = sb("m_y", [P, 2, T], F32, s3)
        gs_.close()
        with ExitStack() as s:
            probs = sb("probs", [P, 2, 1280], F32, s)
            vT = sb("vT", [P, T], F32, s)
            k_hi = sb("k_hi", [P, T], F32R, s)
            sb("pad_u", [P, 2, KC, BATCH * T], F32, s)
            with ExitStack() as s2:
                aw_hi = sb("aw_hi", [P, ATT_W], F32R, s2)
                aw_lo = sb("aw_lo", [P, ATT_W], F32R, s2)
                a_stage = sb("a_stage", [P, ATT_W // 2], F32, s2)
                with ExitStack() as s3:
                    uf2 = sb("uf2", [P, KC, T], F32, s3)
                    tx2 = sb("tx2", [P, KC, T], F32, s3)
                k_lo = sb("k_lo", [P, T], F32R, s2)
                v_hi = sb("v_hi", [P, TB, P], F32R, s2)
                v_lo = sb("v_lo", [P, TB, P], F32R, s2)
                q_hi = sb("q_hi", [P, 2, T], F32R, s2)
                q_lo = sb("q_lo", [P, 2, T], F32R, s2)
                pt_hi = sb("pt_hi", [P, 1280], F32R, s2)
                pt_lo = sb("pt_lo", [P, 1280], F32R, s2)
                cx_hi = sb("cx_hi", [P, HPG, T], F32R, s2)
                cx_lo = sb("cx_lo", [P, HPG, T], F32R, s2)
            with ExitStack() as s2:
                fw_hi = sb("fw_hi", [P, 2, FFN_W], F32R, s2)
                fw_lo = sb("fw_lo", [P, 2, FFN_W], F32R, s2)
                f_stage = sb("f_stage", [P, 2, FFN_W], F32, s2)
                uf3 = sb("uf3", [P, KC, T], F32, s2)
                tx3 = sb("tx3", [P, KC, T], F32, s2)
                f_hi = sb("f_hi", [P, 2, T], F32R, s2)
                f_lo = sb("f_lo", [P, 2, T], F32R, s2)
                f_t = sb("f_t", [P, T], F32, s2)
                f_u = sb("f_u", [P, T], F32, s2)
                f_y = sb("f_y", [P, T], F32, s2)

        loaded, x_loaded, w_loaded = sem("loaded"), sem("x_loaded"), sem("w_loaded")
        masks_ready, setup_step, setup_mm, setup_act = sem("masks_ready"), sem("setup_step"), sem("setup_mm"), sem("setup_act")
        g_in = [sem(f"g_in{i}") for i in range(2)]
        g_out = [sem(f"g_out{i}") for i in range(2)]
        g_exp, g_step = sem("g_exp"), sem("g_step")
        g_fetched, x_tanh, u_ready = sem("g_fetched"), sem("x_tanh"), sem("u_ready")
        u_hi_ready, u_split = sem("u_hi_ready"), sem("u_split")
        dve_step = sem("dve_step")
        dt_raw, dt_abs, dt_exp, dA_ready = sem("dt_raw"), sem("dt_abs"), sem("dt_exp"), sem("dA_ready")
        proj_done, tap0, conv_tapped, conv_tanh, act_ready = (
            sem("proj_done"), sem("tap0"), sem("conv_tapped"), sem("conv_tanh"), sem("act_ready"))
        cs_done, cs_neg, w_exp, ct_hi, ct_ready = sem("cs_done"), sem("cs_neg"), sem("w_exp"), sem("ct_hi"), sem("ct_ready")
        x_transposed, xdt_done, bc_done, bc_copied = sem("x_transposed"), sem("xdt_done"), sem("bc_done"), sem("bc_copied")
        s_done, state_done = sem("s_done"), sem("state_done")
        z_done, z_tanh, zs_done = sem("z_done"), sem("z_tanh"), sem("zs_done")
        r_done, l_done, m_ready, yy_done, y_done = sem("r_done"), sem("l_done"), sem("m_ready"), sem("yy_done"), sem("y_done")
        sq_added = sem("sq_added")
        sq_done, ssum_ready, ssq_done, rms_done, yn_ready = (
            sem("sq_done"), sem("ssum_ready"), sem("ssq_done"), sem("rms_done"), sem("yn_ready"))
        out_done, x_added = sem("out_done"), sem("x_added")
        moe_loaded = sem("moe_loaded")
        logit_done, lg_sub, lg_exp, we_ready, we_T, we_hi, we_lo = (
            sem("logit_done"), sem("lg_sub"), sem("lg_exp"), sem("we_ready"), sem("we_T"), sem("we_hi"), sem("we_lo"))
        b2_done, b2_added = sem("b2_done"), sem("b2_added")
        m_staged, mw_hi_ready, w_split = sem("m_staged"), sem("mw_hi_ready"), sem("w_split")
        sel_ready, up_done, wb_done = sem("sel_ready"), sem("up_done"), sem("wb_done")
        m_act, max_part, r_inv = sem("m_act"), sem("max_part"), sem("r_inv")
        bias_ready, f_scaled = sem("bias_ready"), sem("f_scaled")
        m_tanh, m_lin, glu_used, m_yready = sem("m_tanh"), sem("m_lin"), sem("glu_used"), sem("m_yready")
        y_hi_ready, y_split, moe_down, x_acc = sem("y_hi_ready"), sem("y_split"), sem("moe_down"), sem("x_acc")
        a_staged, aw_hi_ready, aw_split = sem("a_staged"), sem("aw_hi_ready"), sem("aw_split")
        k_done, k_hi_ready, k_split = sem("k_done"), sem("k_hi_ready"), sem("k_split")
        v_done, vt_copied, vt_done, v_hi_ready, v_split = (
            sem("v_done"), sem("vt_copied"), sem("vt_done"), sem("v_hi_ready"), sem("v_split"))
        q_done, q_hi_ready, q_split = sem("q_done"), sem("q_hi_ready"), sem("q_split")
        scores_done, max_ready, exp_done, p_ready = sem("scores_done"), sem("max_ready"), sem("exp_done"), sem("p_ready")
        t_done, pt_hi_ready, pt_split = sem("t_done"), sem("pt_hi_ready"), sem("pt_split")
        c_done, c_hi_ready, c_split = sem("c_done"), sem("c_hi_ready"), sem("c_split")
        dense_done, ax_acc = sem("dense_done"), sem("ax_acc")
        f_staged = [sem(f"f_staged{i}") for i in range(2)]
        fw_hi_ready, fw_split = sem("fw_hi_ready"), sem("fw_split")
        f_up, f_tanh, f_lin, f_used, f_yready, f_hi_ready, f_split, f_down, fx_acc = (
            sem("f_up"), sem("f_tanh"), sem("f_lin"), sem("f_used"), sem("f_yready"), sem("f_hi_ready"), sem("f_split"),
            sem("f_down"), sem("fx_acc"))
        stored = sem("stored")

        PJ, R0, R1, EB, YD, YO, SM = bank[0:2], bank[2], bank[3], bank[4], bank[5], bank[6], bank[7]
        UG, UL, WB, DN = bank[0:2], bank[2:4], bank[4], bank[5:8]
        S_, TT_, PP = bank[0:3], bank[3:5], bank[5:8]
        FG, FU, FD = bank[0:2], bank[2:4], bank[4:8]
        S_AT = [(2, 256, 256), (2, 0, 256), (1, 0, 384), (0, 0, 512)]
        PR_AT = [0, 128, 384, 768]

        def tok(b):
            return bass.ds(b * T, T)

        def three(out, hi_w, lo_w, hi_x, lo_x, start, stop):
            nc.tensor.matmul(out, hi_w, hi_x, start=start, stop=False)
            nc.tensor.matmul(out, hi_w, lo_x, start=False, stop=False)
            return nc.tensor.matmul(out, lo_w, hi_x, start=False, stop=stop)

        class Steps:
            def __init__(self, eng, s):
                self.eng, self.s, self.base, self.n = eng, s, 0, 0

            def inc(self, ins):
                ins.then_inc(self.s, 1)
                self.n += 1

            def wait(self):
                self.eng.wait_ge(self.s, self.base + self.n)

        CONV_ORDER = [XC, XC + 1] + list(range(XC))
        Q_BANK, C_BANK, D_BANK = [2, 0, 1, 0], [2, 1, 2, 0], [1, 2, 0, 1]
        T_GROUP = [(0, 512, 0), (1, 512, 512), (0, 256, 1024)]
        PT_AT = [(0, 512), (512, 384), (1024, 256), (896, 128)]

        N_MASKS = 11 + 5 + 4
        DVE_MAMBA = 82
        SETUP_STEPS = 20
        def finish(sp, s, count):
            n = 0
            for b in range(BATCH):
                sp.wait_ge(s, count - KC * (BATCH - 1 - b))
                sp.dma_start(o_view[:, :, b * T:(b + 1) * T], XT[:, :, b * T:(b + 1) * T]).then_inc(stored, 16)
                n += 16
            sp.wait_ge(stored, n)

        block = ctx.enter_context(nc.Block())
        @block.sync
        def _(sp):
            sp.dma_start(cols[:], cols_d).then_inc(loaded, 16)
            sp.dma_start(rows[:], rows_d).then_inc(loaded, 16)
            sp.dma_start(condT_s[:], condT).then_inc(loaded, 16)

            def gate_load(two, j):
                n, r = two * 2 + j, two + j // 2
                sp.wait_ge(g_out[j % 2], 16 * r)
                src = fT[bass.ds(n % TILES, 1)].rearrange("o p t -> (o p) t")
                sp.dma_start(g_v[:, j % 2, :], src).then_inc(g_in[j % 2], 16)

            def gate_store(two, j):
                n = two * 2 + j
                sp.wait_ge(g_step, G_STEPS * (n + 1))
                dst = g_dram[bass.ds(n, 1)].rearrange("o p t -> (o p) t")
                sp.dma_start(dst, g_v[:, j % 2, :]).then_inc(g_out[j % 2], 16)

            def gates(two, count):
                gate_load(two, 0)
                for j in range(count):
                    if j + 1 < count:
                        gate_load(two, j + 1)
                    gate_store(two, j)

            sp.dma_start(XT[:, :, 0:T], x_view[:, :, 0:T]).then_inc(x_loaded, 16)
            gates(0, G_PRE)
            for b in range(1, BATCH):
                sp.dma_start(XT[:, :, b * T:(b + 1) * T], x_view[:, :, b * T:(b + 1) * T]).then_inc(x_loaded, 16)

            def fetch_gate(layer, b, dst):
                for i in range(2):
                    sp.wait_ge(g_out[i], 16 * (TILES * layer // 2 + 2 * (b + 1)))
                src = g_dram[bass.ds(b * KC + TILES * layer, KC)].rearrange("k p t -> p k t")
                sp.dma_start(dst, src).then_inc(g_fetched, 16)

            with sp.Fori(0, BATCH) as b:
                sp.wait_ge(z_done, PAIRS * b)
                fetch_gate(0, b, um[:])
                gates(b * (G_MAMBA // 2) + G_PRE // 2, G_MAMBA)
            sp.wait_ge(masks_ready, N_MASKS + 2)
            for h in range(2):
                sp.dma_start(b2_s[32 * h:32 * h + E, :], b2_d).then_inc(moe_loaded, 16)
            sp.dma_start(gw[:], gw_d).then_inc(moe_loaded, 16)
            for b in range(BATCH):
                if b:
                    sp.wait_ge(u_split, b)
                    sp.wait_ge(logit_done, b)
                fetch_gate(1, b, uf1[:])

            def stage(s, p):
                if not (isinstance(s, int) and s == 0 and p == 0):
                    sp.wait_ge(w_split, 2 * s + p)
                w0 = p * (MOE_W // 2)
                src = moe_d[s] if isinstance(s, int) else moe_d[bass.ds(s, 1)].rearrange("o p w -> (o p) w")
                sp.dma_start(m_stage[:], src[:, w0:w0 + MOE_W // 2]).then_inc(m_staged, 16)

            stage(0, 0)
            stage(0, 1)

            def expert_loads(e, last):
                two = e * (G_MOE // 2) + (G_PRE + G_MAMBA * BATCH) // 2
                stage(2 * e + 1, 0)
                if last:
                    stage(2 * e + 1, 1)
                    return
                gate_load(two, 0)
                gate_load(two, 1)
                stage(2 * e + 1, 1)
                gate_store(two, 0)
                gate_load(two, 2)
                stage(2 * e + 2, 0)
                gate_store(two, 1)
                gate_load(two, 3)
                stage(2 * e + 2, 1)
                gate_store(two, 2)
                gate_store(two, 3)

            with sp.Fori(0, E - 1) as e:
                expert_loads(e, False)
            expert_loads(E - 1, True)
            sp.wait_ge(x_acc, KC * BATCH * E * HALF)

            def att_stage(g):
                for p in range(2):
                    if not (isinstance(g, int) and g == 0 and p == 0):
                        sp.wait_ge(aw_split, 2 * g + p)
                    w0 = p * (ATT_W // 2)
                    src = att_d[g] if isinstance(g, int) else att_d[bass.ds(g, 1)].rearrange("o p w -> (o p) w")
                    sp.dma_start(a_stage[:], src[:, w0:w0 + ATT_W // 2]).then_inc(a_staged, 16)

            for b in range(BATCH):
                if b:
                    sp.wait_ge(u_split, BATCH + b)
                fetch_gate(2, b, uf2[:])
            with sp.Fori(0, GROUPS) as g:
                att_stage(g)
            sp.wait_ge(ax_acc, KC * BATCH * GROUPS)
            for b in range(BATCH):
                if b:
                    sp.wait_ge(u_split, 2 * BATCH + b)
                fetch_gate(3, b, uf3[:])

            def ffn_stage(s, before, par):
                if before is not None:
                    sp.wait_ge(fw_split, before)
                src = ffn_d[s] if isinstance(s, int) else ffn_d[bass.ds(s, 1)].rearrange("o p w -> (o p) w")
                sp.dma_start(f_stage[:, par, :], src).then_inc(f_staged[par], 16)

            ffn_stage(0, None, 0)
            with sp.Fori(0, FS // 2) as it:
                ffn_stage(it * 2 + 1, it * 2, 1)
                ffn_stage(it * 2 + 2, it * 2 + 1, 0)
            finish(sp, fx_acc, KC * BATCH * FS)

        @block.gpsimd
        def _(pool):
            n = [0]

            def done(ins):
                ins.then_inc(masks_ready, 1)
                n[0] += 1

            def fill(dst, src, op, val, base, pattern, mult):
                pool.wait_ge(masks_ready, n[0])
                done(nc.gpsimd.affine_select(out=dst, in_=src, compare_op=op, fill=val, base=base, pattern=pattern,
                                             channel_multiplier=mult))

            for t_, v_ in ((ident[:], 0.0), (ident_b[:], 0.0), (ones[:], 1.0), (sel_h[:].bitcast(F32), 0.0),
                           (causal_b[:], 0.0), (tri[:], 1.0), (neg4[:], 0.0), (sel_p[:].bitcast(F32), 0.0),
                           (csT[:].bitcast(F32), 0.0), (g_r[:, T - 1:T], 0.0), (eps_c[:], EPS)):
                done(nc.gpsimd.memset(t_, v_))
            fill(ident[:], ident[:], ALU.not_equal, 1.0, 0, [[-1, P]], 1)
            fill(ident_b[:], ident_b[:], ALU.not_equal, 1.0, 0, [[-1, P]], 1)
            fill(causal_b[:], causal_b[:], ALU.is_ge, NEG, 0, [[-1, P]], 1)
            fill(tri[:], tri[:], ALU.is_ge, 0.0, 0, [[1, P]], -1)
            fill(neg4[:], neg4[:], ALU.is_ge, NEG, 0, [[0, TB], [1, P]], -1)
            for h in range(2):
                fill(sel_h[:], sel_h[:], ALU.not_equal, 1.0, -32 * h, [[-1, HEADS_M]], 1)
                fill(sel_p[:], sel_p[:], ALU.not_equal, 1.0, -32 * h, [[-2, PAIRS], [-1, 2], [0, HD]], 1)
            pool.wait_ge(x_added, KC * BATCH)
            done(nc.gpsimd.memset(we_t[:].bitcast(F32), 0.0))
            done(nc.gpsimd.memset(b2_s[:], 0.0))


        @block.scalar
        def _(act):
            act.dma_start(w_in[:], w_in_d).then_inc(w_loaded, 16)
            act.dma_start(w_out[:], w_out_d).then_inc(w_loaded, 16)
            A = nc.scalar.activation
            act.wait_ge(loaded, 48)
            act.wait_ge(masks_ready, N_MASKS)
            A(dec0[:], cols[:, COLS["w"]:COLS["w"] + 16], ACT.Exp).then_inc(setup_act, 1)
            act.wait_ge(setup_act, 1)
            A(dec0[:], dec0[:], ACT.Exp, scale=-1.0).then_inc(setup_act, 1)
            A(a_neg[:], rows[:, HEADS_M:2 * HEADS_M], ACT.Exp).then_inc(setup_act, 1)
            act.wait_ge(setup_mm, 1)
            A(tf[:], bank[0][:, 0:BATCH], ACT.Tanh, scale=0.5).then_inc(setup_act, 1)

            def gate(two, j):
                s_, n = j % 2, two * 2 + j
                act.wait_ge(g_in[s_], 16 * (two + j // 2 + 1))
                if not (isinstance(n, int) and n < 2):
                    act.wait_ge(g_step, G_STEPS * (n - 1))
                un = u_all[:, bass.ds(n, 1)]
                A(g_ek[:, s_, :], g_v[:, s_, :], ACT.Exp).then_inc(g_exp, 1)
                A(g_eu[:, s_, :], g_v[:, s_, :], ACT.Exp, bias=un).then_inc(g_exp, 1)

            act.wait_ge(setup_step, SETUP_STEPS)
            for j in range(G_PRE):
                gate(0, j)

            def tanh_x(k, b, dst, reused):
                if reused is not None:
                    act.wait_ge(u_ready, reused)
                A(dst, XT[:, :, tok(b)], ACT.Tanh, scale=0.5).then_inc(x_tanh, 1)

            act.wait_ge(x_loaded, 16 * BATCH)
            with act.Fori(0, BATCH) as b:
                two = b * (G_MAMBA // 2) + G_PRE // 2
                tanh_x(b, b, txm[:], b)
                act.wait_ge(dt_abs, b + 1)
                A(d_e[:], d_a[:], ACT.Exp, scale=-1.0).then_inc(dt_exp, 1)

                def first_tap(q, ch):
                    act.wait_ge(proj_done, N_CONV * b + q + 1)
                    if q >= 2:
                        act.wait_ge(act_ready, N_CONV * b + q - 1)
                    A(acc[q % 2], PJ[q % 2][:], ACT.Identity, bias=col("conv_b", ch),
                      scale=col("conv_w", 4 * ch + 3)).then_inc(tap0, 1)

                def conv_sig(q):
                    act.wait_ge(conv_tapped, N_CONV * b + q + 1)
                    if q >= 2:
                        act.wait_ge(act_ready, N_CONV * b + q - 1)
                    A(cth[q % 2], acc[q % 2], ACT.Tanh).then_inc(conv_tanh, 1)

                for q, ch in enumerate(CONV_ORDER):
                    first_tap(q, ch)
                    if q == 2:
                        gate(two, 0)
                    if q == 5:
                        gate(two, 1)
                    if q:
                        conv_sig(q - 1)
                    if q == 5:
                        act.wait_ge(cs_neg, b + 1)
                        A(w2e[:], w2[:], ACT.Exp).then_inc(w_exp, 1)
                        A(cdec[:], SM[:, 128:128 + NB], ACT.Exp).then_inc(w_exp, 1)
                        A(csT[0:HEADS_M, :], EB[0:HEADS_M, :], ACT.Copy).then_inc(ct_hi, 1)
                conv_sig(N_CONV - 1)
                for tb in range(TB):
                    act.wait_ge(bc_done, TB * b + tb + 1)
                    A(b_tok[:, tb, :], SM[:, 192:320], ACT.Copy).then_inc(bc_copied, 1)
                    A(cb[:, tb, :], SM[:, 320:448], ACT.Copy).then_inc(bc_copied, 1)
                act.wait_ge(act_ready, N_CONV * (b + 1))

                def square(j):
                    act.wait_ge(y_done, PAIRS * b + j + 1)
                    if j > 1:
                        act.wait_ge(sq_added, (PAIRS - 1) * b + j - 1)
                    A(sq[:] if j else ssum[:], xa[:, j, :], ACT.Square).then_inc(sq_done, 1)

                for j in range(PAIRS):
                    act.wait_ge(r_done, PAIRS * b + j + 1)
                    if j:
                        act.wait_ge(yy_done, PAIRS * b + j)
                        act.wait_ge(y_done, PAIRS * b + j)
                    for hh in range(2):
                        for tb in range(TB):
                            i = tb * HEADS_M + 2 * j + hh
                            A(lm[:, hh, tb * P:(tb + 1) * P], (R0, R1)[hh][:, tb * P:(tb + 1) * P], ACT.Exp,
                              bias=csn[:, i:i + 1]).then_inc(l_done, 1)
                    A(e2[:], EB[:], ACT.Exp).then_inc(l_done, 1)
                    act.wait_ge(z_done, PAIRS * b + j + 1)
                    A(tz[:], PJ[j % 2][:], ACT.Tanh, scale=0.5).then_inc(z_tanh, 1)
                    if j % 2 == 0:
                        gate(two, 2 + j // 2)
                    if j:
                        square(j - 1)
                square(PAIRS - 1)
                act.wait_ge(ssq_done, b + 1)
                A(sq[:], EB[:], ACT.Sqrt, scale=1.0 / D_IN, bias=eps_c[:]).then_inc(rms_done, 1)
                gate(two, 6)
                gate(two, 7)

            def split_u(k, b, src, tx):
                act.wait_ge(u_ready, k + 1)
                A(u_hi[:, :, b * T:(b + 1) * T], src, ACT.Copy).then_inc(u_hi_ready, 1)

            act.wait_ge(x_added, KC * BATCH)
            for b in range(BATCH):
                k = BATCH + b
                tanh_x(k, b, tx1[:], k)
                split_u(k, b, uf1[:], tx1)
                act.wait_ge(lg_sub, b + 1)
                A(ex[:], lg[:], ACT.Exp).then_inc(lg_exp, 1)
                act.wait_ge(we_T, b + 1)
                A(we_t[0:E, b * T:(b + 1) * T], WB[0:E, :], ACT.Copy).then_inc(we_hi, 1)

            def moe_y(e, t):
                half, b = divmod(t, BATCH)
                k = e * (HALF * BATCH) + t
                act.wait_ge(y_split, 2 * k)
                if t == 0:
                    act.wait_ge(bias_ready, 2 * (e + 1))
                for i in range(2):
                    act.wait_ge(up_done, 2 * k + i + 1)
                    ic = half * 2 + i
                    A(m_t[:, i, :], UG[i][:], ACT.Tanh, bias=bias_e[:, ic:ic + 1], scale=0.851).then_inc(m_tanh, 1)
                    A(m_y[:, i, :], UL[i][:], ACT.Identity, bias=bias_e[:, 4 + ic:5 + ic]).then_inc(m_lin, 1)
                for i in range(2):
                    act.wait_ge(m_yready, 2 * k + i + 1)
                    A(my_hi[:, b % 2, i, :], m_y[:, i, :], ACT.Copy).then_inc(y_hi_ready, 1)

            act.wait_ge(we_lo, BATCH)
            for p in range(2):
                act.wait_ge(m_staged, 16 * (p + 1))
                w0 = p * (MOE_W // 2)
                A(mw_hi[:, 0, w0:w0 + MOE_W // 2], m_stage[:], ACT.Copy).then_inc(mw_hi_ready, 1)
            moe_y(0, 0)

            def expert_act(e, last):
                two = e * (G_MOE // 2) + (G_PRE + G_MAMBA * BATCH) // 2
                for t in range(HALF * BATCH):
                    half, b = divmod(t, BATCH)
                    s = 2 * e + half
                    if t < HALF * BATCH - 1:
                        moe_y(e, t + 1)
                    elif not last:
                        moe_y(e + 1, 0)
                    if b in (1, 2) and not (last and half):
                        par = 1 - half
                        act.wait_ge(m_staged, 16 * (2 * (s + 1) + b))
                        act.wait_ge(moe_down, KC * BATCH * s)
                        w0 = (b - 1) * (MOE_W // 2)
                        A(mw_hi[:, par, w0:w0 + MOE_W // 2], m_stage[:], ACT.Copy).then_inc(mw_hi_ready, 1)
                    if b % 2 and not last:
                        gate(two, t // 2)

            with act.Fori(0, E - 1) as e:
                expert_act(e, False)
            expert_act(E - 1, True)
            act.wait_ge(x_acc, KC * BATCH * E * HALF)
            for b in range(BATCH):
                k = 2 * BATCH + b
                tanh_x(k, b, tx2[:], k)
                split_u(k, b, uf2[:], tx2)
            act.wait_ge(u_split, 3 * BATCH - BATCH)
            with act.Fori(0, GROUPS) as g:
                for p in range(2):
                    act.wait_ge(a_staged, 16 * (2 * g + p + 1))
                    act.wait_ge(dense_done, KC * BATCH * g)
                    act.wait_ge(aw_split, 2 * g + p)
                    w0 = p * (ATT_W // 2)
                    A(aw_hi[:, w0:w0 + ATT_W // 2], a_stage[:], ACT.Copy).then_inc(aw_hi_ready, 1)
                with act.Fori(0, BATCH) as b:
                    i = g * BATCH + b

                    def q_split_hi(h):
                        act.wait_ge(q_done, HPG * i + h + 1)
                        if h >= 2:
                            act.wait_ge(scores_done, HPG * i + h - 1)
                        A(q_hi[:, h % 2, :], PP[Q_BANK[h]][:], ACT.Copy).then_inc(q_hi_ready, 1)

                    def probs_exp(h):
                        act.wait_ge(max_ready, HPG * i + h + 1)
                        if h >= 2:
                            act.wait_ge(t_done, 3 * (HPG * i + h - 1))
                        for qb in range(TB):
                            bk, c0, _ = S_AT[qb]
                            w = (qb + 1) * P
                            A(probs[:, h % 2, PR_AT[qb]:PR_AT[qb] + w], S_[bk][:, c0:c0 + w], ACT.Exp,
                              bias=nmx[:, h % 2, qb:qb + 1], scale=SCALE,
                              accum_out=rsum[:, h % 2, qb:qb + 1]).then_inc(exp_done, 1)

                    def pt_hi_copy(h):
                        for r, (bk, w, c0) in enumerate(T_GROUP):
                            act.wait_ge(t_done, 3 * (HPG * i + h) + r + 1)
                            if r == 0:
                                act.wait_ge(c_done, HPG * i + h)
                            A(pt_hi[:, c0:c0 + w], TT_[bk][:, 0:w], ACT.Copy).then_inc(pt_hi_ready, 1)

                    def ctx_hi(h):
                        act.wait_ge(c_done, HPG * i + h + 1)
                        A(cx_hi[:, h, :], PP[C_BANK[h]][:], ACT.Copy).then_inc(c_hi_ready, 1)

                    act.wait_ge(k_done, i + 1)
                    A(k_hi[:], PP[0][:], ACT.Copy).then_inc(k_hi_ready, 1)
                    act.wait_ge(v_done, i + 1)
                    A(vT[:], PP[1][:], ACT.Copy).then_inc(vt_copied, 1)
                    q_split_hi(0)
                    act.wait_ge(vt_done, i + 1)
                    A(v_hi[:], TT_[0][:].rearrange("p (a d) -> p a d", a=TB), ACT.Copy).then_inc(v_hi_ready, 1)
                    q_split_hi(1)
                    probs_exp(0)
                    q_split_hi(2)
                    probs_exp(1)
                    pt_hi_copy(0)
                    q_split_hi(3)
                    ctx_hi(0)
                    probs_exp(2)
                    pt_hi_copy(1)
                    ctx_hi(1)
                    probs_exp(3)
                    pt_hi_copy(2)
                    ctx_hi(2)
                    pt_hi_copy(3)
                    ctx_hi(3)
            act.wait_ge(ax_acc, KC * BATCH * GROUPS)
            for b in range(BATCH):
                k = 3 * BATCH + b
                tanh_x(k, b, tx3[:], k)
                split_u(k, b, uf3[:], tx3)

            def ffn_hi(s, par, uses, free):
                act.wait_ge(f_staged[par], 16 * uses)
                if free is not None:
                    act.wait_ge(f_down, free)
                A(fw_hi[:, par, :], f_stage[:, par, :], ACT.Copy).then_inc(fw_hi_ready, 1)

            def ffn_y(s, b):
                k = s * BATCH + b
                act.wait_ge(f_split, k)
                act.wait_ge(f_up, k + 1)
                if b == 0:
                    act.wait_ge(f_scaled, 2 * (s + 1))
                A(f_t[:], FG[b % 2][:], ACT.Tanh, scale=f_sc[:, 0:1]).then_inc(f_tanh, 1)
                A(f_u[:], FU[b % 2][:], ACT.Copy, scale=f_sc[:, 1:2]).then_inc(f_lin, 1)
                act.wait_ge(f_yready, k + 1)
                A(f_hi[:, b % 2, :], f_y[:], ACT.Copy).then_inc(f_hi_ready, 1)

            ffn_hi(0, 0, 1, None)
            ffn_y(0, 0)

            def ffn_act(it, par, last):
                s = it * 2 + par
                for b in range(BATCH):
                    if b < BATCH - 1:
                        ffn_y(s, b + 1)
                    elif not last:
                        ffn_y(s + 1, 0)
                    if b == 1 and not last:
                        ffn_hi(s + 1, 1 - par, it + 1 + par, KC * BATCH * s)

            with act.Fori(0, FS // 2) as it:
                ffn_act(it, 0, False)
                ffn_act(it, 1, False)
            ffn_act(FS // 2, 0, True)

        @block.vector
        def _(dve):
            V = nc.vector
            setup = Steps(dve, setup_step)
            dve.wait_ge(loaded, 48)

            def spread(name, i):
                return cols[:, COLS[name] + 4 * i:COLS[name] + 4 * i + 4].unsqueeze(1).to_broadcast([P, BATCH, KC])

            def gate_cols(t_, i):
                return t_[:, TILES * i:TILES * (i + 1)].rearrange("p (b c) -> p b c", b=BATCH)

            for i in range(N_GATES):
                setup.inc(V.tensor_copy(gate_cols(u_all, i), spread("u", i)))
            c0 = COLS["b1_glu"]
            setup.inc(V.tensor_scalar(bgs[:], cols[:, c0:c0 + 4 * E], 0.851, None, ALU.mult))
            lin = cols[:, COLS["b1_lin"]:COLS["b1_lin"] + 4 * E]
            setup.inc(V.tensor_scalar(lin, lin, 1.0, None, ALU.add))
            setup.inc(V.tensor_scalar(gsh[:], cols[:, COLS["gate_s"]:COLS["gate_s"] + FS], 0.5, None, ALU.mult))
            cw = cols[:, COLS["conv_w"]:COLS["conv_w"] + 5 * N_CONV]
            setup.inc(V.tensor_scalar(cw, cw, 0.5, None, ALU.mult))
            setup.wait()
            setup.inc(V.tensor_tensor(ush[:], gsh[:], cols[:, COLS["up_s"]:COLS["up_s"] + FS], ALU.mult))
            dve.wait_ge(setup_act, 4)
            setup.inc(V.tensor_scalar(a_neg[:], a_neg[:], -1.0, None, ALU.mult))
            setup.inc(V.tensor_scalar(fac[:], tf[:], 0.25, 0.75, ALU.mult, ALU.add))
            setup.inc(V.tensor_scalar(osc[:], tf[:], 0.05, 0.45, ALU.mult, ALU.add))
            setup.wait()
            for i in range(N_GATES):
                d0 = dec0[:, 4 * i:4 * i + 4].unsqueeze(1).to_broadcast([P, BATCH, KC])
                setup.inc(V.tensor_tensor(gate_cols(decay, i), d0, fac[:].unsqueeze(2).to_broadcast([P, BATCH, KC]), ALU.mult))
                setup.inc(V.tensor_copy(gate_cols(oscale, i), osc[:].unsqueeze(2).to_broadcast([P, BATCH, KC])))
            setup.wait()
            assert setup.n == SETUP_STEPS
            dve.wait_ge(masks_ready, N_MASKS)

            def gate(two, j):
                s_, n = j % 2, two * 2 + j
                v, ek, eu = g_v[:, s_, :], g_ek[:, s_, :], g_eu[:, s_, :]
                st = Steps(dve, g_step)
                st.base = n * G_STEPS
                d = decay[:, bass.ds(n, 1)].to_broadcast([P, T])
                d1 = decay[:, bass.ds(n, 1)].to_broadcast([P, T - 1])

                def past(dst, src):
                    return V.tensor_tensor_scan(dst, d, src, 0.0, ALU.mult, ALU.add)

                def future(dst, src):
                    return V.tensor_tensor_scan(dst[:, 0:T - 1][:, ::-1], src[:, 1:T][:, ::-1], d1, 0.0, ALU.add, ALU.mult)

                dve.wait_ge(g_exp, (n + 1) * 2)
                st.inc(V.tensor_scalar(ek, ek, EXP30, None, ALU.min))
                st.wait()
                st.inc(V.tensor_tensor(g_e[:], ek, v, ALU.mult))
                st.wait()
                st.inc(past(g_f[:], g_e[:]))
                st.inc(future(g_r, g_e))
                st.inc(V.scalar_tensor_tensor(v, eu, EXP30, v, ALU.min, ALU.mult))
                st.wait()
                st.inc(V.tensor_tensor(g_f[:], g_f[:], g_r[:], ALU.add))
                st.wait()
                st.inc(V.tensor_tensor(g_f[:], g_f[:], v, ALU.add))
                st.inc(past(g_e[:], ek))
                st.inc(future(g_r, g_ek[:, s_, :]))
                st.wait()
                st.inc(V.tensor_tensor(g_e[:], g_e[:], g_r[:], ALU.add))
                st.wait()
                st.inc(V.scalar_tensor_tensor(g_e[:], eu, EXP30, g_e[:], ALU.min, ALU.add))
                st.wait()
                st.inc(V.tensor_scalar(g_e[:], g_e[:], 1e-8, None, ALU.max))
                st.wait()
                st.inc(V.reciprocal(ek, g_e[:]))
                st.wait()
                st.inc(V.scalar_tensor_tensor(v, g_f[:], oscale[:, bass.ds(n, 1)], ek, ALU.mult, ALU.mult))
                assert st.n == G_STEPS

            for j in range(G_PRE):
                gate(0, j)

            def gated(k, u, tx):
                dve.wait_ge(x_tanh, k + 1)
                dve.wait_ge(g_fetched, 16 * (k + 1))
                V.scalar_tensor_tensor(u, tx, 1.0, u, ALU.add, ALU.mult).then_inc(u_ready, 1)

            step = Steps(dve, dve_step)
            with dve.Fori(0, BATCH) as b:
                two = b * (G_MAMBA // 2) + G_PRE // 2
                step.base = b * DVE_MAMBA
                gated(b, um[:].rearrange("p k t -> p (k t)"), txm[:].rearrange("p k t -> p (k t)"))
                dve.wait_ge(dt_raw, b + 1)
                dtb = rows[:, 0:HEADS_M].unsqueeze(1).to_broadcast([P, TB, HEADS_M])

                def th(t_):
                    return t_[:].rearrange("p (a h) -> p a h", a=TB)

                step.inc(V.tensor_tensor(th(d_x), SM[:, 0:NB].rearrange("p (a h) -> p a h", a=TB), dtb, ALU.add))
                step.wait()
                V.scalar_tensor_tensor(d_a[:], d_x[:], -1.0, d_x[:], ALU.mult, ALU.max).then_inc(dt_abs, 1)
                dve.wait_ge(dt_exp, b + 1)
                step.inc(V.tensor_scalar(d_s[:], d_e[:], 2.0, None, ALU.add))
                step.wait()
                step.inc(V.reciprocal(d_p[:], d_s[:]))
                step.wait()
                step.inc(V.tensor_tensor(d_s[:], d_e[:], d_p[:], ALU.mult))
                step.wait()
                step.inc(V.tensor_tensor(d_q[:], d_s[:], d_s[:], ALU.mult))
                step.wait()
                step.inc(V.tensor_scalar(d_p[:], d_q[:], 1.0 / 17, None, ALU.mult))
                for i in range(7, 0, -1):
                    step.wait()
                    step.inc(V.scalar_tensor_tensor(d_p[:], d_p[:], 1.0 / (2 * i + 1), d_q[:], ALU.add, ALU.mult))
                step.wait()
                step.inc(V.scalar_tensor_tensor(d_p[:], d_p[:], 1.0, d_s[:], ALU.add, ALU.mult))
                step.inc(V.tensor_scalar(d_x[:], d_x[:], 0.0, None, ALU.max))
                step.wait()
                step.inc(V.scalar_tensor_tensor(dt_t[:], d_p[:], 2.0, d_x[:], ALU.mult, ALU.add))
                step.wait()
                V.tensor_tensor(th(d_A), th(dt_t), a_neg[:].unsqueeze(1).to_broadcast([P, TB, HEADS_M]),
                                ALU.mult).then_inc(dA_ready, 1)

                def taps(q, ch):
                    dve.wait_ge(tap0, N_CONV * b + q + 1)
                    for k in range(1, 4):
                        if k > 1:
                            step.wait()
                        ins = V.scalar_tensor_tensor(acc[q % 2][:, k:T], PJ[q % 2][:, 0:T - k], col("conv_w", 4 * ch + 3 - k),
                                                     acc[q % 2][:, k:T], ALU.mult, ALU.add)
                        if k < 3:
                            step.inc(ins)
                        else:
                            ins.then_inc(conv_tapped, 1)

                def conv_out(q, ch):
                    dve.wait_ge(conv_tanh, N_CONV * b + q + 1)
                    dst = xa[:, ch, :] if ch < XC else (bT, cT)[ch - XC][:]
                    V.scalar_tensor_tensor(dst, cth[q % 2], 1.0, acc[q % 2], ALU.add, ALU.mult).then_inc(act_ready, 1)

                for q, ch in enumerate(CONV_ORDER):
                    taps(q, ch)
                    if q:
                        conv_out(q - 1, CONV_ORDER[q - 1])
                    if q == 4:
                        dve.wait_ge(cs_done, b + 1)
                        step.inc(V.tensor_scalar(csn[:], SM[:, 64:64 + NB], -1.0, None, ALU.mult))
                        step.wait()
                        V.tensor_tensor(w2[:], SM[:, 128:128 + NB], csn[:], ALU.add).then_inc(cs_neg, 1)
                    if q == 6:
                        dve.wait_ge(w_exp, 2 * (b + 1))
                        step.inc(V.tensor_tensor(dts[:], w2e[:], dt_t[:], ALU.mult))
                        dve.wait_ge(ct_hi, b + 1)
                        V.tensor_tensor(csT[32:32 + HEADS_M, :], EB[0:HEADS_M, :], csT[0:HEADS_M, :].bitcast(F32),
                                        ALU.subtract).then_inc(ct_ready, 1)
                        gate(two, 0)
                conv_out(N_CONV - 1, CONV_ORDER[-1])
                gate(two, 1)
                step.wait()

                def per_head(t_, tb, half):
                    h0 = tb * HEADS_M + 8 * half
                    return t_[:, h0:h0 + 8].unsqueeze(2).to_broadcast([P, 8, HD])

                for tb in range(TB):
                    dve.wait_ge(x_transposed, TB * b + tb + 1)
                    if tb:
                        dve.wait_ge(s_done, (TB - 1) * b + tb)
                    for half in range(2):
                        xt = (R0, R1)[half][:].rearrange("p (h d) -> p h d", h=8)
                        o = slice(half * 512, half * 512 + 512)
                        step.inc(V.tensor_tensor(xdt[:, tb, o].rearrange("p (h d) -> p h d", h=8), xt,
                                                 per_head(dt_t, tb, half), ALU.mult))
                        ins = V.tensor_tensor(xdt2[:, o].rearrange("p (h d) -> p h d", h=8), xt,
                                              per_head(dts, tb, half), ALU.mult)
                        if half:
                            ins.then_inc(xdt_done, 1)
                        else:
                            step.inc(ins)
                    if tb < TB - 1:
                        dve.wait_ge(s_done, (TB - 1) * b + tb + 1)
                        for half in range(2):
                            o = slice(half * 512, half * 512 + 512)
                            if tb:
                                if half == 0:
                                    dve.wait_ge(state_done, (TB - 1) * b + tb)
                                step.inc(V.tensor_tensor(state[:, tb, o].rearrange("p (h d) -> p h d", h=8),
                                                         state[:, tb - 1, o].rearrange("p (h d) -> p h d", h=8),
                                                         per_head(cdec, tb, half), ALU.mult))
                                step.wait()
                                ins = V.tensor_tensor(state[:, tb, o], state[:, tb, o], PJ[half][:], ALU.add)
                            else:
                                ins = V.tensor_copy(state[:, tb, o], PJ[half][:])
                            if half:
                                ins.then_inc(state_done, 1)
                            else:
                                step.inc(ins)

                def add_square(j):
                    dve.wait_ge(sq_done, PAIRS * b + j + 1)
                    if j > 1:
                        dve.wait_ge(sq_added, (PAIRS - 1) * b + j - 1)
                    V.tensor_tensor(ssum[:], ssum[:], sq[:], ALU.add).then_inc(sq_added, 1)

                for j in range(PAIRS):
                    dve.wait_ge(l_done, 9 * (PAIRS * b + j + 1))
                    for hh in range(2):
                        V.tensor_tensor(lm[:, hh, :], lm[:, hh, :], cb[:].rearrange("p a l -> p (a l)"),
                                        ALU.mult).then_inc(m_ready, 1)
                    dve.wait_ge(z_tanh, PAIRS * b + j + 1)
                    V.scalar_tensor_tensor(tz[:], tz[:], 1.0, PJ[j % 2][:], ALU.add, ALU.mult).then_inc(zs_done, 1)
                    dve.wait_ge(yy_done, PAIRS * b + j + 1)
                    xj = xa[:, j, :]
                    step.inc(V.scalar_tensor_tensor(xj, xj, col("d_skip", j), YD[:], ALU.mult, ALU.add))
                    step.inc(V.tensor_tensor(e2[:, P:T], YO[:, P:T], e2[:, P:T], ALU.mult))
                    step.wait()
                    step.inc(V.tensor_tensor(xj[:, P:T], xj[:, P:T], e2[:, P:T], ALU.add))
                    step.wait()
                    V.scalar_tensor_tensor(xj, xj, 0.5, tz[:], ALU.mult, ALU.mult).then_inc(y_done, 1)
                    if j > 1:
                        add_square(j - 1)
                    if j % 2 == 0:
                        gate(two, 2 + j // 2)
                add_square(PAIRS - 1)
                dve.wait_ge(rms_done, b + 1)
                step.inc(V.reciprocal(ssum[:], sq[:]))
                step.wait()
                for j in range(XC):
                    V.scalar_tensor_tensor(xa[:, j, :], xa[:, j, :], col("norm_w", j), ssum[:], ALU.mult,
                                           ALU.mult).then_inc(yn_ready, 1)
                gate(two, 6)
                for m in range(KC):
                    dve.wait_ge(out_done, KC * b + m + 1)
                    V.tensor_tensor(XT[:, m, tok(b)], XT[:, m, tok(b)], PJ[m % 2][:], ALU.add).then_inc(x_added, 1)
                gate(two, 7)
                assert step.n == DVE_MAMBA, step.n

            def split_u(k, b, src):
                dve.wait_ge(u_hi_ready, k - BATCH + 1)
                V.tensor_tensor(u_lo[:, :, b * T:(b + 1) * T], src, u_hi[:, :, b * T:(b + 1) * T].bitcast(F32),
                                ALU.subtract).then_inc(u_split, 1)

            def flat(t_):
                return t_[:].rearrange("p k t -> p (k t)")

            route = Steps(dve, dve_step)
            route.base = DVE_MAMBA * BATCH
            dve.wait_ge(masks_ready, N_MASKS + 2)
            route.inc(V.memset(rst[:], 1.0))
            route.wait()
            route.inc(V.memset(rst[:, :, 0:1], 0.0))
            for b in range(BATCH):
                k = BATCH + b
                gated(k, flat(uf1), flat(tx1))
                split_u(k, b, uf1[:])
                dve.wait_ge(logit_done, b + 1)
                gb = rows[:, 2 * HEADS_M:2 * HEADS_M + E].unsqueeze(1).to_broadcast([P, TB, E])
                route.inc(V.tensor_tensor(lg[:], DN[0][:, 0:TB * E].rearrange("p (a e) -> p a e", a=TB), gb, ALU.add))
                route.wait()
                for tb in range(TB):
                    route.inc(V.max(mx8[:, tb, :], lg[:, tb, :]))
                route.wait()
                m2 = mx8[:, :, 1:2].to_broadcast([P, TB, E])
                route.inc(V.tensor_tensor(gt[:], lg[:], m2, ALU.is_gt))
                route.inc(V.tensor_tensor(eq[:], lg[:], m2, ALU.is_equal))
                route.wait()
                V.tensor_tensor(lg[:], lg[:], mx8[:, :, 0:1].to_broadcast([P, TB, E]), ALU.subtract).then_inc(lg_sub, 1)
                route.inc(V.tensor_reduce(r4[:, 0, :], gt[:], AX.X, ALU.add))
                route.inc(V.tensor_tensor_scan(pre[:].rearrange("p a e -> p (a e)"), rst[:].rearrange("p a e -> p (a e)"),
                                               eq[:].rearrange("p a e -> p (a e)"), 0.0, ALU.mult, ALU.add))
                route.wait()
                route.inc(V.tensor_scalar(r4[:, 0, :], r4[:, 0, :], -1.0, 2.0, ALU.mult, ALU.add))
                route.wait()
                route.inc(V.tensor_tensor(pre[:], pre[:], r4[:, 0, :].unsqueeze(2).to_broadcast([P, TB, E]), ALU.is_le))
                route.wait()
                route.inc(V.tensor_tensor(eq[:], eq[:], pre[:], ALU.mult))
                route.wait()
                route.inc(V.tensor_tensor(gt[:], gt[:], eq[:], ALU.add))
                route.wait()
                dve.wait_ge(lg_exp, b + 1)
                route.inc(V.tensor_tensor(wx[:], ex[:], gt[:], ALU.mult))
                route.wait()
                route.inc(V.tensor_reduce(r4[:, 0, :], wx[:], AX.X, ALU.add))
                route.wait()
                route.inc(V.reciprocal(r4[:, 1, :], r4[:, 0, :]))
                route.wait()
                V.tensor_tensor(wx[:], wx[:], r4[:, 1, :].unsqueeze(2).to_broadcast([P, TB, E]), ALU.mult).then_inc(we_ready, 1)
                dve.wait_ge(we_hi, b + 1)
                V.tensor_tensor(we_t[32:32 + E, b * T:(b + 1) * T], WB[0:E, :], we_t[0:E, b * T:(b + 1) * T].bitcast(F32),
                                ALU.subtract).then_inc(we_lo, 1)
                for m in range(KC):
                    dve.wait_ge(b2_done, KC * b + m + 1)
                    xm = XT[:, m, b * T:(b + 1) * T]
                    V.tensor_tensor(xm, xm, DN[1 + m % 2][:], ALU.add).then_inc(b2_added, 1)

            def moe_lo(par, p, q):
                dve.wait_ge(mw_hi_ready, q + 1)
                o = slice(p * (MOE_W // 2), (p + 1) * (MOE_W // 2))
                V.tensor_tensor(mw_lo[:, par, o], m_stage[:], mw_hi[:, par, o].bitcast(F32), ALU.subtract).then_inc(w_split, 1)

            def moe_y(e, t):
                half, b = divmod(t, BATCH)
                k = e * (HALF * BATCH) + t
                for i in range(2):
                    c0 = e * 4 + half * 2 + i
                    y, tn = m_y[:, i, :], m_t[:, i, :]
                    dve.wait_ge(m_lin, 2 * k + i + 1)
                    V.scalar_tensor_tensor(y, UG[i][:], cols[:, bass.ds(c0 + COLS["b1_glu"], 1)], y, ALU.add,
                                           ALU.mult).then_inc(glu_used, 1)
                    dve.wait_ge(glu_used, 2 * k + i + 1)
                    V.scalar_tensor_tensor(y, tn, 1.0, y, ALU.add, ALU.mult).then_inc(m_act, 1)
                dve.wait_ge(wb_done, k + 1)
                for i in range(2):
                    y = m_y[:, i, :]
                    dve.wait_ge(m_act, 2 * k + i + 1)
                    V.tensor_tensor(y, y, WB[:], ALU.mult).then_inc(m_yready, 1)
                for i in range(2):
                    dve.wait_ge(y_hi_ready, 2 * k + i + 1)
                    V.tensor_tensor(my_lo[:, b % 2, i, :], m_y[:, i, :], my_hi[:, b % 2, i, :].bitcast(F32),
                                    ALU.subtract).then_inc(y_split, 1)

            def moe_add(e, t):
                b = t % BATCH
                k = e * (HALF * BATCH) + t
                for m in range(KC):
                    dve.wait_ge(moe_down, KC * k + m + 1)
                    xm = XT[:, m, b * T:(b + 1) * T]
                    V.tensor_tensor(xm, xm, DN[m % 3][:], ALU.add).then_inc(x_acc, 1)

            def tables(e):
                V.tensor_scalar(sel_e[:], sel_h[:, bass.ds(e, 1)].bitcast(F32).to_broadcast([64, P]), 0.5, None,
                                ALU.mult).then_inc(sel_ready, 1)
                V.tensor_scalar(bias_e[:, 0:4], bgs[:, bass.ds(e * 4, 4)], 1.0, None, ALU.mult).then_inc(bias_ready, 1)
                V.tensor_scalar(bias_e[:, 4:8], cols[:, bass.ds(e * 4 + COLS["b1_lin"], 4)], 1.0, None,
                                ALU.mult).then_inc(bias_ready, 1)

            tables(0)
            moe_lo(0, 0, 0)
            moe_lo(0, 1, 1)
            moe_y(0, 0)

            def expert_dve(e, last):
                two = e * (G_MOE // 2) + (G_PRE + G_MAMBA * BATCH) // 2
                for t in range(HALF * BATCH):
                    half, b = divmod(t, BATCH)
                    s = 2 * e + half
                    if t < HALF * BATCH - 1:
                        moe_y(e, t + 1)
                        if t == HALF * BATCH - 2 and not last:
                            tables(e + 1)
                    elif not last:
                        moe_y(e + 1, 0)
                    moe_add(e, t)
                    if b in (1, 2) and not (last and half):
                        moe_lo(1 - half, b - 1, 2 * (s + 1) + b - 1)
                    if b % 2 and not last:
                        gate(two, t // 2)

            with dve.Fori(0, E - 1) as e:
                expert_dve(e, False)
            expert_dve(E - 1, True)
            for b in range(BATCH):
                k = 2 * BATCH + b
                gated(k, flat(uf2), flat(tx2))
                split_u(k, b, uf2[:])
            with dve.Fori(0, GROUPS) as g:
                for p in range(2):
                    dve.wait_ge(aw_hi_ready, 2 * g + p + 1)
                    o = slice(p * (ATT_W // 2), (p + 1) * (ATT_W // 2))
                    V.tensor_tensor(aw_lo[:, o], a_stage[:], aw_hi[:, o].bitcast(F32), ALU.subtract).then_inc(aw_split, 1)
                with dve.Fori(0, BATCH) as b:
                    i = g * BATCH + b

                    def q_lo_split(h):
                        dve.wait_ge(q_hi_ready, HPG * i + h + 1)
                        V.tensor_tensor(q_lo[:, h % 2, :], PP[Q_BANK[h]][:], q_hi[:, h % 2, :].bitcast(F32),
                                        ALU.subtract).then_inc(q_split, 1)

                    def row_max(h):
                        dve.wait_ge(scores_done, HPG * i + h + 1)
                        for qb in range(TB):
                            bk, c0, _ = S_AT[qb]
                            V.tensor_reduce(rinv[:, h % 2, qb:qb + 1], S_[bk][:, c0:c0 + (qb + 1) * P], AX.X,
                                            ALU.max).then_inc(max_part, 1)
                        dve.wait_ge(max_part, TB * (HPG * i + h + 1))
                        V.tensor_scalar(nmx[:, h % 2, :], rinv[:, h % 2, :], -SCALE, None, ALU.mult).then_inc(max_ready, 1)

                    def normalise(h):
                        dve.wait_ge(exp_done, TB * (HPG * i + h + 1))
                        dve.wait_ge(max_ready, HPG * i + h + 1)
                        V.reciprocal(rinv[:, h % 2, :], rsum[:, h % 2, :]).then_inc(r_inv, 1)
                        dve.wait_ge(r_inv, HPG * i + h + 1)
                        for qb in range(TB):
                            pr = probs[:, h % 2, PR_AT[qb]:PR_AT[qb] + (qb + 1) * P]
                            V.tensor_scalar(pr, pr, rinv[:, h % 2, qb:qb + 1], None, ALU.mult).then_inc(p_ready, 1)

                    def pt_lo_split(h):
                        for r, (bk, w, c0) in enumerate(T_GROUP):
                            dve.wait_ge(pt_hi_ready, 3 * (HPG * i + h) + r + 1)
                            V.tensor_tensor(pt_lo[:, c0:c0 + w], TT_[bk][:, 0:w], pt_hi[:, c0:c0 + w].bitcast(F32),
                                            ALU.subtract).then_inc(pt_split, 1)

                    def ctx_lo(h):
                        dve.wait_ge(c_hi_ready, HPG * i + h + 1)
                        V.tensor_tensor(cx_lo[:, h, :], PP[C_BANK[h]][:], cx_hi[:, h, :].bitcast(F32),
                                        ALU.subtract).then_inc(c_split, 1)

                    dve.wait_ge(k_hi_ready, i + 1)
                    V.tensor_tensor(k_lo[:], PP[0][:], k_hi[:].bitcast(F32), ALU.subtract).then_inc(k_split, 1)
                    q_lo_split(0)
                    dve.wait_ge(v_hi_ready, i + 1)
                    V.tensor_tensor(v_lo[:], TT_[0][:].rearrange("p (a d) -> p a d", a=TB), v_hi[:].bitcast(F32),
                                    ALU.subtract).then_inc(v_split, 1)
                    q_lo_split(1)
                    row_max(0)
                    q_lo_split(2)
                    normalise(0)
                    row_max(1)
                    pt_lo_split(0)
                    normalise(1)
                    q_lo_split(3)
                    ctx_lo(0)
                    row_max(2)
                    pt_lo_split(1)
                    normalise(2)
                    ctx_lo(1)
                    row_max(3)
                    pt_lo_split(2)
                    normalise(3)
                    ctx_lo(2)
                    pt_lo_split(3)
                    ctx_lo(3)
                    for m in range(KC):
                        dve.wait_ge(dense_done, KC * i + m + 1)
                        xm = XT[:, m, tok(b)]
                        V.tensor_tensor(xm, xm, PP[D_BANK[m]][:], ALU.add).then_inc(ax_acc, 1)
            for b in range(BATCH):
                k = 3 * BATCH + b
                gated(k, flat(uf3), flat(tx3))
                split_u(k, b, uf3[:])

            def ffn_lo(s, par):
                dve.wait_ge(fw_hi_ready, s + 1)
                V.tensor_tensor(fw_lo[:, par, :], f_stage[:, par, :], fw_hi[:, par, :].bitcast(F32),
                                ALU.subtract).then_inc(fw_split, 1)

            def ffn_y(s, b):
                k = s * BATCH + b
                dve.wait_ge(f_tanh, k + 1)
                V.scalar_tensor_tensor(f_t[:], f_t[:], 1.0, FG[b % 2][:], ALU.add, ALU.mult).then_inc(f_used, 1)
                dve.wait_ge(f_lin, k + 1)
                dve.wait_ge(f_used, k + 1)
                V.tensor_tensor(f_y[:], f_t[:], f_u[:], ALU.mult).then_inc(f_yready, 1)
                dve.wait_ge(f_hi_ready, k + 1)
                V.tensor_tensor(f_lo[:, b % 2, :], f_y[:], f_hi[:, b % 2, :].bitcast(F32), ALU.subtract).then_inc(f_split, 1)

            def ffn_add(s, b):
                for m in range(KC):
                    dve.wait_ge(f_down, KC * (s * BATCH + b) + m + 1)
                    xm = XT[:, m, b * T:(b + 1) * T]
                    V.scalar_tensor_tensor(xm, FD[m][:], col("down_s", m), xm, ALU.mult, ALU.add).then_inc(fx_acc, 1)

            def scales(s):
                V.tensor_scalar(f_sc[:, 0:1], gsh[:, bass.ds(s, 1)], 1.0, None, ALU.mult).then_inc(f_scaled, 1)
                V.tensor_scalar(f_sc[:, 1:2], ush[:, bass.ds(s, 1)], 1.0, None, ALU.mult).then_inc(f_scaled, 1)

            scales(0)
            ffn_lo(0, 0)
            ffn_y(0, 0)

            def ffn_dve(s, par, last):
                for b in range(BATCH):
                    if b < BATCH - 1:
                        ffn_y(s, b + 1)
                        if b == BATCH - 2 and not last:
                            scales(s + 1)
                    elif not last:
                        ffn_y(s + 1, 0)
                    ffn_add(s, b)
                    if b == 1 and not last:
                        ffn_lo(s + 1, 1 - par)

            with dve.Fori(0, FS // 2) as it:
                ffn_dve(it * 2, 0, False)
                ffn_dve(it * 2 + 1, 1, False)
            ffn_dve(FS - 1, 0, True)

        @block.tensor
        def _(pe):
            M = nc.tensor.matmul
            pe.wait_ge(masks_ready, N_MASKS)
            pe.wait_ge(loaded, 48)
            M(bank[0][:, 0:BATCH], ones[:], condT_s[:], start=True, stop=True).then_inc(setup_mm, 1)
            pe.wait_ge(w_loaded, 32)
            with pe.Fori(0, BATCH) as b:
                pe.wait_ge(u_ready, b + 1)
                for tb in range(TB):
                    for k in range(KC):
                        mm = M(SM[:, tb * HEADS_M:(tb + 1) * HEADS_M], um[:, k, tb * P:(tb + 1) * P], w_in[:, k, DT_COL:IN_COLS],
                               start=(k == 0), stop=(k == KC - 1))
                mm.then_inc(dt_raw, 1)

                def project(dst, c0):
                    for k in range(KC):
                        mm = M(dst[:], w_in[:, k, c0:c0 + P], um[:, k, :], start=(k == 0), stop=(k == KC - 1))
                    return mm

                for q, ch in enumerate(CONV_ORDER):
                    if q >= 2:
                        pe.wait_ge(conv_tapped, N_CONV * b + q - 1)
                    project(PJ[q % 2], D_IN + ch * P).then_inc(proj_done, 1)
                    if q == 3:
                        pe.wait_ge(dA_ready, b + 1)
                        M(SM[:, 64:64 + NB], tri[:], d_A[:], start=True, stop=True)
                        M(SM[:, 128:128 + NB], ones[:], d_A[:], start=True, stop=True)
                        for tb in range(TB):
                            mm = M(EB[0:HEADS_M, tb * P:(tb + 1) * P], d_A[:, tb * HEADS_M:(tb + 1) * HEADS_M], tri[:],
                                   start=True, stop=True)
                        mm.then_inc(cs_done, 1)
                pe.wait_ge(act_ready, N_CONV * (b + 1))
                for tb in range(TB):
                    o = slice(tb * P, (tb + 1) * P)
                    if tb:
                        pe.wait_ge(xdt_done, TB * b + tb)
                    for ch in range(XC):
                        mm = nc.tensor.transpose((R0, R1)[ch // 4][:, (ch % 4) * P:(ch % 4 + 1) * P], xa[:, ch, o], ident[:])
                    mm.then_inc(x_transposed, 1)
                    if tb:
                        pe.wait_ge(bc_copied, 2 * (TB * b + tb))
                    nc.tensor.transpose(SM[:, 192:320], bT[:, o], ident[:])
                    M(SM[:, 320:448], bT[:, o], cT[:, o], start=True, stop=True).then_inc(bc_done, 1)
                    if tb < TB - 1:
                        pe.wait_ge(xdt_done, TB * b + tb + 1)
                        pe.wait_ge(bc_copied, 2 * (TB * b + tb + 1))
                        if tb:
                            pe.wait_ge(state_done, (TB - 1) * b + tb)
                        for half in range(2):
                            mm = M(PJ[half][:], b_tok[:, tb, :], xdt2[:, half * 512:(half + 1) * 512], start=True, stop=True)
                        mm.then_inc(s_done, 1)

                def z_chunk(j):
                    if j >= 2:
                        pe.wait_ge(zs_done, PAIRS * b + j - 1)
                    else:
                        pe.wait_ge(state_done, (TB - 1) * (b + 1))
                    project(PJ[j % 2], j * P).then_inc(z_done, 1)

                def sums(j):
                    if j:
                        pe.wait_ge(l_done, 9 * (PAIRS * b + j))
                    for hh in range(2):
                        M((R0, R1)[hh][:], ident_b[:], neg4[:].rearrange("p a l -> p (a l)"), start=True, stop=False)
                        M((R0, R1)[hh][:], sel_h[:, 2 * j + hh:2 * j + hh + 1].to_broadcast([64, P]), csT[:], start=False, stop=True)
                    M(EB[:], sel_p[:, j, :], csT[:], start=True, stop=True).then_inc(r_done, 1)

                z_chunk(0)
                pe.wait_ge(ct_ready, b + 1)
                pe.wait_ge(xdt_done, TB * (b + 1))
                sums(0)
                pe.wait_ge(bc_copied, 2 * TB * (b + 1))
                for j in range(PAIRS):
                    if j < PAIRS - 1:
                        z_chunk(j + 1)
                        sums(j + 1)
                    pe.wait_ge(m_ready, 2 * (PAIRS * b + j + 1))
                    if j:
                        pe.wait_ge(y_done, PAIRS * b + j)
                    for hh in range(2):
                        for tb in range(TB):
                            M(YD[hh * HD:(hh + 1) * HD, tb * P:(tb + 1) * P], xdt[:, tb, (2 * j + hh) * HD:(2 * j + hh + 1) * HD],
                              lm[:, hh, tb * P:(tb + 1) * P], start=True, stop=True)
                    for tb in range(1, TB):
                        mm = M(YO[:, tb * P:(tb + 1) * P], state[:, tb - 1, j * P:(j + 1) * P], cT[:, tb * P:(tb + 1) * P],
                               start=True, stop=True)
                    mm.then_inc(yy_done, 1)
                pe.wait_ge(sq_added, (PAIRS - 1) * (b + 1))
                M(EB[:], ones[:], ssum[:], start=True, stop=True).then_inc(ssq_done, 1)
                for m in range(KC):
                    if m >= 2:
                        pe.wait_ge(x_added, KC * b + m - 1)
                    for j in range(XC):
                        if m == 0:
                            pe.wait_ge(yn_ready, XC * b + j + 1)
                        mm = M(PJ[m % 2][:], w_out[:, j, m * P:(m + 1) * P], xa[:, j, :], start=(j == 0), stop=(j == XC - 1))
                    mm.then_inc(out_done, 1)
            pe.wait_ge(x_added, KC * BATCH)
            pe.wait_ge(moe_loaded, 48)
            for b in range(BATCH):
                pe.wait_ge(u_ready, BATCH + b + 1)
                if b:
                    pe.wait_ge(lg_sub, b)
                for tb in range(TB):
                    for k in range(KC):
                        mm = M(DN[0][:, tb * E:(tb + 1) * E], uf1[:, k, tb * P:(tb + 1) * P], gw[:, k, :],
                               start=(k == 0), stop=(k == KC - 1))
                mm.then_inc(logit_done, 1)
                pe.wait_ge(we_ready, b + 1)
                if b:
                    pe.wait_ge(we_lo, b)
                for tb in range(TB):
                    mm = nc.tensor.transpose(WB[0:E, tb * P:(tb + 1) * P], wx[:, tb, :], ident[:])
                mm.then_inc(we_T, 1)
                pe.wait_ge(we_lo, b + 1)
                for m in range(KC):
                    if KC * b + m >= 2:
                        pe.wait_ge(b2_added, KC * b + m - 1)
                    M(DN[1 + m % 2][:], b2_s[:, m * P:(m + 1) * P], we_t[:, b * T:(b + 1) * T].bitcast(F32),
                      start=True, stop=True).then_inc(b2_done, 1)
            pe.wait_ge(b2_added, KC * BATCH)

            def moe_up(e, t):
                half, b = divmod(t, BATCH)
                k = e * (HALF * BATCH) + t
                pe.wait_ge(glu_used, 2 * k)
                if b == 0:
                    pe.wait_ge(w_split, 2 * (2 * e + half + 1))
                for i in range(2):
                    for dst, gl in ((UG[i], 0), (UL[i], 1)):
                        for kc in range(KC):
                            o = slice(kc * 512 + gl * 256 + i * P, kc * 512 + gl * 256 + (i + 1) * P)
                            x = slice(b * T, (b + 1) * T)
                            mm = three(dst[:], mw_hi[:, half, o], mw_lo[:, half, o], u_hi[:, kc, x], u_lo[:, kc, x],
                                       kc == 0, kc == KC - 1)
                    mm.then_inc(up_done, 1)
                if t == 0:
                    pe.wait_ge(sel_ready, e + 1)
                pe.wait_ge(m_yready, 2 * k)
                M(WB[:], sel_e[:], we_t[:, b * T:(b + 1) * T], start=True, stop=True).then_inc(wb_done, 1)

            def moe_down_mm(e, t):
                half, b = divmod(t, BATCH)
                k = e * (HALF * BATCH) + t
                pe.wait_ge(y_split, 2 * (k + 1))
                for m in range(KC):
                    pe.wait_ge(x_acc, KC * k + (1 if m == 3 else 0))
                    for i in range(2):
                        o = slice(MOE_UP + i * C + m * P, MOE_UP + i * C + (m + 1) * P)
                        mm = three(DN[m % 3][:], mw_hi[:, half, o], mw_lo[:, half, o], my_hi[:, b % 2, i, :], my_lo[:, b % 2, i, :],
                                   i == 0, i == 1)
                    mm.then_inc(moe_down, 1)

            pe.wait_ge(u_split, BATCH)
            moe_up(0, 0)

            def expert_pe(e, last):
                for t in range(HALF * BATCH):
                    if t < HALF * BATCH - 1:
                        moe_up(e, t + 1)
                    elif not last:
                        moe_up(e + 1, 0)
                    moe_down_mm(e, t)

            with pe.Fori(0, E - 1) as e:
                expert_pe(e, False)
            expert_pe(E - 1, True)
            pe.wait_ge(x_acc, KC * BATCH * E * HALF)
            pe.wait_ge(u_split, 2 * BATCH)
            with pe.Fori(0, GROUPS) as g:
                with pe.Fori(0, BATCH) as b:
                    i = g * BATCH + b

                    def project(dst, at, width, c0):
                        for kc in range(KC):
                            o = slice(at + kc * width + c0, at + kc * width + c0 + P)
                            mm = three(dst[:], aw_hi[:, o], aw_lo[:, o], u_hi[:, kc, tok(b)], u_lo[:, kc, tok(b)],
                                       kc == 0, kc == KC - 1)
                        return mm

                    def query(h):
                        project(PP[Q_BANK[h]], A_Q, C, h * DH).then_inc(q_done, 1)

                    def scores(h):
                        pe.wait_ge(q_split, HPG * i + h + 1)
                        pe.wait_ge(exp_done, TB * (HPG * i + h))
                        for qb in range(TB - 1, -1, -1):
                            bk, c0, w = S_AT[qb]
                            qs = slice(qb * P, (qb + 1) * P)
                            d = S_[bk][:, c0:c0 + w]
                            three(d, q_hi[:, h % 2, qs], q_lo[:, h % 2, qs], k_hi[:, 0:w], k_lo[:, 0:w], True, False)
                            mm = M(S_[bk][:, c0 + qb * P:c0 + (qb + 1) * P], ident_b[:], causal_b[:], start=False, stop=True)
                        mm.then_inc(scores_done, 1)

                    def transposes(h):
                        pe.wait_ge(p_ready, TB * (HPG * i + h + 1))
                        n = 3 * (HPG * i + h)
                        for r, blocks in enumerate((((0, 0),), ((1, 0), (3, 384)), ((2, 0),))):
                            bk = T_GROUP[r][0]
                            pe.wait_ge(pt_split, n + (1 if r == 2 else 0))
                            for kb, c0 in blocks:
                                for qb in range(kb, TB):
                                    o = PR_AT[qb] + kb * P
                                    mm = nc.tensor.transpose(TT_[bk][:, c0 + (qb - kb) * P:c0 + (qb - kb + 1) * P],
                                                             probs[:, h % 2, o:o + P], ident[:])
                            mm.then_inc(t_done, 1)

                    def context(h):
                        pe.wait_ge(pt_split, 3 * (HPG * i + h + 1))
                        for kb in range(TB):
                            o, w = PT_AT[kb]
                            mm = three(PP[C_BANK[h]][:, kb * P:T], v_hi[:, kb, :], v_lo[:, kb, :], pt_hi[:, o:o + w], pt_lo[:, o:o + w],
                                       kb == 0, kb == TB - 1)
                        mm.then_inc(c_done, 1)

                    pe.wait_ge(aw_split, 2 * (g + 1))
                    pe.wait_ge(ax_acc, KC * i)
                    project(PP[0], A_K, P, 0).then_inc(k_done, 1)
                    project(PP[1], A_V, P, 0).then_inc(v_done, 1)
                    query(0)
                    pe.wait_ge(vt_copied, i + 1)
                    pe.wait_ge(pt_split, 3 * HPG * i)
                    for tb in range(TB):
                        mm = nc.tensor.transpose(TT_[0][:, tb * P:(tb + 1) * P], vT[:, tb * P:(tb + 1) * P], ident[:])
                    mm.then_inc(vt_done, 1)
                    pe.wait_ge(k_split, i + 1)
                    query(1)
                    scores(0)
                    query(2)
                    scores(1)
                    pe.wait_ge(v_split, i + 1)
                    transposes(0)
                    query(3)
                    context(0)
                    scores(2)
                    transposes(1)
                    context(1)
                    scores(3)
                    transposes(2)
                    pe.wait_ge(c_split, HPG * i + 1)
                    context(2)
                    transposes(3)
                    context(3)
                    pe.wait_ge(c_split, HPG * (i + 1))
                    for m in range(KC):
                        if m == 3:
                            pe.wait_ge(ax_acc, KC * i + 1)
                        for h in range(HPG):
                            o = slice(A_D + h * C + m * P, A_D + h * C + (m + 1) * P)
                            mm = three(PP[D_BANK[m]][:], aw_hi[:, o], aw_lo[:, o], cx_hi[:, h, :], cx_lo[:, h, :], h == 0, h == HPG - 1)
                        mm.then_inc(dense_done, 1)
            pe.wait_ge(ax_acc, KC * BATCH * GROUPS)
            pe.wait_ge(u_split, 3 * BATCH)

            def ffn_up(s, par, b):
                k = s * BATCH + b
                if b == 0:
                    pe.wait_ge(fw_split, s + 1)
                if not (isinstance(s, int) and s == 0 and b < 2):
                    pe.wait_ge(f_yready, k - 1)
                x = slice(b * T, (b + 1) * T)
                for dst, gu in ((FG[b % 2], 0), (FU[b % 2], 1)):
                    for kc in range(KC):
                        o = slice(kc * 256 + gu * P, kc * 256 + (gu + 1) * P)
                        mm = three(dst[:], fw_hi[:, par, o], fw_lo[:, par, o], u_hi[:, kc, x], u_lo[:, kc, x], kc == 0, kc == KC - 1)
                mm.then_inc(f_up, 1)

            def ffn_down(s, par, b):
                k = s * BATCH + b
                pe.wait_ge(f_split, k + 1)
                pe.wait_ge(fx_acc, KC * k)
                for m in range(KC):
                    o = slice(FFN_UP + m * P, FFN_UP + (m + 1) * P)
                    three(FD[m][:], fw_hi[:, par, o], fw_lo[:, par, o], f_hi[:, b % 2, :], f_lo[:, b % 2, :], True, True).then_inc(f_down, 1)

            ffn_up(0, 0, 0)

            def ffn_pe(s, par, last):
                for b in range(BATCH):
                    if b < BATCH - 1:
                        ffn_up(s, par, b + 1)
                    elif not last:
                        ffn_up(s + 1, 1 - par, 0)
                    ffn_down(s, par, b)

            with pe.Fori(0, FS // 2) as it:
                ffn_pe(it * 2, 0, False)
                ffn_pe(it * 2 + 1, 1, False)
            ffn_pe(FS - 1, 0, True)


_SHAPES = dict(xT=(C, BATCH * T), fT=(TILES, P, T), condT=(P, BATCH), cols=(P, N_COLS), rows=(P, N_ROWS),
               w_in=(P, KC, IN_COLS), w_out=(P, XC, C), moe=(E * HALF, P, MOE_W), gw=(P, KC, E), b2=(E, C),
               att=(GROUPS, P, ATT_W), ffn=(FS, P, FFN_W))


def lay_out(i):
    i = {k: np.asarray(v) for k, v in i.items()}
    chunks = lambda v: v.reshape(-1, P).T
    b1 = i["L0_ffn_b1"].reshape(E, I_MOE // P, P, 2)
    gates = ("L0_cond", "L0_cond2", "L1_cond", "L1_cond2")
    conv = i["L0_attn_conv_w"].reshape(N_CONV, P, 4).transpose(1, 0, 2).reshape(P, -1)
    d_skip = np.repeat(i["L0_attn_D_skip"], HD)
    cols = np.concatenate(
        [chunks(i[g + "_u"]) for g in gates] + [chunks(i[g + "_w"]) for g in gates]
        + [conv, chunks(i["L0_attn_conv_b"]), chunks(i["L0_attn_norm_w"]), chunks(d_skip),
           b1[..., 0].transpose(2, 0, 1).reshape(P, -1), b1[..., 1].transpose(2, 0, 1).reshape(P, -1),
           chunks(i["L1_ffn_gate_s"]), chunks(i["L1_ffn_up_s"]), chunks(i["L1_ffn_down_s"])], axis=1)
    row = np.concatenate([i["L0_attn_dt_bias"], i["L0_attn_A_log"], i["L0_ffn_gate_b"]])
    w1 = i["L0_ffn_w1"].reshape(E, HALF, 2 * P, 2, KC, P).transpose(0, 1, 5, 4, 3, 2).reshape(E * HALF, P, MOE_UP)
    w2 = i["L0_ffn_w2"].reshape(E, C, HALF, 2, P).transpose(0, 2, 4, 3, 1).reshape(E * HALF, P, MOE_DN)
    wq = i["L1_attn_w_q"].reshape(KC, P, GROUPS, HPG * DH).transpose(2, 1, 0, 3).reshape(GROUPS, P, -1)
    wkv = i["L1_attn_w_kv"].reshape(KC, P, 2, GROUPS, DH).transpose(2, 3, 1, 0, 4).reshape(2, GROUPS, P, -1)
    wd = i["L1_attn_w_dense"].reshape(GROUPS, HPG, DH, C).transpose(0, 2, 1, 3).reshape(GROUPS, P, -1)
    up = np.stack([i["L1_ffn_gate_w"], i["L1_ffn_up_w"]]).reshape(2, FS, P, KC, P).transpose(1, 4, 3, 0, 2).reshape(FS, P, -1)
    down = i["L1_ffn_down_w"].reshape(C, FS, P).transpose(1, 2, 0)
    out = dict(
        xT=i["x"].transpose(2, 0, 1).reshape(C, -1),
        fT=i["fside_BxSxS_0"].transpose(0, 2, 1).reshape(TILES, P, T),
        condT=i["cond_512"].T, cols=cols, rows=np.broadcast_to(row, (P, N_ROWS)),
        w_in=i["L0_attn_in_proj_w"].T.reshape(KC, P, IN_COLS).transpose(1, 0, 2),
        w_out=i["L0_attn_out_proj_w"].T.reshape(XC, P, C).transpose(1, 0, 2),
        moe=np.concatenate([w1, w2], axis=2), gw=i["L0_ffn_gate_w"].T.reshape(KC, P, E).transpose(1, 0, 2),
        b2=i["L0_ffn_b2"], att=np.concatenate([wq, wkv[0], wkv[1], wd], axis=2), ffn=np.concatenate([up, down], axis=2))
    return {k: np.ascontiguousarray(v) for k, v in out.items()}


def build(nc):
    aps = [nc.dram_tensor(f"in_{n}", s, F32, kind="ExternalInput").ap() for n, s in _SHAPES.items()]
    out = nc.dram_tensor("outT", (C, BATCH * T), F32, kind="ExternalOutput").ap()
    network(nc, *aps, out)


def kernel(**inputs):
    import concourse.bacc as bacc
    from concourse.bass_utils import run_bass_kernel_spmd

    nc = bacc.Bacc("TRN2", target_bir_lowering=False, num_devices=1)
    build(nc)
    arrays = {f"in_{k}": v for k, v in lay_out(inputs).items()}
    r = run_bass_kernel_spmd(nc, [arrays], core_ids=[0])
    return np.ascontiguousarray(r.results[0]["outT"].reshape(C, BATCH, T).transpose(1, 2, 0))
```

```python
from contextlib import ExitStack

import numpy as np
import concourse.bass as bass
from concourse import mybir

F32, F32R, BF16, I32 = mybir.dt.float32, mybir.dt.float32r, mybir.dt.bfloat16, mybir.dt.int32
ALU, ACT, AX = mybir.AluOpType, mybir.ActivationFunctionType, mybir.AxisListType

P = 128
BATCH, T, C = 4, 512, 512
KC = C // P
TB = T // P
N_GATES = 4
TILES = BATCH * KC
EXP30 = float(np.exp(np.float32(30.0)))
HEADS_M, HD, D_IN = 16, 64, 1024
XC = D_IN // P
N_CONV = XC + 2
IN_COLS = 2 * D_IN + 2 * P + HEADS_M
DT_COL = 2 * D_IN + 2 * P
PAIRS = HEADS_M // 2
EPS = 1e-5
E, I_MOE = 8, 512
M_PIECES, M_PIECE = 3, KC * I_MOE
MOE_W = M_PIECES * M_PIECE
TOKENS = BATCH * T
NT = TOKENS // P
NBLK = (2 * TOKENS + E * (P - 1)) // P
ROUND = 1.5 * 2 ** 23
RC = {}
_at = 0
for _name, _n in (("iota", P), ("before", P), ("rst", NT * E), ("rst2", NT * E), ("full", NT), ("blk", 2 * NT), ("place", 1)):
    RC[_name] = _at
    _at += _n
N_RC = _at
GROUPS, HPG, DH = 4, 4, 128
SCALE = DH ** -0.5
A_Q, A_K, A_V, A_D = 0, KC * 512, KC * 512 + C, KC * 512 + 2 * C
ATT_W = A_D + HPG * C
FS = 11
FFN_UP, FFN_W = KC * 256, KC * 256 + C
NEG = -1e30

COLS = {}
_at = 0
for _name, _n in (("u", 16), ("w", 16), ("conv_w", 4 * N_CONV), ("conv_b", N_CONV), ("norm_w", XC), ("d_skip", XC),
                  ("gate_s", FS), ("up_s", FS), ("down_s", KC)):
    COLS[_name] = _at
    _at += _n
N_COLS = _at
N_ROWS = 2 * HEADS_M + E
G_PRE, G_MAMBA = 6, 8
G_STEPS = 14


def network(nc, xT, fT, condT, cols_d, rows_d, w_in_d, w_out_d, moe_d, gw_d, bias_d, rc_d, att_d, ffn_d, outT):
    g_dram = nc.dram_tensor("gates", (N_GATES * TILES, P, T), F32, kind="Internal").ap()
    u_dram = nc.dram_tensor("u_tok", (TOKENS, C), F32, kind="Internal").ap()
    y_dram = nc.dram_tensor("y_slot", (NBLK * P, C), F32, kind="Internal").ap()
    x_view = xT.rearrange("(k p) n -> p k n", p=P)
    o_view = outT.rearrange("(k p) n -> p k n", p=P)
    ctx = ExitStack()
    with ctx:
        def sem(name):
            return ctx.enter_context(nc.semaphore(name))

        def sb(name, shape, dt=F32, stack=ctx):
            return stack.enter_context(nc.sbuf_tensor(name, shape, dt))

        XT = sb("XT", [P, KC, BATCH * T])
        cols = sb("cols", [P, N_COLS])
        rows = sb("rows", [P, N_ROWS])
        u_all = sb("u_all", [P, N_GATES * TILES])
        decay = sb("decay", [P, N_GATES * TILES])
        oscale = sb("oscale", [P, N_GATES * TILES])
        ident = sb("ident", [P, P])
        ident_b = sb("ident_b", [P, P], BF16)
        ones = sb("ones", [P, P])
        sel_h = sb("sel_h", [64, HEADS_M], F32R)
        causal_b = sb("causal_b", [P, P], BF16)
        gsh = sb("gsh", [P, FS])
        ush = sb("ush", [P, FS])
        pos_i = sb("pos_i", [P, 2, NT], I32)
        we = sb("we", [P, 2, NT])
        f_sc = sb("f_sc", [P, 2])
        nmx = sb("nmx", [P, 2, TB])
        rsum = sb("rsum", [P, 2, TB])
        rinv = sb("rinv", [P, 2, TB])
        g_v = sb("g_v", [P, 2, T])
        bank = [ctx.enter_context(nc.psum_tensor(f"bank{i}", [P, 512], F32)) for i in range(8)]

        def col(name, i):
            return cols[:, COLS[name] + i:COLS[name] + i + 1]

        with ExitStack() as s:
            condT_s = sb("condT_s", [P, BATCH], F32, s)
            tf = sb("tf", [P, BATCH], F32, s)
            fac = sb("fac", [P, BATCH], F32, s)
            osc = sb("osc", [P, BATCH], F32, s)
            dec0 = sb("dec0", [P, 16], F32, s)
        gs_ = ctx.enter_context(ExitStack())
        g_ek = sb("g_ek", [P, 2, T], F32, gs_)
        g_eu = sb("g_eu", [P, 2, T], F32, gs_)
        g_e = sb("g_e", [P, T], F32, gs_)
        g_f = sb("g_f", [P, T], F32, gs_)
        g_r = sb("g_r", [P, T], F32, gs_)
        with ExitStack() as s:
            w_in = sb("w_in", [P, KC, IN_COLS], F32, s)
            w_out = sb("w_out", [P, XC, C], F32, s)
            um = sb("um", [P, KC, T], F32, s)
            txm = sb("txm", [P, KC, T], F32, s)
            tri = sb("tri", [P, P], F32, s)
            neg4 = sb("neg4", [P, TB, P], BF16, s)
            sel_p = sb("sel_p", [64, PAIRS, P], F32R, s)
            xa = sb("xa", [P, XC, T], F32, s)
            bT = sb("bT", [P, T], F32, s)
            cT = sb("cT", [P, T], F32, s)
            b_tok = sb("b_tok", [P, TB, P], F32, s)
            cb = sb("cb", [P, TB, P], F32, s)
            xdt = sb("xdt", [P, TB, D_IN], F32, s)
            xdt2 = sb("xdt2", [P, D_IN], F32, s)
            state = sb("state", [P, TB - 1, D_IN], F32, s)
            csT = sb("csT", [64, T], F32R, s)
            lm = sb("lm", [P, 2, T], F32, s)
            e2 = sb("e2", [P, T], F32, s)
            tz = sb("tz", [P, T], F32, s)
            sq = sb("sq", [P, T], F32, s)
            ssum = sb("ssum", [P, T], F32, s)
            NB = TB * HEADS_M
            d_x, d_a, d_e, d_s, d_p, d_q, dt_t, d_A, csn, w2, w2e, dts, cdec = (
                sb(f"dt{i}", [P, NB], F32, s) for i in range(13))
            a_neg = sb("a_neg", [P, HEADS_M], F32, s)
            eps_c = sb("eps_c", [P, 1], F32, s)
        acc = [lm[:, 0, :], lm[:, 1, :]]
        cth = [e2[:, :], tz[:, :]]
        with ExitStack() as s:
            m_stage = sb("m_stage", [P, MOE_W], F32, s)
            mw = sb("mw", [P, 2, 2, MOE_W], F32R, s)
            ug = sb("ug", [P, 3, C], F32, s)
            bu_hi = sb("bu_hi", [P, KC, P], F32R, s)
            bu_lo = sb("bu_lo", [P, KC, P], F32R, s)
            m_t = sb("m_t", [P, I_MOE], F32, s)
            m_y = sb("m_y", [P, I_MOE], F32, s)
            by_hi = sb("by_hi", [P, KC, P], F32R, s)
            by_lo = sb("by_lo", [P, KC, P], F32R, s)
            m_o = sb("m_o", [P, 3, C], F32, s)
            bias_r = sb("bias_r", [64, 2 * I_MOE + C], F32R, s)
            sel_e = sb("sel_e", [64, 3, P], F32R, s)
            idx = sb("idx", [P, NBLK], I32, s)
            tab = sb("tab", [P, 3, NBLK + 1], I32, s)
        with ExitStack() as s:
            sb("pad_m", [P, 3, MOE_W], F32, s)
            rc = sb("rc", [P, N_RC], F32, s)
            gw = sb("gw", [P, KC, E], F32, s)
            bias_f = sb("bias_f", [64, 2 * I_MOE + C], F32, s)
            tx1 = sb("tx1", [P, KC, T], F32, s)
            lgT = sb("lgT", [E, 2, T], F32, s)
            lg, ex, gt, eq, pre, wx, sel1, sel2, posm, incl, excl, rtmp = (sb(f"rt{i}", [P, NT, E], F32, s) for i in range(12))
            mx8 = sb("mx8", [P, NT, 8], F32, s)
            r4 = sb("r4", [P, 2, NT], F32, s)
            nb = sb("nb", [P, 3, E], F32, s)
            posf = sb("posf", [P, 3, 2, NT], F32, s)
            etab = sb("etab", [P, 3, NBLK + 1], F32, s)
            ecmp = sb("ecmp", [P, NBLK + 1, E], F32, s)
            idx_f = sb("idx_f", [P, NBLK], F32, s)
            with ExitStack() as s2:
                uf1 = sb("uf1", [P, BATCH, KC, T], F32, s2)
                ut = sb("ut", [P, 4, C], F32, s2)
            with ExitStack() as s2:
                oh_r = sb("oh_r", [P, 2 * NT, P], BF16, s2)
                oh_j = sb("oh_j", [P, 2 * NT, NBLK], F32, s2)
                oh_v = sb("oh_v", [P, 2 * NT, 2, NBLK], BF16, s2)
        gs_.close()
        with ExitStack() as s:
            probs = sb("probs", [P, 2, 1280], F32, s)
            vT = sb("vT", [P, T], F32, s)
            k_hi = sb("k_hi", [P, T], F32R, s)
            with ExitStack() as s2:
                u_g = sb("u_g", [P, KC, BATCH * T], F32, s2)
                u_in = sb("u_in", [P, KC, BATCH * T], F32, s2)
                sb("pad_a", [P, ATT_W], F32, s2)
                aw_in = sb("aw_in", [P, ATT_W], F32, s2)
            u_hi = sb("u_hi", [P, KC, BATCH * T], F32R, s)
            u_lo = sb("u_lo", [P, KC, BATCH * T], F32R, s)
            with ExitStack() as s2:
                aw_hi = sb("aw_hi", [P, ATT_W], F32R, s2)
                aw_lo = sb("aw_lo", [P, ATT_W], F32R, s2)
                og = sb("og", [P, 2, 2, C], F32, s2)
                k_lo = sb("k_lo", [P, T], F32R, s2)
                v_hi = sb("v_hi", [P, TB, P], F32R, s2)
                v_lo = sb("v_lo", [P, TB, P], F32R, s2)
                q_hi = sb("q_hi", [P, 2, T], F32R, s2)
                q_lo = sb("q_lo", [P, 2, T], F32R, s2)
                pt_hi = sb("pt_hi", [P, 1280], F32R, s2)
                pt_lo = sb("pt_lo", [P, 1280], F32R, s2)
                cx_hi = sb("cx_hi", [P, HPG, T], F32R, s2)
                cx_lo = sb("cx_lo", [P, HPG, T], F32R, s2)
            with ExitStack() as s2:
                fw_hi = sb("fw_hi", [P, 2, FFN_W], F32R, s2)
                fw_lo = sb("fw_lo", [P, 2, FFN_W], F32R, s2)
                f_stage = sb("f_stage", [P, 2, FFN_W], F32, s2)
                uf3 = sb("uf3", [P, KC, T], F32, s2)
                tx3 = sb("tx3", [P, KC, T], F32, s2)
                f_hi = sb("f_hi", [P, 2, T], F32R, s2)
                f_lo = sb("f_lo", [P, 2, T], F32R, s2)
                f_t = sb("f_t", [P, T], F32, s2)
                f_u = sb("f_u", [P, T], F32, s2)
                f_y = sb("f_y", [P, T], F32, s2)

        loaded, x_loaded, w_loaded = sem("loaded"), sem("x_loaded"), sem("w_loaded")
        masks_ready, setup_step, setup_mm, setup_act = sem("masks_ready"), sem("setup_step"), sem("setup_mm"), sem("setup_act")
        g_in = [sem(f"g_in{i}") for i in range(2)]
        g_out = [sem(f"g_out{i}") for i in range(2)]
        g_exp, g_step = sem("g_exp"), sem("g_step")
        gm_fetched, x_tanh, u_ready = sem("gm_fetched"), sem("x_tanh"), sem("u_ready")
        g_fetched = [sem(f"g_fetched{b}") for b in range(BATCH)]
        u_hi_ready, u_split = sem("u_hi_ready"), sem("u_split")
        dve_step = sem("dve_step")
        dt_raw, dt_abs, dt_exp, dA_ready = sem("dt_raw"), sem("dt_abs"), sem("dt_exp"), sem("dA_ready")
        proj_done, tap0, conv_tapped, conv_tanh, act_ready = (
            sem("proj_done"), sem("tap0"), sem("conv_tapped"), sem("conv_tanh"), sem("act_ready"))
        cs_done, cs_neg, w_exp, ct_hi, ct_ready = sem("cs_done"), sem("cs_neg"), sem("w_exp"), sem("ct_hi"), sem("ct_ready")
        x_transposed, xdt_done, bc_done, bc_copied = sem("x_transposed"), sem("xdt_done"), sem("bc_done"), sem("bc_copied")
        s_done, state_done = sem("s_done"), sem("state_done")
        z_done, z_tanh, zs_done = sem("z_done"), sem("z_tanh"), sem("zs_done")
        r_done, l_done, m_ready, yy_done, y_done = sem("r_done"), sem("l_done"), sem("m_ready"), sem("yy_done"), sem("y_done")
        sq_added = sem("sq_added")
        sq_done, ssum_ready, ssq_done, rms_done, yn_ready = (
            sem("sq_done"), sem("ssum_ready"), sem("ssq_done"), sem("rms_done"), sem("yn_ready"))
        out_done, x_added = sem("out_done"), sem("x_added")
        moe_loaded = sem("moe_loaded")
        lgt_done, lgt_copied, lgt_used, ut_T = sem("lgt_done"), sem("lgt_copied"), sem("lgt_used"), sem("ut_T")
        ut_copied = [sem(f"ut_copied{i}") for i in range(2)]
        ut_stored = [sem(f"ut_stored{i}") for i in range(4)]
        route_mm, route_vec, lg_exp = sem("route_mm"), sem("route_vec"), sem("lg_exp")
        LGP_DONE, U_DONE, PREFIX_DONE, IDX_DONE = 1, 2, 3, 4
        LG_SUB, MASK_READY, ONEHOT_READY, TAB_READY, IDX_READY = 1, 2, 3, 4, 5
        m_staged = [sem(f"m_staged{i}") for i in range(M_PIECES)]
        mw_hi_ready, w_split, sel_ready = sem("mw_hi_ready"), sem("w_split"), sem("sel_ready")
        gathered = [sem(f"gathered{i}") for i in range(3)]
        y_stored = [sem(f"y_stored{i}") for i in range(3)]
        tu_done, bu_hi_ready, bu_split, g_done, l2_done, m_tanh, m_act, y_ready, ty_done, by_hi_ready, y_split, dn_done, out_copied = (
            sem("tu_done"), sem("bu_hi_ready"), sem("bu_split"), sem("g_done"), sem("l2_done"), sem("m_tanh"), sem("m_act"),
            sem("y_ready"), sem("ty_done"), sem("by_hi_ready"), sem("y_split"), sem("dn_done"), sem("out_copied"))
        og_in = [[sem(f"og_in{i}_{k}") for k in range(2)] for i in range(2)]
        cb_first, cb_sum, cb_T, cb_done = sem("cb_first"), sem("cb_sum"), sem("cb_T"), sem("cb_done")
        a_staged, aw_hi_ready, aw_split = ([sem(f"{n}{i}") for i in range(2)] for n in ("a_staged", "aw_hi_ready", "aw_split"))
        k_done, k_hi_ready, k_split = sem("k_done"), sem("k_hi_ready"), sem("k_split")
        v_done, vt_copied, vt_done, v_hi_ready, v_split = (
            sem("v_done"), sem("vt_copied"), sem("vt_done"), sem("v_hi_ready"), sem("v_split"))
        q_done, q_hi_ready, q_split = sem("q_done"), sem("q_hi_ready"), sem("q_split")
        scores_done, max_ready, exp_done, p_ready = sem("scores_done"), sem("max_ready"), sem("exp_done"), sem("p_ready")
        t_done, pt_hi_ready, pt_split = sem("t_done"), sem("pt_hi_ready"), sem("pt_split")
        c_done, c_hi_ready, c_split = sem("c_done"), sem("c_hi_ready"), sem("c_split")
        dense_done, ax_acc = sem("dense_done"), sem("ax_acc")
        max_part, r_inv, f_scaled = sem("max_part"), sem("r_inv"), sem("f_scaled")
        f_staged = [sem(f"f_staged{i}") for i in range(2)]
        fw_hi_ready, fw_split = sem("fw_hi_ready"), sem("fw_split")
        f_up, f_tanh, f_lin, f_used, f_yready, f_hi_ready, f_split, f_down, fx_acc = (
            sem("f_up"), sem("f_tanh"), sem("f_lin"), sem("f_used"), sem("f_yready"), sem("f_hi_ready"), sem("f_split"),
            sem("f_down"), sem("fx_acc"))
        stored = sem("stored")

        FIRST, FIRST_DMA = 1, 16
        PJ, R0, R1, EB, YD, YO, SM = bank[0:2], bank[2], bank[3], bank[4], bank[5], bank[6], bank[7]
        LGT, UT, LGP = bank[0:2], bank[2:6], bank[6]
        UG, UL, DN, TP = bank[0:3], bank[3:6], bank[6], bank[7]
        CB = bank[4]
        S_, TT_, PP = bank[0:3], bank[3:5], bank[5:8]
        FG, FU, FD = bank[0:2], bank[2:4], bank[4:8]
        S_AT = [(2, 256, 256), (2, 0, 256), (1, 0, 384), (0, 0, 512)]
        PR_AT = [0, 128, 384, 768]

        def tok(b):
            return bass.ds(b * T, T)

        def three(out, hi_w, lo_w, hi_x, lo_x, start, stop):
            nc.tensor.matmul(out, hi_w, hi_x, start=start, stop=False)
            nc.tensor.matmul(out, hi_w, lo_x, start=False, stop=False)
            return nc.tensor.matmul(out, lo_w, hi_x, start=False, stop=stop)

        class Steps:
            def __init__(self, eng, s):
                self.eng, self.s, self.base, self.n = eng, s, 0, 0

            def inc(self, ins):
                ins.then_inc(self.s, 1)
                self.n += 1

            def wait(self):
                self.eng.wait_ge(self.s, self.base + self.n)

        CONV_ORDER = [XC, XC + 1] + list(range(XC))
        Q_BANK, C_BANK, D_BANK = [2, 0, 1, 0], [2, 1, 2, 0], [1, 2, 0, 1]
        T_GROUP = [(0, 512, 0), (1, 512, 512), (0, 256, 1024)]
        PT_AT = [(0, 512), (512, 384), (1024, 256), (896, 128)]

        N_MASKS = 11 + 5 + 4
        DVE_MAMBA = 82
        SETUP_STEPS = 18
        def finish(sp, s, count, per):
            n = 0
            for b in range(BATCH):
                sp.wait_ge(s, count - per * (BATCH - 1 - b))
                sp.dma_start(o_view[:, :, b * T:(b + 1) * T], XT[:, :, b * T:(b + 1) * T]).then_inc(stored, 16)
                n += 16
            sp.wait_ge(stored, n)

        def g_load(eng, two, j):
            n, r = two * 2 + j, two + j // 2
            eng.wait_ge(g_out[j % 2], FIRST_DMA + 16 * r)
            src = fT[bass.ds(n % TILES, 1)].rearrange("o p t -> (o p) t")
            eng.dma_start(g_v[:, j % 2, :], src).then_inc(g_in[j % 2], 16)

        def g_store(eng, two, j):
            n = two * 2 + j
            eng.wait_ge(g_step, G_STEPS * (n + 1))
            dst = g_dram[bass.ds(n, 1)].rearrange("o p t -> (o p) t")
            eng.dma_start(dst, g_v[:, j % 2, :]).then_inc(g_out[j % 2], 16)

        def token_copies(eng, b):
            odd = eng is nc.vector
            if not odd:
                eng.wait_ge(lgt_done, b + 1)
                if b >= 2:
                    eng.wait_ge(lgt_used, b - 1)
                nc.scalar.activation(lgT[:, b % 2, :], LGT[b % 2][0:E, :], ACT.Copy).then_inc(lgt_copied, 1)
            for tb in range(1 if odd else 0, TB, 2):
                a = b * TB + tb
                eng.wait_ge(ut_T, a + 1)
                if b:
                    eng.wait_ge(ut_stored[tb], 16 * b)
                if odd:
                    nc.vector.tensor_copy(ut[:, tb, :], UT[tb][:]).then_inc(ut_copied[1], 1)
                else:
                    nc.scalar.activation(ut[:, tb, :], UT[tb][:], ACT.Copy).then_inc(ut_copied[0], 1)

        G0 = (G_PRE + G_MAMBA * BATCH) // 2

        block = ctx.enter_context(nc.Block())
        @block.sync
        def _(sp):
            for counted in (*g_out,):
                sp.sem_inc(counted, FIRST_DMA)
            sp.dma_start(cols[:], cols_d).then_inc(loaded, 16)
            sp.dma_start(rows[:], rows_d).then_inc(loaded, 16)
            sp.dma_start(condT_s[:], condT).then_inc(loaded, 16)

            def gates(two, count, first):
                g_load(sp, two, 0)
                for j in range(count):
                    if not (first and j == 0):
                        g_store(sp, two - (1 if j == 0 else 0), j - 1 if j else 1)
                    if j + 1 < count:
                        g_load(sp, two, j + 1)

            sp.dma_start(XT[:, :, 0:T], x_view[:, :, 0:T]).then_inc(x_loaded, 16)
            gates(0, G_PRE, True)
            for b in range(1, BATCH):
                sp.dma_start(XT[:, :, b * T:(b + 1) * T], x_view[:, :, b * T:(b + 1) * T]).then_inc(x_loaded, 16)

            def fetch_gate(layer, b, dst, fetched):
                for i in range(2):
                    sp.wait_ge(g_out[i], FIRST_DMA + 16 * (TILES * layer // 2 + 2 * (b + 1)))
                src = g_dram[bass.ds(b * KC + TILES * layer, KC)].rearrange("k p t -> p k t")
                sp.dma_start(dst, src).then_inc(fetched, 16)

            with sp.Fori(0, BATCH) as b:
                sp.wait_ge(z_done, FIRST + PAIRS * b)
                fetch_gate(0, b, um[:], gm_fetched)
                gates(b * (G_MAMBA // 2) + G_PRE // 2, G_MAMBA, False)
            sp.wait_ge(x_added, KC * BATCH)
            sp.wait_ge(masks_ready, N_MASKS + 1)
            for b in range(BATCH):
                fetch_gate(1, b, uf1[:, b], g_fetched[b])
            sp.dma_start(rc[:], rc_d).then_inc(moe_loaded, 16)
            sp.dma_start(gw[:], gw_d).then_inc(moe_loaded, 16)
            for h in range(2):
                sp.dma_start(bias_f[32 * h:32 * h + E, :], bias_d).then_inc(moe_loaded, 16)

            def stage(e):
                for p in range(M_PIECES):
                    if not isinstance(e, int):
                        sp.wait_ge(w_split, M_PIECES * (e - 1) + p + 1)
                    src = moe_d[e] if isinstance(e, int) else moe_d[bass.ds(e, 1)].rearrange("o p w -> (o p) w")
                    o = slice(p * M_PIECE, (p + 1) * M_PIECE)
                    sp.dma_start(m_stage[:, o], src[:, o]).then_inc(m_staged[p], 16)

            for a in range(NT):
                if a == KC:
                    stage(0)
                sp.wait_ge(ut_copied[a % 2], a // 2 + 1)
                sp.dma_start(u_dram[a * P:(a + 1) * P, :], ut[:, a % 4, :]).then_inc(ut_stored[a % 4], 16)
            with sp.Fori(1, E) as e:
                stage(e)
            sp.wait_ge(dn_done, FIRST + NBLK)
            for i in range(3):
                sp.wait_ge(y_stored[i], FIRST_DMA + 16 * (NBLK // 3))
            for b in range(BATCH):
                fetch_gate(2, b, u_g[:, :, b * T:(b + 1) * T], g_fetched[b])

            def att_load(g, lo, hi):
                src = att_d[g] if isinstance(g, int) else att_d[bass.ds(g, 1)].rearrange("o p w -> (o p) w")
                sp.dma_start(aw_in[:, lo:hi], src[:, lo:hi]).then_inc(a_staged[0 if lo == 0 else 1], 16)

            att_load(0, 0, A_D)

            def att_group(g, last):
                if not (isinstance(g, int) and g == 0):
                    sp.wait_ge(dense_done, KC * BATCH * g)
                att_load(g, A_D, ATT_W)
                if not last:
                    sp.wait_ge(q_done, HPG * BATCH * (g + 1))
                    att_load(g + 1, 0, A_D)

            att_group(0, False)
            with sp.Fori(1, GROUPS - 1) as g:
                att_group(g, False)
            att_group(GROUPS - 1, True)
            sp.wait_ge(ax_acc, FIRST + KC * BATCH * GROUPS)
            for b in range(BATCH):
                if b:
                    sp.wait_ge(u_split, BATCH + b)
                fetch_gate(3, b, uf3[:], g_fetched[b])

            def ffn_stage(s, before, par):
                if before is not None:
                    sp.wait_ge(fw_split, FIRST + before)
                src = ffn_d[s] if isinstance(s, int) else ffn_d[bass.ds(s, 1)].rearrange("o p w -> (o p) w")
                sp.dma_start(f_stage[:, par, :], src).then_inc(f_staged[par], 16)

            ffn_stage(0, None, 0)
            with sp.Fori(0, FS // 2) as it:
                ffn_stage(it * 2 + 1, it * 2, 1)
                ffn_stage(it * 2 + 2, it * 2 + 1, 0)
            finish(sp, fx_acc, FIRST + KC * BATCH * FS, KC)

        @block.gpsimd
        def _(pool):
            n = [0]

            def done(ins):
                ins.then_inc(masks_ready, 1)
                n[0] += 1

            def fill(dst, src, op, val, base, pattern, mult):
                pool.wait_ge(masks_ready, n[0])
                done(nc.gpsimd.affine_select(out=dst, in_=src, compare_op=op, fill=val, base=base, pattern=pattern,
                                             channel_multiplier=mult))

            for t_, v_ in ((ident[:], 0.0), (ident_b[:], 0.0), (ones[:], 1.0), (sel_h[:].bitcast(F32), 0.0),
                           (causal_b[:], 0.0), (tri[:], 1.0), (neg4[:], 0.0), (sel_p[:].bitcast(F32), 0.0),
                           (csT[:].bitcast(F32), 0.0), (g_r[:, T - 1:T], 0.0), (eps_c[:], EPS)):
                done(nc.gpsimd.memset(t_, v_))
            fill(ident[:], ident[:], ALU.not_equal, 1.0, 0, [[-1, P]], 1)
            fill(ident_b[:], ident_b[:], ALU.not_equal, 1.0, 0, [[-1, P]], 1)
            fill(causal_b[:], causal_b[:], ALU.is_ge, NEG, 0, [[-1, P]], 1)
            fill(tri[:], tri[:], ALU.is_ge, 0.0, 0, [[1, P]], -1)
            fill(neg4[:], neg4[:], ALU.is_ge, NEG, 0, [[0, TB], [1, P]], -1)
            for h in range(2):
                fill(sel_h[:], sel_h[:], ALU.not_equal, 1.0, -32 * h, [[-1, HEADS_M]], 1)
                fill(sel_p[:], sel_p[:], ALU.not_equal, 1.0, -32 * h, [[-2, PAIRS], [-1, 2], [0, HD]], 1)
            pool.wait_ge(x_added, KC * BATCH)
            done(nc.gpsimd.memset(bias_f[:], 0.0))
            pool.wait_ge(route_vec, IDX_READY)
            for i in range(4):
                pool.wait_ge(ut_stored[i], 16 * (NT // 4))
            for j in range(NBLK):
                if j >= 3:
                    pool.wait_ge(tu_done, j - 2)
                nc.gpsimd.indirect_dma_start(ug[:, j % 3, :], None, u_dram,
                                             bass.IndirectOffsetOnAxis(ap=idx[:, j:j + 1], axis=0)).then_inc(gathered[j % 3], 16)
            pool.wait_ge(dn_done, FIRST + NBLK)
            for i in range(3):
                pool.wait_ge(y_stored[i], FIRST_DMA + 16 * (NBLK // 3))
            for a in range(NT):
                if a >= 2:
                    pool.wait_ge(cb_T, a - 1)
                for k in range(2):
                    nc.gpsimd.indirect_dma_start(
                        og[:, a % 2, k, :], None, y_dram,
                        bass.IndirectOffsetOnAxis(ap=pos_i[:, k, a:a + 1], axis=0)).then_inc(og_in[a % 2][k], 16)

        @block.scalar
        def _(act):
            for counted in (*y_stored,):
                act.sem_inc(counted, FIRST_DMA)
            for counted in (out_copied, exp_done):
                act.sem_inc(counted, FIRST)
            act.dma_start(w_in[:], w_in_d).then_inc(w_loaded, 16)
            act.dma_start(w_out[:], w_out_d).then_inc(w_loaded, 16)
            A = nc.scalar.activation
            act.wait_ge(loaded, 48)
            act.wait_ge(masks_ready, N_MASKS)
            A(dec0[:], cols[:, COLS["w"]:COLS["w"] + 16], ACT.Exp).then_inc(setup_act, 1)
            act.wait_ge(setup_act, 1)
            A(dec0[:], dec0[:], ACT.Exp, scale=-1.0).then_inc(setup_act, 1)
            A(a_neg[:], rows[:, HEADS_M:2 * HEADS_M], ACT.Exp).then_inc(setup_act, 1)
            act.wait_ge(setup_mm, 1)
            A(tf[:], bank[0][:, 0:BATCH], ACT.Tanh, scale=0.5).then_inc(setup_act, 1)

            def gate(two, j):
                s_, n = j % 2, two * 2 + j
                act.wait_ge(g_in[s_], 16 * (two + j // 2 + 1))
                if not (isinstance(n, int) and n < 2):
                    act.wait_ge(g_step, G_STEPS * (n - 1))
                un = u_all[:, bass.ds(n, 1)]
                A(g_ek[:, s_, :], g_v[:, s_, :], ACT.Exp).then_inc(g_exp, 1)
                A(g_eu[:, s_, :], g_v[:, s_, :], ACT.Exp, bias=un).then_inc(g_exp, 1)

            act.wait_ge(setup_step, SETUP_STEPS)
            for j in range(G_PRE):
                gate(0, j)

            def tanh_x(k, b, dst, reused):
                if reused is not None:
                    act.wait_ge(u_ready, FIRST + reused)
                A(dst, XT[:, :, tok(b)], ACT.Tanh, scale=0.5).then_inc(x_tanh, 1)

            act.wait_ge(x_loaded, 16 * BATCH)
            with act.Fori(0, BATCH) as b:
                two = b * (G_MAMBA // 2) + G_PRE // 2
                tanh_x(b, b, txm[:], b)
                act.wait_ge(dt_abs, b + 1)
                A(d_e[:], d_a[:], ACT.Exp, scale=-1.0).then_inc(dt_exp, 1)

                def first_tap(q, ch):
                    act.wait_ge(proj_done, N_CONV * b + q + 1)
                    if q >= 2:
                        act.wait_ge(act_ready, N_CONV * b + q - 1)
                    A(acc[q % 2], PJ[q % 2][:], ACT.Identity, bias=col("conv_b", ch),
                      scale=col("conv_w", 4 * ch + 3)).then_inc(tap0, 1)

                def conv_sig(q):
                    act.wait_ge(conv_tapped, N_CONV * b + q + 1)
                    if q >= 2:
                        act.wait_ge(act_ready, N_CONV * b + q - 1)
                    A(cth[q % 2], acc[q % 2], ACT.Tanh).then_inc(conv_tanh, 1)

                for q, ch in enumerate(CONV_ORDER):
                    first_tap(q, ch)
                    if q == 2:
                        gate(two, 0)
                    if q == 5:
                        gate(two, 1)
                    if q:
                        conv_sig(q - 1)
                    if q == 5:
                        act.wait_ge(cs_neg, b + 1)
                        A(w2e[:], w2[:], ACT.Exp).then_inc(w_exp, 1)
                        A(cdec[:], SM[:, 128:128 + NB], ACT.Exp).then_inc(w_exp, 1)
                        A(csT[0:HEADS_M, :], EB[0:HEADS_M, :], ACT.Copy).then_inc(ct_hi, 1)
                conv_sig(N_CONV - 1)
                for tb in range(TB):
                    act.wait_ge(bc_done, TB * b + tb + 1)
                    A(b_tok[:, tb, :], SM[:, 192:320], ACT.Copy).then_inc(bc_copied, 1)
                    A(cb[:, tb, :], SM[:, 320:448], ACT.Copy).then_inc(bc_copied, 1)
                act.wait_ge(act_ready, N_CONV * (b + 1))

                def square(j):
                    act.wait_ge(y_done, PAIRS * b + j + 1)
                    if j > 1:
                        act.wait_ge(sq_added, (PAIRS - 1) * b + j - 1)
                    A(sq[:] if j else ssum[:], xa[:, j, :], ACT.Square).then_inc(sq_done, 1)

                for j in range(PAIRS):
                    act.wait_ge(r_done, PAIRS * b + j + 1)
                    if j:
                        act.wait_ge(yy_done, PAIRS * b + j)
                        act.wait_ge(y_done, PAIRS * b + j)
                    for hh in range(2):
                        for tb in range(TB):
                            i = tb * HEADS_M + 2 * j + hh
                            A(lm[:, hh, tb * P:(tb + 1) * P], (R0, R1)[hh][:, tb * P:(tb + 1) * P], ACT.Exp,
                              bias=csn[:, i:i + 1]).then_inc(l_done, 1)
                    A(e2[:], EB[:], ACT.Exp).then_inc(l_done, 1)
                    act.wait_ge(z_done, FIRST + PAIRS * b + j + 1)
                    A(tz[:], PJ[j % 2][:], ACT.Tanh, scale=0.5).then_inc(z_tanh, 1)
                    if j % 2 == 0:
                        gate(two, 2 + j // 2)
                    if j:
                        square(j - 1)
                square(PAIRS - 1)
                act.wait_ge(ssq_done, b + 1)
                A(sq[:], EB[:], ACT.Sqrt, scale=1.0 / D_IN, bias=eps_c[:]).then_inc(rms_done, 1)
                gate(two, 6)
                gate(two, 7)

            act.wait_ge(x_added, KC * BATCH)
            for b in range(BATCH):
                tanh_x(BATCH + b, b, tx1[:], BATCH + b)
                if b:
                    token_copies(act, b - 1)
            token_copies(act, BATCH - 1)
            act.wait_ge(route_vec, LG_SUB)
            A(ex[:], lg[:], ACT.Exp).then_inc(lg_exp, 1)

            def up_tanh(j, q):
                act.wait_ge(g_done, j + 1)
                if not (isinstance(j, int) and j == 0):
                    act.wait_ge(y_ready, j)
                A(m_t[:], UG[q][:], ACT.Tanh, scale=0.851).then_inc(m_tanh, 1)

            def u_hi_copy(j):
                act.wait_ge(tu_done, j + 1)
                A(bu_hi[:].rearrange("p k t -> p (k t)"), TP[:], ACT.Copy).then_inc(bu_hi_ready, 1)

            def split_hi(e, slot):
                for p in range(M_PIECES):
                    act.wait_ge(m_staged[p], 16 * (e + 1))
                    o = slice(p * M_PIECE, (p + 1) * M_PIECE)
                    act.wait_ge(masks_ready, N_MASKS)
                    dst = mw[:, slot, 0, o] if isinstance(slot, int) else mw[:, bass.ds(slot, 1), 0, o].rearrange("p o w -> p (o w)")
                    A(dst, m_stage[:, o], ACT.Copy).then_inc(mw_hi_ready, 1)

            def block_act(it, q, last):
                j = it * 3 + q
                two = it + G0
                if not (last and q == 2):
                    f = act.value_load(tab[0:1, 2, j:j + 1] if last else tab[0:1, 2, bass.ds(j, 1)], min_val=0, max_val=1)
                    with act.If(f != 0):
                        e = act.value_load(tab[0:1, 1, j + 1:j + 2] if last else tab[0:1, 1, bass.ds(j + 1, 1)], min_val=1, max_val=E - 1)
                        act.wait_ge(dn_done, FIRST + j)
                        split_hi(e, e % 2)
                if q == 1:
                    g_load(act, two, 1)
                if q == 2 and not last:
                    g_load(act, two + 1, 0)
                if not (last and q == 2):
                    up_tanh(j + 1, (q + 1) % 3)
                act.wait_ge(ty_done, j + 1)
                A(by_hi[:].rearrange("p k t -> p (k t)"), TP[:], ACT.Copy).then_inc(by_hi_ready, 1)
                if not (last and q >= 1):
                    u_hi_copy(j + 2)
                act.wait_ge(dn_done, FIRST + j + 1)
                act.wait_ge(y_stored[q], FIRST_DMA + 16 * it)
                A(m_o[:, q, :], DN[:], ACT.Copy, scale=0.5).then_inc(out_copied, 1)
                if q == 0:
                    g_store(act, two - 1, 1)
                if q == 1:
                    gate(two, 1)
                    g_store(act, two, 0)
                if q == 2 and not last:
                    gate(two + 1, 0)
                act.wait_ge(out_copied, FIRST + j + 1)
                dst = y_dram[j * P:(j + 1) * P, :] if last else y_dram[bass.ds(j * P, P), :]
                act.dma_start(dst, m_o[:, q, :]).then_inc(y_stored[q], 16)

            act.wait_ge(route_vec, IDX_READY)
            act.wait_ge(route_vec, TAB_READY)
            split_hi(0, 0)
            g_load(act, G0, 0)
            gate(G0, 0)
            u_hi_copy(0)
            up_tanh(0, 0)
            u_hi_copy(1)
            with act.Fori(0, NBLK // 3 - 1) as it:
                for q in range(3):
                    block_act(it, q, False)
            for q in range(3):
                block_act(NBLK // 3 - 1, q, True)
            g_store(act, N_GATES * TILES // 2 - 1, 1)
            def gated_input(b):
                k = 2 * BATCH + b
                act.wait_ge(cb_done, TB * (b + 1))
                A(u_in[:, :, tok(b % BATCH)], XT[:, :, tok(b % BATCH)], ACT.Tanh, scale=0.5).then_inc(x_tanh, 1)
                act.wait_ge(u_ready, FIRST + k + 1)
                act.wait_ge(masks_ready, N_MASKS)
                A(u_hi[:, :, tok(b % BATCH)], u_in[:, :, tok(b % BATCH)], ACT.Copy).then_inc(u_hi_ready, 1)

            def att_hi(n, part):
                act.wait_ge(a_staged[part], 16 * n)
                o = slice(0, A_D) if part == 0 else slice(A_D, ATT_W)
                A(aw_hi[:, o], aw_in[:, o], ACT.Copy).then_inc(aw_hi_ready[part], 1)

            gated_input(0)
            att_hi(1, 0)
            with act.Fori(0, GROUPS) as g:
                with act.Fori(0, BATCH) as b:
                    i = g * BATCH + b

                    def q_split_hi(h):
                        act.wait_ge(q_done, HPG * i + h + 1)
                        if h >= 2:
                            act.wait_ge(scores_done, HPG * i + h - 1)
                        A(q_hi[:, h % 2, :], PP[Q_BANK[h]][:], ACT.Copy).then_inc(q_hi_ready, 1)

                    def probs_exp(h):
                        act.wait_ge(max_ready, HPG * i + h + 1)
                        if h >= 2:
                            act.wait_ge(t_done, 3 * (HPG * i + h - 1))
                        for qb in range(TB):
                            bk, c0, _ = S_AT[qb]
                            w = (qb + 1) * P
                            A(probs[:, h % 2, PR_AT[qb]:PR_AT[qb] + w], S_[bk][:, c0:c0 + w], ACT.Exp,
                              bias=nmx[:, h % 2, qb:qb + 1], scale=SCALE,
                              accum_out=rsum[:, h % 2, qb:qb + 1]).then_inc(exp_done, 1)

                    def pt_hi_copy(h):
                        for r, (bk, w, c0) in enumerate(T_GROUP):
                            act.wait_ge(t_done, 3 * (HPG * i + h) + r + 1)
                            if r == 0:
                                act.wait_ge(c_done, FIRST + HPG * i + h)
                            A(pt_hi[:, c0:c0 + w], TT_[bk][:, 0:w], ACT.Copy).then_inc(pt_hi_ready, 1)

                    def ctx_hi(h):
                        act.wait_ge(c_done, FIRST + HPG * i + h + 1)
                        A(cx_hi[:, h, :], PP[C_BANK[h]][:], ACT.Copy).then_inc(c_hi_ready, 1)

                    act.wait_ge(k_done, i + 1)
                    A(k_hi[:], PP[0][:], ACT.Copy).then_inc(k_hi_ready, 1)
                    act.wait_ge(v_done, i + 1)
                    A(vT[:], PP[1][:], ACT.Copy).then_inc(vt_copied, 1)
                    q_split_hi(0)
                    act.wait_ge(vt_done, i + 1)
                    A(v_hi[:], TT_[0][:].rearrange("p (a d) -> p a d", a=TB), ACT.Copy).then_inc(v_hi_ready, 1)
                    q_split_hi(1)
                    with act.If(b == 0):
                        att_hi(g + 1, 1)
                    probs_exp(0)
                    q_split_hi(2)
                    probs_exp(1)
                    pt_hi_copy(0)
                    q_split_hi(3)
                    ctx_hi(0)
                    probs_exp(2)
                    pt_hi_copy(1)
                    ctx_hi(1)
                    probs_exp(3)
                    pt_hi_copy(2)
                    ctx_hi(2)
                    with act.If(i < BATCH - 1):
                        gated_input(b + 1)
                    with act.If(b == BATCH - 1):
                        with act.If(g < GROUPS - 1):
                            att_hi(g + 2, 0)
                    pt_hi_copy(3)
                    ctx_hi(3)
            act.wait_ge(ax_acc, FIRST + KC * BATCH * GROUPS)
            for b in range(BATCH):
                k = 3 * BATCH + b
                tanh_x(k, b, tx3[:], k)
                act.wait_ge(u_ready, FIRST + k + 1)
                A(u_hi[:, :, b * T:(b + 1) * T], uf3[:], ACT.Copy).then_inc(u_hi_ready, 1)

            def ffn_hi(s, par, uses, free):
                act.wait_ge(f_staged[par], 16 * uses)
                if free is not None:
                    act.wait_ge(f_down, FIRST + free)
                A(fw_hi[:, par, :], f_stage[:, par, :], ACT.Copy).then_inc(fw_hi_ready, 1)

            def ffn_y(s, b):
                k = s * BATCH + b
                act.wait_ge(f_split, FIRST + k)
                act.wait_ge(f_up, k + 1)
                if b == 0:
                    act.wait_ge(f_scaled, 2 * (s + 1))
                A(f_t[:], FG[b % 2][:], ACT.Tanh, scale=f_sc[:, 0:1]).then_inc(f_tanh, 1)
                A(f_u[:], FU[b % 2][:], ACT.Copy, scale=f_sc[:, 1:2]).then_inc(f_lin, 1)
                act.wait_ge(f_yready, FIRST + k + 1)
                A(f_hi[:, b % 2, :], f_y[:], ACT.Copy).then_inc(f_hi_ready, 1)

            ffn_hi(0, 0, 1, None)
            ffn_y(0, 0)

            def ffn_act(it, par, last):
                s = it * 2 + par
                for b in range(BATCH):
                    if b < BATCH - 1:
                        ffn_y(s, b + 1)
                    elif not last:
                        ffn_y(s + 1, 0)
                    if b == 1 and not last:
                        ffn_hi(s + 1, 1 - par, it + 1 + par, KC * BATCH * s)

            with act.Fori(0, FS // 2) as it:
                ffn_act(it, 0, False)
                ffn_act(it, 1, False)
            ffn_act(FS // 2, 0, True)

        @block.vector
        def _(dve):
            for counted in (u_ready, fw_split, f_split, pt_split, ax_acc, f_yready, fx_acc):
                dve.sem_inc(counted, FIRST)
            V = nc.vector
            setup = Steps(dve, setup_step)
            dve.wait_ge(loaded, 48)

            def spread(name, i):
                return cols[:, COLS[name] + 4 * i:COLS[name] + 4 * i + 4].unsqueeze(1).to_broadcast([P, BATCH, KC])

            def gate_cols(t_, i):
                return t_[:, TILES * i:TILES * (i + 1)].rearrange("p (b c) -> p b c", b=BATCH)

            for i in range(N_GATES):
                setup.inc(V.tensor_copy(gate_cols(u_all, i), spread("u", i)))
            setup.inc(V.tensor_scalar(gsh[:], cols[:, COLS["gate_s"]:COLS["gate_s"] + FS], 0.5, None, ALU.mult))
            cw = cols[:, COLS["conv_w"]:COLS["conv_w"] + 5 * N_CONV]
            setup.inc(V.tensor_scalar(cw, cw, 0.5, None, ALU.mult))
            setup.wait()
            setup.inc(V.tensor_tensor(ush[:], gsh[:], cols[:, COLS["up_s"]:COLS["up_s"] + FS], ALU.mult))
            dve.wait_ge(setup_act, 4)
            setup.inc(V.tensor_scalar(a_neg[:], a_neg[:], -1.0, None, ALU.mult))
            setup.inc(V.tensor_scalar(fac[:], tf[:], 0.25, 0.75, ALU.mult, ALU.add))
            setup.inc(V.tensor_scalar(osc[:], tf[:], 0.05, 0.45, ALU.mult, ALU.add))
            setup.wait()
            for i in range(N_GATES):
                d0 = dec0[:, 4 * i:4 * i + 4].unsqueeze(1).to_broadcast([P, BATCH, KC])
                setup.inc(V.tensor_tensor(gate_cols(decay, i), d0, fac[:].unsqueeze(2).to_broadcast([P, BATCH, KC]), ALU.mult))
                setup.inc(V.tensor_copy(gate_cols(oscale, i), osc[:].unsqueeze(2).to_broadcast([P, BATCH, KC])))
            setup.wait()
            assert setup.n == SETUP_STEPS
            dve.wait_ge(masks_ready, N_MASKS)

            def gate_part(two, j, part):
                s_, n = j % 2, two * 2 + j
                v, ek, eu = g_v[:, s_, :], g_ek[:, s_, :], g_eu[:, s_, :]
                st = Steps(dve, g_step)
                st.base, st.n = n * G_STEPS, (0, 5, 11)[part]
                d = decay[:, bass.ds(n, 1)].to_broadcast([P, T])
                d1 = decay[:, bass.ds(n, 1)].to_broadcast([P, T - 1])

                def past(dst, src):
                    return V.tensor_tensor_scan(dst, d, src, 0.0, ALU.mult, ALU.add)

                def future(dst, src):
                    return V.tensor_tensor_scan(dst[:, 0:T - 1][:, ::-1], src[:, 1:T][:, ::-1], d1, 0.0, ALU.add, ALU.mult)

                if part == 0:
                    dve.wait_ge(g_exp, (n + 1) * 2)
                    st.inc(V.tensor_scalar(ek, ek, EXP30, None, ALU.min))
                    st.wait()
                    st.inc(V.tensor_tensor(g_e[:], ek, v, ALU.mult))
                    st.wait()
                    st.inc(past(g_f[:], g_e[:]))
                    st.inc(future(g_r, g_e))
                    st.inc(V.scalar_tensor_tensor(v, eu, EXP30, v, ALU.min, ALU.mult))
                elif part == 1:
                    st.wait()
                    st.inc(V.tensor_tensor(g_f[:], g_f[:], g_r[:], ALU.add))
                    st.wait()
                    st.inc(V.tensor_tensor(g_f[:], g_f[:], v, ALU.add))
                    st.inc(past(g_e[:], ek))
                    st.inc(future(g_r, g_ek[:, s_, :]))
                    st.wait()
                    st.inc(V.tensor_tensor(g_e[:], g_e[:], g_r[:], ALU.add))
                    st.wait()
                    st.inc(V.scalar_tensor_tensor(g_e[:], eu, EXP30, g_e[:], ALU.min, ALU.add))
                else:
                    st.wait()
                    st.inc(V.tensor_scalar(g_e[:], g_e[:], 1e-8, None, ALU.max))
                    st.wait()
                    st.inc(V.reciprocal(ek, g_e[:]))
                    st.wait()
                    st.inc(V.scalar_tensor_tensor(v, g_f[:], oscale[:, bass.ds(n, 1)], ek, ALU.mult, ALU.mult))
                assert st.n == (5, 11, G_STEPS)[part]

            def gate(two, j):
                for part in range(3):
                    gate_part(two, j, part)

            for j in range(G_PRE):
                gate(0, j)

            def gated(k, u, tx, fetched, n):
                dve.wait_ge(x_tanh, k + 1)
                dve.wait_ge(fetched, 16 * n)
                V.scalar_tensor_tensor(u, tx, 1.0, u, ALU.add, ALU.mult).then_inc(u_ready, 1)

            step = Steps(dve, dve_step)
            with dve.Fori(0, BATCH) as b:
                two = b * (G_MAMBA // 2) + G_PRE // 2
                step.base = b * DVE_MAMBA
                gated(b, um[:].rearrange("p k t -> p (k t)"), txm[:].rearrange("p k t -> p (k t)"), gm_fetched, b + 1)
                dve.wait_ge(dt_raw, b + 1)
                dtb = rows[:, 0:HEADS_M].unsqueeze(1).to_broadcast([P, TB, HEADS_M])

                def th(t_):
                    return t_[:].rearrange("p (a h) -> p a h", a=TB)

                step.inc(V.tensor_tensor(th(d_x), SM[:, 0:NB].rearrange("p (a h) -> p a h", a=TB), dtb, ALU.add))
                step.wait()
                V.scalar_tensor_tensor(d_a[:], d_x[:], -1.0, d_x[:], ALU.mult, ALU.max).then_inc(dt_abs, 1)
                dve.wait_ge(dt_exp, b + 1)
                step.inc(V.tensor_scalar(d_s[:], d_e[:], 2.0, None, ALU.add))
                step.wait()
                step.inc(V.reciprocal(d_p[:], d_s[:]))
                step.wait()
                step.inc(V.tensor_tensor(d_s[:], d_e[:], d_p[:], ALU.mult))
                step.wait()
                step.inc(V.tensor_tensor(d_q[:], d_s[:], d_s[:], ALU.mult))
                step.wait()
                step.inc(V.tensor_scalar(d_p[:], d_q[:], 1.0 / 17, None, ALU.mult))
                for i in range(7, 0, -1):
                    step.wait()
                    step.inc(V.scalar_tensor_tensor(d_p[:], d_p[:], 1.0 / (2 * i + 1), d_q[:], ALU.add, ALU.mult))
                step.wait()
                step.inc(V.scalar_tensor_tensor(d_p[:], d_p[:], 1.0, d_s[:], ALU.add, ALU.mult))
                step.inc(V.tensor_scalar(d_x[:], d_x[:], 0.0, None, ALU.max))
                step.wait()
                step.inc(V.scalar_tensor_tensor(dt_t[:], d_p[:], 2.0, d_x[:], ALU.mult, ALU.add))
                step.wait()
                V.tensor_tensor(th(d_A), th(dt_t), a_neg[:].unsqueeze(1).to_broadcast([P, TB, HEADS_M]),
                                ALU.mult).then_inc(dA_ready, 1)

                def taps(q, ch):
                    dve.wait_ge(tap0, N_CONV * b + q + 1)
                    for k in range(1, 4):
                        if k > 1:
                            step.wait()
                        ins = V.scalar_tensor_tensor(acc[q % 2][:, k:T], PJ[q % 2][:, 0:T - k], col("conv_w", 4 * ch + 3 - k),
                                                     acc[q % 2][:, k:T], ALU.mult, ALU.add)
                        if k < 3:
                            step.inc(ins)
                        else:
                            ins.then_inc(conv_tapped, 1)

                def conv_out(q, ch):
                    dve.wait_ge(conv_tanh, N_CONV * b + q + 1)
                    dst = xa[:, ch, :] if ch < XC else (bT, cT)[ch - XC][:]
                    V.scalar_tensor_tensor(dst, cth[q % 2], 1.0, acc[q % 2], ALU.add, ALU.mult).then_inc(act_ready, 1)

                for q, ch in enumerate(CONV_ORDER):
                    taps(q, ch)
                    if q:
                        conv_out(q - 1, CONV_ORDER[q - 1])
                    if q == 4:
                        dve.wait_ge(cs_done, b + 1)
                        step.inc(V.tensor_scalar(csn[:], SM[:, 64:64 + NB], -1.0, None, ALU.mult))
                        step.wait()
                        V.tensor_tensor(w2[:], SM[:, 128:128 + NB], csn[:], ALU.add).then_inc(cs_neg, 1)
                    if q == 6:
                        dve.wait_ge(w_exp, 2 * (b + 1))
                        step.inc(V.tensor_tensor(dts[:], w2e[:], dt_t[:], ALU.mult))
                        dve.wait_ge(ct_hi, b + 1)
                        V.tensor_tensor(csT[32:32 + HEADS_M, :], EB[0:HEADS_M, :], csT[0:HEADS_M, :].bitcast(F32),
                                        ALU.subtract).then_inc(ct_ready, 1)
                        gate(two, 0)
                conv_out(N_CONV - 1, CONV_ORDER[-1])
                gate(two, 1)
                step.wait()

                def per_head(t_, tb, half):
                    h0 = tb * HEADS_M + 8 * half
                    return t_[:, h0:h0 + 8].unsqueeze(2).to_broadcast([P, 8, HD])

                for tb in range(TB):
                    dve.wait_ge(x_transposed, TB * b + tb + 1)
                    if tb:
                        dve.wait_ge(s_done, (TB - 1) * b + tb)
                    for half in range(2):
                        xt = (R0, R1)[half][:].rearrange("p (h d) -> p h d", h=8)
                        o = slice(half * 512, half * 512 + 512)
                        step.inc(V.tensor_tensor(xdt[:, tb, o].rearrange("p (h d) -> p h d", h=8), xt,
                                                 per_head(dt_t, tb, half), ALU.mult))
                        ins = V.tensor_tensor(xdt2[:, o].rearrange("p (h d) -> p h d", h=8), xt,
                                              per_head(dts, tb, half), ALU.mult)
                        if half:
                            ins.then_inc(xdt_done, 1)
                        else:
                            step.inc(ins)
                    if tb < TB - 1:
                        dve.wait_ge(s_done, (TB - 1) * b + tb + 1)
                        for half in range(2):
                            o = slice(half * 512, half * 512 + 512)
                            if tb:
                                if half == 0:
                                    dve.wait_ge(state_done, (TB - 1) * b + tb)
                                step.inc(V.tensor_tensor(state[:, tb, o].rearrange("p (h d) -> p h d", h=8),
                                                         state[:, tb - 1, o].rearrange("p (h d) -> p h d", h=8),
                                                         per_head(cdec, tb, half), ALU.mult))
                                step.wait()
                                ins = V.tensor_tensor(state[:, tb, o], state[:, tb, o], PJ[half][:], ALU.add)
                            else:
                                ins = V.tensor_copy(state[:, tb, o], PJ[half][:])
                            if half:
                                ins.then_inc(state_done, 1)
                            else:
                                step.inc(ins)

                def add_square(j):
                    dve.wait_ge(sq_done, PAIRS * b + j + 1)
                    if j > 1:
                        dve.wait_ge(sq_added, (PAIRS - 1) * b + j - 1)
                    V.tensor_tensor(ssum[:], ssum[:], sq[:], ALU.add).then_inc(sq_added, 1)

                for j in range(PAIRS):
                    dve.wait_ge(l_done, 9 * (PAIRS * b + j + 1))
                    for hh in range(2):
                        V.tensor_tensor(lm[:, hh, :], lm[:, hh, :], cb[:].rearrange("p a l -> p (a l)"),
                                        ALU.mult).then_inc(m_ready, 1)
                    dve.wait_ge(z_tanh, PAIRS * b + j + 1)
                    V.scalar_tensor_tensor(tz[:], tz[:], 1.0, PJ[j % 2][:], ALU.add, ALU.mult).then_inc(zs_done, 1)
                    dve.wait_ge(yy_done, PAIRS * b + j + 1)
                    xj = xa[:, j, :]
                    step.inc(V.scalar_tensor_tensor(xj, xj, col("d_skip", j), YD[:], ALU.mult, ALU.add))
                    step.inc(V.tensor_tensor(e2[:, P:T], YO[:, P:T], e2[:, P:T], ALU.mult))
                    step.wait()
                    step.inc(V.tensor_tensor(xj[:, P:T], xj[:, P:T], e2[:, P:T], ALU.add))
                    step.wait()
                    V.scalar_tensor_tensor(xj, xj, 0.5, tz[:], ALU.mult, ALU.mult).then_inc(y_done, 1)
                    if j > 1:
                        add_square(j - 1)
                    if j % 2 == 0:
                        gate(two, 2 + j // 2)
                add_square(PAIRS - 1)
                dve.wait_ge(rms_done, b + 1)
                step.inc(V.reciprocal(ssum[:], sq[:]))
                step.wait()
                for j in range(XC):
                    V.scalar_tensor_tensor(xa[:, j, :], xa[:, j, :], col("norm_w", j), ssum[:], ALU.mult,
                                           ALU.mult).then_inc(yn_ready, 1)
                gate(two, 6)
                for m in range(KC):
                    dve.wait_ge(out_done, KC * b + m + 1)
                    V.tensor_tensor(XT[:, m, tok(b)], XT[:, m, tok(b)], PJ[m % 2][:], ALU.add).then_inc(x_added, 1)
                gate(two, 7)
                assert step.n == DVE_MAMBA, step.n
            def flat(t_):
                return t_.rearrange("p k t -> p (k t)")

            route = Steps(dve, dve_step)
            route.base = DVE_MAMBA * BATCH

            def rconst(name, n, at=0):
                return rc[:, RC[name] + at:RC[name] + at + n]

            def each(ins):
                route.inc(ins)
                route.wait()

            dve.wait_ge(moe_loaded, 64)
            each(V.tensor_scalar(bias_f[:, 2 * I_MOE:], bias_f[:, 2 * I_MOE:], 2.0, None, ALU.mult))
            each(V.tensor_copy(bias_r[:], bias_f[:]))
            route.inc(V.tensor_tensor(bias_r[32:32 + E, :], bias_f[32:32 + E, :], bias_r[32:32 + E, :].bitcast(F32), ALU.subtract))
            for b in range(BATCH):
                gated(BATCH + b, flat(uf1[:, b]), flat(tx1[:]), g_fetched[b], 1)
                if b:
                    token_copies(dve, b - 1)
            token_copies(dve, BATCH - 1)
            wide = [P, NT, E]
            dve.wait_ge(route_mm, LGP_DONE)
            gb = rows[:, 2 * HEADS_M:2 * HEADS_M + E].unsqueeze(1).to_broadcast(wide)
            each(V.tensor_tensor(lg[:], LGP[:, 0:NT * E].rearrange("p (a e) -> p a e", a=NT), gb, ALU.add))
            for a in range(NT):
                route.inc(V.max(mx8[:, a, :], lg[:, a, :]))
            route.wait()
            m2 = mx8[:, :, 1:2].to_broadcast(wide)
            route.inc(V.tensor_tensor(gt[:], lg[:], m2, ALU.is_gt))
            each(V.tensor_tensor(eq[:], lg[:], m2, ALU.is_equal))
            V.tensor_tensor(lg[:], lg[:], mx8[:, :, 0:1].to_broadcast(wide), ALU.subtract).then_inc(route_vec, 1)
            rst = rconst("rst", NT * E)
            route.inc(V.tensor_reduce(r4[:, 0, :], gt[:], AX.X, ALU.add))
            each(V.tensor_tensor_scan(pre[:].rearrange("p a e -> p (a e)"), rst, eq[:].rearrange("p a e -> p (a e)"), 0.0,
                                      ALU.mult, ALU.add))
            each(V.tensor_scalar(r4[:, 0, :], r4[:, 0, :], -1.0, 2.0, ALU.mult, ALU.add))
            each(V.tensor_tensor(pre[:], pre[:], r4[:, 0, :].unsqueeze(2).to_broadcast(wide), ALU.is_le))
            each(V.tensor_tensor(eq[:], eq[:], pre[:], ALU.mult))
            V.tensor_tensor(gt[:], gt[:], eq[:], ALU.add).then_inc(route_vec, 1)
            dve.wait_ge(route_vec, MASK_READY)
            route.inc(V.tensor_tensor_scan(pre[:].rearrange("p a e -> p (a e)"), rst, gt[:].rearrange("p a e -> p (a e)"), 0.0,
                                           ALU.mult, ALU.add))
            dve.wait_ge(lg_exp, 1)
            each(V.tensor_tensor(wx[:], ex[:], gt[:], ALU.mult))
            route.inc(V.scalar_tensor_tensor(sel1[:], pre[:], 1.5, gt[:], ALU.is_lt, ALU.mult))
            each(V.tensor_reduce(r4[:, 0, :], wx[:], AX.X, ALU.add))
            route.inc(V.tensor_tensor(sel2[:], gt[:], sel1[:], ALU.subtract))
            each(V.reciprocal(r4[:, 1, :], r4[:, 0, :]))
            dve.wait_ge(route_mm, PREFIX_DONE)
            each(V.tensor_copy(excl[:].rearrange("p a e -> p (a e)").rearrange("p (e a) -> p e a", e=E),
                               LGP[:, 256:384].rearrange("p (a e) -> p e a", a=NT)))
            each(V.tensor_tensor_scan(incl[:].rearrange("p a e -> p (a e)"), rconst("rst2", NT * E),
                                      excl[:].rearrange("p a e -> p (a e)"), 0.0, ALU.mult, ALU.add))
            by_e = incl[:].rearrange("p a e -> p (a e)").rearrange("p (e a) -> p e a", e=E)
            ex_e = excl[:].rearrange("p a e -> p (a e)").rearrange("p (e a) -> p e a", e=E)
            route.inc(V.tensor_tensor(excl[:], incl[:], excl[:], ALU.subtract))
            cmp_ = rtmp[:].rearrange("p a e -> p (a e)").rearrange("p (e a) -> p e a", e=E)
            each(V.tensor_tensor(cmp_, by_e[:, :, NT - 1:NT].to_broadcast([P, E, NT]),
                                 rconst("full", NT).unsqueeze(1).to_broadcast([P, E, NT]), ALU.is_gt))
            each(V.tensor_reduce(nb[:, 0, :], cmp_, AX.X, ALU.add))
            each(V.tensor_tensor_scan(nb[:, 1, :], ones[:, 0:E], nb[:, 0, :], 0.0, ALU.mult, ALU.add))
            each(V.tensor_tensor(nb[:, 2, :], nb[:, 1, :], nb[:, 0, :], ALU.subtract))
            route.inc(V.tensor_tensor(posm[:], LGP[:, 128:256].rearrange("p (a e) -> p a e", a=NT),
                                      ex_e.rearrange("p e a -> p a e"), ALU.add))
            each(V.tensor_scalar(nb[:, 2, :], nb[:, 2, :], float(P), None, ALU.mult))
            each(V.tensor_tensor(posm[:], posm[:], nb[:, 2, :].unsqueeze(1).to_broadcast(wide), ALU.add))
            for k, sel in enumerate((sel1, sel2)):
                each(V.tensor_tensor(rtmp[:], sel[:], posm[:], ALU.mult))
                each(V.tensor_reduce(posf[:, 0, k, :], rtmp[:], AX.X, ALU.add))
            each(V.tensor_scalar(posf[:, 1], posf[:, 0], 63.5, 1.0 / P, ALU.subtract, ALU.mult))
            each(V.tensor_scalar(posf[:, 1], posf[:, 1], ROUND, ROUND, ALU.add, ALU.subtract))
            each(V.scalar_tensor_tensor(posf[:, 2], posf[:, 1], -float(P), posf[:, 0], ALU.mult, ALU.add))

            def choices(i, n):
                return posf[:, i].rearrange("p k a -> p (k a)").unsqueeze(2).to_broadcast([P, 2 * NT, n])

            dve.wait_ge(route_mm, U_DONE)
            for i in range(4):
                dve.wait_ge(ut_stored[i], 16 * (NT // 4))
            route.inc(V.tensor_tensor(oh_r[:], choices(2, P), rconst("iota", P).unsqueeze(1).to_broadcast([P, 2 * NT, P]),
                                      ALU.is_equal))
            each(V.tensor_tensor(oh_j[:], choices(1, NBLK), rconst("iota", NBLK).unsqueeze(1).to_broadcast([P, 2 * NT, NBLK]),
                                 ALU.is_equal))
            route.inc(V.tensor_tensor(oh_v[:, :, 0, :], oh_j[:], rconst("blk", 2 * NT).unsqueeze(2).to_broadcast([P, 2 * NT, NBLK]),
                                      ALU.mult))
            V.tensor_scalar(oh_v[:, :, 1, :], oh_j[:], rconst("place", 1), None, ALU.mult).then_inc(route_vec, 1)
            each(V.tensor_tensor(ecmp[:], nb[:, 1, :].unsqueeze(1).to_broadcast([P, NBLK + 1, E]),
                                 rconst("iota", NBLK + 1).unsqueeze(2).to_broadcast([P, NBLK + 1, E]), ALU.is_le))
            each(V.tensor_reduce(etab[:, 0, :], ecmp[:], AX.X, ALU.add))
            route.inc(V.memset(etab[:, 1, 0:1], 0.0))
            route.inc(V.memset(etab[:, 2, NBLK:NBLK + 1], 0.0))
            each(V.tensor_scalar(etab[:, 0, :], etab[:, 0, :], E - 1.0, None, ALU.min))
            each(V.tensor_scalar(etab[:, 1, 1:NBLK + 1], etab[:, 0, 0:NBLK], 1.0, E - 1.0, ALU.add, ALU.min))
            each(V.tensor_tensor(etab[:, 2, 0:NBLK], etab[:, 1, 1:NBLK + 1], etab[:, 1, 0:NBLK], ALU.subtract))
            V.tensor_copy(tab[:], etab[:]).then_inc(route_vec, 1)
            route.inc(V.tensor_copy(pos_i[:], posf[:, 0]))
            each(V.tensor_tensor(wx[:], wx[:], r4[:, 1, :].unsqueeze(2).to_broadcast(wide), ALU.mult))
            for k, sel in enumerate((sel1, sel2)):
                each(V.tensor_tensor(rtmp[:], sel[:], wx[:], ALU.mult))
                each(V.tensor_reduce(we[:, k, :], rtmp[:], AX.X, ALU.add))
            dve.wait_ge(route_mm, IDX_DONE)
            each(V.tensor_copy(idx_f[:], LGP[:, NBLK:2 * NBLK]))
            each(V.scalar_tensor_tensor(idx_f[:], LGP[:, 0:NBLK], float(P), idx_f[:], ALU.mult, ALU.add))
            V.tensor_copy(idx[:], idx_f[:]).then_inc(route_vec, 1)
            dve.wait_ge(route_vec, IDX_READY)
            dve.wait_ge(route_vec, TAB_READY)

            def split_lo(e, slot):
                for p in range(M_PIECES):
                    dve.wait_ge(mw_hi_ready, M_PIECES * e + p + 1)
                    o = slice(p * M_PIECE, (p + 1) * M_PIECE)
                    hi, lo = ((mw[:, slot, i, o] if isinstance(slot, int) else mw[:, bass.ds(slot, 1), i, o].rearrange("p o w -> p (o w)"))
                              for i in range(2))
                    V.tensor_tensor(lo, m_stage[:, o], hi.bitcast(F32), ALU.subtract).then_inc(w_split, 1)

            def select(j, q, e):
                if not (isinstance(j, int) and j < 3):
                    dve.wait_ge(dn_done, FIRST + j - 2)
                V.tensor_scalar(sel_e[:, q, :], sel_h[:, bass.ds(e, 1)].bitcast(F32).to_broadcast([64, P]), 1.0, None,
                                ALU.mult).then_inc(sel_ready, 1)

            def glu(j, q):
                dve.wait_ge(m_tanh, j + 1)
                V.scalar_tensor_tensor(m_t[:], m_t[:], 1.0, UG[q][:], ALU.add, ALU.mult).then_inc(m_act, 1)

            def inner(j, q):
                dve.wait_ge(l2_done, j + 1)
                dve.wait_ge(m_act, j + 1)
                V.scalar_tensor_tensor(m_y[:], UL[q][:], 1.0, m_t[:], ALU.add, ALU.mult).then_inc(y_ready, 1)

            def u_lo_split(j):
                dve.wait_ge(bu_hi_ready, j + 1)
                V.tensor_tensor(flat(bu_lo[:]), TP[:], flat(bu_hi[:]).bitcast(F32), ALU.subtract).then_inc(bu_split, 1)

            def block_dve(it, q, last):
                j = it * 3 + q
                if not (last and q == 2):
                    f = dve.value_load(tab[0:1, 2, j:j + 1] if last else tab[0:1, 2, bass.ds(j, 1)], min_val=0, max_val=1)
                    with dve.If(f != 0):
                        e = dve.value_load(tab[0:1, 1, j + 1:j + 2] if last else tab[0:1, 1, bass.ds(j + 1, 1)], min_val=1, max_val=E - 1)
                        split_lo(e, e % 2)
                    glu(j + 1, (q + 1) % 3)
                dve.wait_ge(by_hi_ready, j + 1)
                V.tensor_tensor(flat(by_lo[:]), TP[:], flat(by_hi[:]).bitcast(F32), ALU.subtract).then_inc(y_split, 1)
                if not (last and q == 2):
                    inner(j + 1, (q + 1) % 3)
                if not (last and q >= 1):
                    e2 = dve.value_load(tab[0:1, 0, j + 2:j + 3] if last else tab[0:1, 0, bass.ds(j + 2, 1)], min_val=0, max_val=E - 1)
                    select(j + 2, (q + 2) % 3, e2)
                    u_lo_split(j + 2)
                for i in (2 * q, 2 * q + 1):
                    gate_part(it + G0, i // 3, i % 3)

            split_lo(0, 0)
            select(0, 0, 0)
            e_1 = dve.value_load(tab[0:1, 0, 1:2], min_val=0, max_val=E - 1)
            select(1, 1, e_1)
            u_lo_split(0)
            glu(0, 0)
            inner(0, 0)
            u_lo_split(1)
            with dve.Fori(0, NBLK // 3 - 1) as it:
                for q in range(3):
                    block_dve(it, q, False)
            for q in range(3):
                block_dve(NBLK // 3 - 1, q, True)

            def weighted(b, tb):
                a, s_ = b * TB + tb, tb % 2
                for k in range(2):
                    dve.wait_ge(og_in[s_][k], 16 * (b * 2 + tb // 2 + 1))
                V.tensor_scalar(og[:, s_, 0, :], og[:, s_, 0, :], we[:, 0, bass.ds(a % NT, 1)], None, ALU.mult).then_inc(cb_first, 1)
                dve.wait_ge(cb_first, a + 1)
                V.scalar_tensor_tensor(og[:, s_, 0, :], og[:, s_, 1, :], we[:, 1, bass.ds(a % NT, 1)], og[:, s_, 0, :], ALU.mult,
                                       ALU.add).then_inc(cb_sum, 1)

            def combine(b, tb):
                a = b * TB + tb
                dve.wait_ge(cb_T, a + 1)
                xa_ = XT[:, :, bass.ds(a % NT * P, P)]
                V.tensor_tensor(xa_, xa_, CB[:].rearrange("p (k t) -> p k t", k=KC), ALU.add).then_inc(cb_done, 1)

            def gated_input(b):
                k = 2 * BATCH + b
                u = u_in[:, :, tok(b % BATCH)]
                dve.wait_ge(x_tanh, k + 1)
                for i in range(BATCH):
                    dve.wait_ge(g_fetched[i], 32)
                V.scalar_tensor_tensor(u, u, 1.0, u_g[:, :, tok(b % BATCH)], ALU.add, ALU.mult).then_inc(u_ready, 1)
                dve.wait_ge(u_hi_ready, b + 1)
                V.tensor_tensor(u_lo[:, :, tok(b % BATCH)], u, u_hi[:, :, tok(b % BATCH)].bitcast(F32), ALU.subtract).then_inc(u_split, 1)

            def att_lo(n, part):
                dve.wait_ge(aw_hi_ready[part], n)
                o = slice(0, A_D) if part == 0 else slice(A_D, ATT_W)
                V.tensor_tensor(aw_lo[:, o], aw_in[:, o], aw_hi[:, o].bitcast(F32), ALU.subtract).then_inc(aw_split[part], 1)

            weighted(0, 0)
            for tb in range(TB):
                if tb < TB - 1:
                    weighted(0, tb + 1)
                combine(0, tb)
            gated_input(0)
            att_lo(1, 0)
            with dve.Fori(0, GROUPS) as g:
                with dve.Fori(0, BATCH) as b:
                    i = g * BATCH + b

                    def q_lo_split(h):
                        dve.wait_ge(q_hi_ready, HPG * i + h + 1)
                        V.tensor_tensor(q_lo[:, h % 2, :], PP[Q_BANK[h]][:], q_hi[:, h % 2, :].bitcast(F32),
                                        ALU.subtract).then_inc(q_split, 1)

                    def row_max(h):
                        dve.wait_ge(scores_done, HPG * i + h + 1)
                        for qb in range(TB):
                            bk, c0, _ = S_AT[qb]
                            V.tensor_reduce(rinv[:, h % 2, qb:qb + 1], S_[bk][:, c0:c0 + (qb + 1) * P], AX.X,
                                            ALU.max).then_inc(max_part, 1)
                        dve.wait_ge(max_part, TB * (HPG * i + h + 1))
                        V.tensor_scalar(nmx[:, h % 2, :], rinv[:, h % 2, :], -SCALE, None, ALU.mult).then_inc(max_ready, 1)

                    def normalise(h):
                        dve.wait_ge(exp_done, FIRST + TB * (HPG * i + h + 1))
                        dve.wait_ge(max_ready, HPG * i + h + 1)
                        V.reciprocal(rinv[:, h % 2, :], rsum[:, h % 2, :]).then_inc(r_inv, 1)
                        dve.wait_ge(r_inv, HPG * i + h + 1)
                        for qb in range(TB):
                            pr = probs[:, h % 2, PR_AT[qb]:PR_AT[qb] + (qb + 1) * P]
                            V.tensor_scalar(pr, pr, rinv[:, h % 2, qb:qb + 1], None, ALU.mult).then_inc(p_ready, 1)

                    def pt_lo_split(h):
                        for r, (bk, w, c0) in enumerate(T_GROUP):
                            dve.wait_ge(pt_hi_ready, 3 * (HPG * i + h) + r + 1)
                            V.tensor_tensor(pt_lo[:, c0:c0 + w], TT_[bk][:, 0:w], pt_hi[:, c0:c0 + w].bitcast(F32),
                                            ALU.subtract).then_inc(pt_split, 1)

                    def ctx_lo(h):
                        dve.wait_ge(c_hi_ready, HPG * i + h + 1)
                        V.tensor_tensor(cx_lo[:, h, :], PP[C_BANK[h]][:], cx_hi[:, h, :].bitcast(F32),
                                        ALU.subtract).then_inc(c_split, 1)

                    dve.wait_ge(k_hi_ready, i + 1)
                    V.tensor_tensor(k_lo[:], PP[0][:], k_hi[:].bitcast(F32), ALU.subtract).then_inc(k_split, 1)
                    q_lo_split(0)
                    dve.wait_ge(v_hi_ready, i + 1)
                    V.tensor_tensor(v_lo[:], TT_[0][:].rearrange("p (a d) -> p a d", a=TB), v_hi[:].bitcast(F32),
                                    ALU.subtract).then_inc(v_split, 1)
                    q_lo_split(1)
                    with dve.If(b == 0):
                        att_lo(g + 1, 1)
                    with dve.If(i < BATCH - 1):
                        weighted(b + 1, 0)
                        for tb in range(TB):
                            if tb < TB - 1:
                                weighted(b + 1, tb + 1)
                            combine(b + 1, tb)
                    row_max(0)
                    q_lo_split(2)
                    normalise(0)
                    row_max(1)
                    pt_lo_split(0)
                    normalise(1)
                    q_lo_split(3)
                    ctx_lo(0)
                    row_max(2)
                    pt_lo_split(1)
                    normalise(2)
                    ctx_lo(1)
                    row_max(3)
                    pt_lo_split(2)
                    normalise(3)
                    ctx_lo(2)
                    with dve.If(i < BATCH - 1):
                        gated_input(b + 1)
                    with dve.If(b == BATCH - 1):
                        with dve.If(g < GROUPS - 1):
                            att_lo(g + 2, 0)
                    pt_lo_split(3)
                    ctx_lo(3)
                    for m in range(KC):
                        dve.wait_ge(dense_done, KC * i + m + 1)
                        xm = XT[:, m, tok(b)]
                        V.tensor_tensor(xm, xm, PP[D_BANK[m]][:], ALU.add).then_inc(ax_acc, 1)
            for b in range(BATCH):
                k = 3 * BATCH + b
                gated(k, flat(uf3[:]), flat(tx3[:]), g_fetched[b], 3)
                dve.wait_ge(u_hi_ready, k - 2 * BATCH + 1)
                V.tensor_tensor(u_lo[:, :, b * T:(b + 1) * T], uf3[:], u_hi[:, :, b * T:(b + 1) * T].bitcast(F32),
                                ALU.subtract).then_inc(u_split, 1)

            def ffn_lo(s, par):
                dve.wait_ge(fw_hi_ready, s + 1)
                V.tensor_tensor(fw_lo[:, par, :], f_stage[:, par, :], fw_hi[:, par, :].bitcast(F32),
                                ALU.subtract).then_inc(fw_split, 1)

            def ffn_y(s, b):
                k = s * BATCH + b
                dve.wait_ge(f_tanh, k + 1)
                V.scalar_tensor_tensor(f_t[:], f_t[:], 1.0, FG[b % 2][:], ALU.add, ALU.mult).then_inc(f_used, 1)
                dve.wait_ge(f_lin, k + 1)
                dve.wait_ge(f_used, k + 1)
                V.tensor_tensor(f_y[:], f_t[:], f_u[:], ALU.mult).then_inc(f_yready, 1)
                dve.wait_ge(f_hi_ready, k + 1)
                V.tensor_tensor(f_lo[:, b % 2, :], f_y[:], f_hi[:, b % 2, :].bitcast(F32), ALU.subtract).then_inc(f_split, 1)

            def ffn_add(s, b):
                for m in range(KC):
                    dve.wait_ge(f_down, FIRST + KC * (s * BATCH + b) + m + 1)
                    xm = XT[:, m, b * T:(b + 1) * T]
                    V.scalar_tensor_tensor(xm, FD[m][:], col("down_s", m), xm, ALU.mult, ALU.add).then_inc(fx_acc, 1)

            def scales(s):
                V.tensor_scalar(f_sc[:, 0:1], gsh[:, bass.ds(s, 1)], 1.0, None, ALU.mult).then_inc(f_scaled, 1)
                V.tensor_scalar(f_sc[:, 1:2], ush[:, bass.ds(s, 1)], 1.0, None, ALU.mult).then_inc(f_scaled, 1)

            scales(0)
            ffn_lo(0, 0)
            ffn_y(0, 0)

            def ffn_dve(s, par, last):
                for b in range(BATCH):
                    if b < BATCH - 1:
                        ffn_y(s, b + 1)
                        if b == BATCH - 2 and not last:
                            scales(s + 1)
                    elif not last:
                        ffn_y(s + 1, 0)
                    ffn_add(s, b)
                    if b == 1 and not last:
                        ffn_lo(s + 1, 1 - par)

            with dve.Fori(0, FS // 2) as it:
                ffn_dve(it * 2, 0, False)
                ffn_dve(it * 2 + 1, 1, False)
            ffn_dve(FS - 1, 0, True)

        @block.tensor
        def _(pe):
            for counted in (z_done, dn_done, c_done, f_down):
                pe.sem_inc(counted, FIRST)
            M = nc.tensor.matmul
            pe.wait_ge(masks_ready, N_MASKS)
            pe.wait_ge(loaded, 48)
            M(bank[0][:, 0:BATCH], ones[:], condT_s[:], start=True, stop=True).then_inc(setup_mm, 1)
            pe.wait_ge(w_loaded, 32)
            with pe.Fori(0, BATCH) as b:
                pe.wait_ge(u_ready, FIRST + b + 1)
                for tb in range(TB):
                    for k in range(KC):
                        mm = M(SM[:, tb * HEADS_M:(tb + 1) * HEADS_M], um[:, k, tb * P:(tb + 1) * P], w_in[:, k, DT_COL:IN_COLS],
                               start=(k == 0), stop=(k == KC - 1))
                mm.then_inc(dt_raw, 1)

                def project(dst, c0):
                    for k in range(KC):
                        mm = M(dst[:], w_in[:, k, c0:c0 + P], um[:, k, :], start=(k == 0), stop=(k == KC - 1))
                    return mm

                for q, ch in enumerate(CONV_ORDER):
                    if q >= 2:
                        pe.wait_ge(conv_tapped, N_CONV * b + q - 1)
                    project(PJ[q % 2], D_IN + ch * P).then_inc(proj_done, 1)
                    if q == 3:
                        pe.wait_ge(dA_ready, b + 1)
                        M(SM[:, 64:64 + NB], tri[:], d_A[:], start=True, stop=True)
                        M(SM[:, 128:128 + NB], ones[:], d_A[:], start=True, stop=True)
                        for tb in range(TB):
                            mm = M(EB[0:HEADS_M, tb * P:(tb + 1) * P], d_A[:, tb * HEADS_M:(tb + 1) * HEADS_M], tri[:],
                                   start=True, stop=True)
                        mm.then_inc(cs_done, 1)
                pe.wait_ge(act_ready, N_CONV * (b + 1))
                for tb in range(TB):
                    o = slice(tb * P, (tb + 1) * P)
                    if tb:
                        pe.wait_ge(xdt_done, TB * b + tb)
                    for ch in range(XC):
                        mm = nc.tensor.transpose((R0, R1)[ch // 4][:, (ch % 4) * P:(ch % 4 + 1) * P], xa[:, ch, o], ident[:])
                    mm.then_inc(x_transposed, 1)
                    if tb:
                        pe.wait_ge(bc_copied, 2 * (TB * b + tb))
                    nc.tensor.transpose(SM[:, 192:320], bT[:, o], ident[:])
                    M(SM[:, 320:448], bT[:, o], cT[:, o], start=True, stop=True).then_inc(bc_done, 1)
                    if tb < TB - 1:
                        pe.wait_ge(xdt_done, TB * b + tb + 1)
                        pe.wait_ge(bc_copied, 2 * (TB * b + tb + 1))
                        if tb:
                            pe.wait_ge(state_done, (TB - 1) * b + tb)
                        for half in range(2):
                            mm = M(PJ[half][:], b_tok[:, tb, :], xdt2[:, half * 512:(half + 1) * 512], start=True, stop=True)
                        mm.then_inc(s_done, 1)

                def z_chunk(j):
                    if j >= 2:
                        pe.wait_ge(zs_done, PAIRS * b + j - 1)
                    else:
                        pe.wait_ge(state_done, (TB - 1) * (b + 1))
                    project(PJ[j % 2], j * P).then_inc(z_done, 1)

                def sums(j):
                    if j:
                        pe.wait_ge(l_done, 9 * (PAIRS * b + j))
                    for hh in range(2):
                        M((R0, R1)[hh][:], ident_b[:], neg4[:].rearrange("p a l -> p (a l)"), start=True, stop=False)
                        M((R0, R1)[hh][:], sel_h[:, 2 * j + hh:2 * j + hh + 1].to_broadcast([64, P]), csT[:], start=False, stop=True)
                    M(EB[:], sel_p[:, j, :], csT[:], start=True, stop=True).then_inc(r_done, 1)

                z_chunk(0)
                pe.wait_ge(ct_ready, b + 1)
                pe.wait_ge(xdt_done, TB * (b + 1))
                sums(0)
                pe.wait_ge(bc_copied, 2 * TB * (b + 1))
                for j in range(PAIRS):
                    if j < PAIRS - 1:
                        z_chunk(j + 1)
                        sums(j + 1)
                    pe.wait_ge(m_ready, 2 * (PAIRS * b + j + 1))
                    if j:
                        pe.wait_ge(y_done, PAIRS * b + j)
                    for hh in range(2):
                        for tb in range(TB):
                            M(YD[hh * HD:(hh + 1) * HD, tb * P:(tb + 1) * P], xdt[:, tb, (2 * j + hh) * HD:(2 * j + hh + 1) * HD],
                              lm[:, hh, tb * P:(tb + 1) * P], start=True, stop=True)
                    for tb in range(1, TB):
                        mm = M(YO[:, tb * P:(tb + 1) * P], state[:, tb - 1, j * P:(j + 1) * P], cT[:, tb * P:(tb + 1) * P],
                               start=True, stop=True)
                    mm.then_inc(yy_done, 1)
                pe.wait_ge(sq_added, (PAIRS - 1) * (b + 1))
                M(EB[:], ones[:], ssum[:], start=True, stop=True).then_inc(ssq_done, 1)
                for m in range(KC):
                    if m >= 2:
                        pe.wait_ge(x_added, KC * b + m - 1)
                    for j in range(XC):
                        if m == 0:
                            pe.wait_ge(yn_ready, XC * b + j + 1)
                        mm = M(PJ[m % 2][:], w_out[:, j, m * P:(m + 1) * P], xa[:, j, :], start=(j == 0), stop=(j == XC - 1))
                    mm.then_inc(out_done, 1)
            def transposed(out, src, dim=P):
                return nc.tensor.transpose(out, src, ident[0:dim, 0:dim])

            pe.wait_ge(x_added, KC * BATCH)
            pe.wait_ge(moe_loaded, 64)
            for b in range(BATCH):
                pe.wait_ge(u_ready, FIRST + BATCH + b + 1)
                for kc in range(KC):
                    mm = M(LGT[b % 2][0:E, :], gw[:, kc, :], uf1[:, b, kc, :], start=(kc == 0), stop=(kc == KC - 1))
                mm.then_inc(lgt_done, 1)
                for tb in range(TB):
                    a = b * TB + tb
                    if a >= 4:
                        pe.wait_ge(ut_copied[a % 2], (a - 4) // 2 + 1)
                    for kc in range(KC):
                        mm = transposed(UT[tb][:, kc * P:(kc + 1) * P], uf1[:, b, kc, tb * P:(tb + 1) * P])
                    mm.then_inc(ut_T, 1)
                pe.wait_ge(lgt_copied, b + 1)
                for tb in range(TB):
                    a = b * TB + tb
                    mm = transposed(LGP[:, a * E:(a + 1) * E], lgT[:, b % 2, tb * P:(tb + 1) * P], E)
                if b == BATCH - 1:
                    mm.then_inc(route_mm, 1)
                else:
                    mm.then_inc(lgt_used, 1)
            pe.wait_ge(route_vec, MASK_READY)
            gt2 = gt[:].rearrange("p a e -> p (a e)")
            M(LGP[:, 128:256], rc[:, RC["before"]:RC["before"] + P], gt2, start=True, stop=True).then_inc(route_mm, 1)
            M(LGP[:, 256:384], ones[:], gt2, start=True, stop=True).then_inc(route_mm, 1)
            pe.wait_ge(route_vec, ONEHOT_READY)
            for c in range(2 * NT):
                mm = M(LGP[:, 0:2 * NBLK], oh_r[:, c, :], oh_v[:, c].rearrange("p v j -> p (v j)"), start=(c == 0), stop=(c == 2 * NT - 1))
            mm.then_inc(route_mm, 1)

            def product(out, x_hi, x_lo, slot, c0, q, bias):
                M(out, sel_e[:, q, :], bias_r[:, bias:bias + C], start=True, stop=False)
                for kc in range(KC):
                    o = slice(c0 + kc * C, c0 + (kc + 1) * C)
                    hi, lo = ((mw[:, slot, i, o] if isinstance(slot, int) else mw[:, bass.ds(slot, 1), i, o].rearrange("p o w -> p (o w)"))
                              for i in range(2))
                    M(out, x_hi[:, kc, :], hi, start=False, stop=False)
                    M(out, x_hi[:, kc, :], lo, start=False, stop=False)
                    mm = M(out, x_lo[:, kc, :], hi, start=False, stop=(kc == KC - 1))
                return mm

            def up_glu(j, q, e, slot):
                pe.wait_ge(bu_split, j + 1)
                pe.wait_ge(sel_ready, j + 1)
                pe.wait_ge(w_split, M_PIECES * e + 1)
                product(UG[q][:], bu_hi, bu_lo, slot, 0, q, 0).then_inc(g_done, 1)

            def up_lin(j, q, e, slot):
                pe.wait_ge(w_split, M_PIECES * e + 2)
                product(UL[q][:], bu_hi, bu_lo, slot, M_PIECE, q, I_MOE).then_inc(l2_done, 1)

            def inputs_T(j, q, it):
                pe.wait_ge(gathered[q], 16 * (it + 1))
                for kc in range(KC):
                    mm = transposed(TP[:, kc * P:(kc + 1) * P], ug[:, q, kc * P:(kc + 1) * P])
                mm.then_inc(tu_done, 1)

            def block_pe(it, q, last):
                j = it * 3 + q
                e0 = pe.value_load(tab[0:1, 0, j:j + 1] if last else tab[0:1, 0, bass.ds(j, 1)], min_val=0, max_val=E - 1)
                if not (last and q == 2):
                    e1 = pe.value_load(tab[0:1, 0, j + 1:j + 2] if last else tab[0:1, 0, bass.ds(j + 1, 1)], min_val=0, max_val=E - 1)
                    up_glu(j + 1, (q + 1) % 3, e1, e1 % 2)
                pe.wait_ge(y_ready, j + 1)
                for kc in range(KC):
                    mm = transposed(TP[:, kc * P:(kc + 1) * P], m_y[:, kc * P:(kc + 1) * P])
                mm.then_inc(ty_done, 1)
                if not (last and q == 2):
                    up_lin(j + 1, (q + 1) % 3, e1, e1 % 2)
                pe.wait_ge(y_split, j + 1)
                if not (last and q >= 1):
                    inputs_T(j + 2, (q + 2) % 3, it + (q + 2) // 3)
                pe.wait_ge(w_split, M_PIECES * (e0 + 1))
                pe.wait_ge(out_copied, FIRST + j)
                product(DN[:], by_hi, by_lo, e0 % 2, 2 * M_PIECE, q, 2 * I_MOE).then_inc(dn_done, 1)

            pe.wait_ge(route_vec, TAB_READY)
            inputs_T(0, 0, 0)
            up_glu(0, 0, 0, 0)
            up_lin(0, 0, 0, 0)
            pe.wait_ge(bu_split, 1)
            inputs_T(1, 1, 0)
            with pe.Fori(0, NBLK // 3 - 1) as it:
                for q in range(3):
                    block_pe(it, q, False)
            for q in range(3):
                block_pe(NBLK // 3 - 1, q, True)

            def combine_T(b, tb):
                a, s_ = b * TB + tb, tb % 2
                pe.wait_ge(cb_sum, a + 1)
                if not (isinstance(a, int) and a == 0):
                    pe.wait_ge(cb_done, a)
                for kc in range(KC):
                    mm = transposed(CB[:, kc * P:(kc + 1) * P], og[:, s_, 0, kc * P:(kc + 1) * P])
                mm.then_inc(cb_T, 1)

            for tb in range(TB):
                combine_T(0, tb)
            with pe.Fori(0, GROUPS) as g:
                with pe.Fori(0, BATCH) as b:
                    i = g * BATCH + b

                    def project(dst, at, width, c0):
                        for kc in range(KC):
                            o = slice(at + kc * width + c0, at + kc * width + c0 + P)
                            mm = three(dst[:], aw_hi[:, o], aw_lo[:, o], u_hi[:, kc, tok(b)], u_lo[:, kc, tok(b)],
                                       kc == 0, kc == KC - 1)
                        return mm

                    def query(h):
                        project(PP[Q_BANK[h]], A_Q, C, h * DH).then_inc(q_done, 1)

                    def scores(h):
                        pe.wait_ge(q_split, HPG * i + h + 1)
                        pe.wait_ge(exp_done, FIRST + TB * (HPG * i + h))
                        for qb in range(TB - 1, -1, -1):
                            bk, c0, w = S_AT[qb]
                            qs = slice(qb * P, (qb + 1) * P)
                            d = S_[bk][:, c0:c0 + w]
                            three(d, q_hi[:, h % 2, qs], q_lo[:, h % 2, qs], k_hi[:, 0:w], k_lo[:, 0:w], True, False)
                            mm = M(S_[bk][:, c0 + qb * P:c0 + (qb + 1) * P], ident_b[:], causal_b[:], start=False, stop=True)
                        mm.then_inc(scores_done, 1)

                    def transposes(h):
                        pe.wait_ge(p_ready, TB * (HPG * i + h + 1))
                        n = 3 * (HPG * i + h)
                        for r, blocks in enumerate((((0, 0),), ((1, 0), (3, 384)), ((2, 0),))):
                            bk = T_GROUP[r][0]
                            pe.wait_ge(pt_split, FIRST + n + (1 if r == 2 else 0))
                            for kb, c0 in blocks:
                                for qb in range(kb, TB):
                                    o = PR_AT[qb] + kb * P
                                    mm = nc.tensor.transpose(TT_[bk][:, c0 + (qb - kb) * P:c0 + (qb - kb + 1) * P],
                                                             probs[:, h % 2, o:o + P], ident[:])
                            mm.then_inc(t_done, 1)

                    def context(h):
                        pe.wait_ge(pt_split, FIRST + 3 * (HPG * i + h + 1))
                        for kb in range(TB):
                            o, w = PT_AT[kb]
                            mm = three(PP[C_BANK[h]][:, kb * P:T], v_hi[:, kb, :], v_lo[:, kb, :], pt_hi[:, o:o + w], pt_lo[:, o:o + w],
                                       kb == 0, kb == TB - 1)
                        mm.then_inc(c_done, 1)

                    pe.wait_ge(aw_split[0], g + 1)
                    with pe.If(g == 0):
                        pe.wait_ge(u_split, b + 1)
                    pe.wait_ge(ax_acc, FIRST + KC * i)
                    project(PP[0], A_K, P, 0).then_inc(k_done, 1)
                    project(PP[1], A_V, P, 0).then_inc(v_done, 1)
                    query(0)
                    pe.wait_ge(vt_copied, i + 1)
                    pe.wait_ge(pt_split, FIRST + 3 * HPG * i)
                    for tb in range(TB):
                        mm = nc.tensor.transpose(TT_[0][:, tb * P:(tb + 1) * P], vT[:, tb * P:(tb + 1) * P], ident[:])
                    mm.then_inc(vt_done, 1)
                    pe.wait_ge(k_split, i + 1)
                    query(1)
                    with pe.If(i < BATCH - 1):
                        for tb in range(TB):
                            combine_T(b + 1, tb)
                        pe.wait_ge(cb_done, TB * (b + 2))
                    scores(0)
                    query(2)
                    scores(1)
                    pe.wait_ge(v_split, i + 1)
                    transposes(0)
                    query(3)
                    context(0)
                    scores(2)
                    transposes(1)
                    context(1)
                    scores(3)
                    transposes(2)
                    pe.wait_ge(c_split, HPG * i + 1)
                    context(2)
                    transposes(3)
                    context(3)
                    pe.wait_ge(c_split, HPG * (i + 1))
                    pe.wait_ge(aw_split[1], g + 1)
                    for m in range(KC):
                        if m == 3:
                            pe.wait_ge(ax_acc, FIRST + KC * i + 1)
                        for h in range(HPG):
                            o = slice(A_D + h * C + m * P, A_D + h * C + (m + 1) * P)
                            mm = three(PP[D_BANK[m]][:], aw_hi[:, o], aw_lo[:, o], cx_hi[:, h, :], cx_lo[:, h, :], h == 0, h == HPG - 1)
                        mm.then_inc(dense_done, 1)
            pe.wait_ge(ax_acc, FIRST + KC * BATCH * GROUPS)
            pe.wait_ge(u_split, 2 * BATCH)

            def ffn_up(s, par, b):
                k = s * BATCH + b
                if b == 0:
                    pe.wait_ge(fw_split, FIRST + s + 1)
                if not (isinstance(s, int) and s == 0 and b < 2):
                    pe.wait_ge(f_yready, FIRST + k - 1)
                x = slice(b * T, (b + 1) * T)
                for dst, gu in ((FG[b % 2], 0), (FU[b % 2], 1)):
                    for kc in range(KC):
                        o = slice(kc * 256 + gu * P, kc * 256 + (gu + 1) * P)
                        mm = three(dst[:], fw_hi[:, par, o], fw_lo[:, par, o], u_hi[:, kc, x], u_lo[:, kc, x], kc == 0, kc == KC - 1)
                mm.then_inc(f_up, 1)

            def ffn_down(s, par, b):
                k = s * BATCH + b
                pe.wait_ge(f_split, FIRST + k + 1)
                pe.wait_ge(fx_acc, FIRST + KC * k)
                for m in range(KC):
                    o = slice(FFN_UP + m * P, FFN_UP + (m + 1) * P)
                    three(FD[m][:], fw_hi[:, par, o], fw_lo[:, par, o], f_hi[:, b % 2, :], f_lo[:, b % 2, :], True, True).then_inc(f_down, 1)

            ffn_up(0, 0, 0)

            def ffn_pe(s, par, last):
                for b in range(BATCH):
                    if b < BATCH - 1:
                        ffn_up(s, par, b + 1)
                    elif not last:
                        ffn_up(s + 1, 1 - par, 0)
                    ffn_down(s, par, b)

            with pe.Fori(0, FS // 2) as it:
                ffn_pe(it * 2, 0, False)
                ffn_pe(it * 2 + 1, 1, False)
            ffn_pe(FS - 1, 0, True)


_SHAPES = dict(xT=(C, BATCH * T), fT=(TILES, P, T), condT=(P, BATCH), cols=(P, N_COLS), rows=(P, N_ROWS),
               w_in=(P, KC, IN_COLS), w_out=(P, XC, C), moe=(E, P, MOE_W), gw=(P, KC, E), bias=(E, 2 * I_MOE + C), rc=(P, N_RC),
               att=(GROUPS, P, ATT_W), ffn=(FS, P, FFN_W))


def routing_constants():
    one = np.ones((P, 1), np.float32)
    n = np.arange(P)
    parts = dict(iota=one * n, before=n[:, None] < n[None, :], rst=one * (np.arange(NT * E) % E > 0),
                 rst2=one * (np.arange(NT * E) % NT > 0), full=one * np.where(np.arange(NT) == 0, -1, P * np.arange(NT)),
                 blk=one * (np.arange(2 * NT) % NT), place=n[:, None])
    return np.concatenate([parts[k] for k in RC], axis=1).astype(np.float32)


def lay_out(i):
    i = {k: np.asarray(v) for k, v in i.items()}
    chunks = lambda v: v.reshape(-1, P).T
    b1 = i["L0_ffn_b1"].reshape(E, I_MOE, 2)
    gates = ("L0_cond", "L0_cond2", "L1_cond", "L1_cond2")
    conv = i["L0_attn_conv_w"].reshape(N_CONV, P, 4).transpose(1, 0, 2).reshape(P, -1)
    d_skip = np.repeat(i["L0_attn_D_skip"], HD)
    cols = np.concatenate(
        [chunks(i[g + "_u"]) for g in gates] + [chunks(i[g + "_w"]) for g in gates]
        + [conv, chunks(i["L0_attn_conv_b"]), chunks(i["L0_attn_norm_w"]), chunks(d_skip),
           chunks(i["L1_ffn_gate_s"]), chunks(i["L1_ffn_up_s"]), chunks(i["L1_ffn_down_s"])], axis=1)
    row = np.concatenate([i["L0_attn_dt_bias"], i["L0_attn_A_log"], i["L0_ffn_gate_b"]])
    w1 = i["L0_ffn_w1"].reshape(E, I_MOE, 2, KC, P).transpose(0, 4, 2, 3, 1).reshape(E, P, 2 * M_PIECE)
    w2 = i["L0_ffn_w2"].reshape(E, C, I_MOE // P, P).transpose(0, 3, 2, 1).reshape(E, P, M_PIECE)
    wq = i["L1_attn_w_q"].reshape(KC, P, GROUPS, HPG * DH).transpose(2, 1, 0, 3).reshape(GROUPS, P, -1)
    wkv = i["L1_attn_w_kv"].reshape(KC, P, 2, GROUPS, DH).transpose(2, 3, 1, 0, 4).reshape(2, GROUPS, P, -1)
    wd = i["L1_attn_w_dense"].reshape(GROUPS, HPG, DH, C).transpose(0, 2, 1, 3).reshape(GROUPS, P, -1)
    up = np.stack([i["L1_ffn_gate_w"], i["L1_ffn_up_w"]]).reshape(2, FS, P, KC, P).transpose(1, 4, 3, 0, 2).reshape(FS, P, -1)
    down = i["L1_ffn_down_w"].reshape(C, FS, P).transpose(1, 2, 0)
    out = dict(
        xT=i["x"].transpose(2, 0, 1).reshape(C, -1),
        fT=i["fside_BxSxS_0"].transpose(0, 2, 1).reshape(TILES, P, T),
        condT=i["cond_512"].T, cols=cols, rows=np.broadcast_to(row, (P, N_ROWS)),
        w_in=i["L0_attn_in_proj_w"].T.reshape(KC, P, IN_COLS).transpose(1, 0, 2),
        w_out=i["L0_attn_out_proj_w"].T.reshape(XC, P, C).transpose(1, 0, 2),
        moe=np.concatenate([w1, w2], axis=2), gw=i["L0_ffn_gate_w"].T.reshape(KC, P, E).transpose(1, 0, 2),
        bias=np.concatenate([b1[..., 0], b1[..., 1], i["L0_ffn_b2"]], axis=1), rc=routing_constants(), att=np.concatenate([wq, wkv[0], wkv[1], wd], axis=2), ffn=np.concatenate([up, down], axis=2))
    return {k: np.ascontiguousarray(v) for k, v in out.items()}


def build(nc):
    aps = [nc.dram_tensor(f"in_{n}", s, F32, kind="ExternalInput").ap() for n, s in _SHAPES.items()]
    out = nc.dram_tensor("outT", (C, BATCH * T), F32, kind="ExternalOutput").ap()
    network(nc, *aps, out)


def kernel(**inputs):
    import concourse.bacc as bacc
    from concourse.bass_utils import run_bass_kernel_spmd

    nc = bacc.Bacc("TRN2", target_bir_lowering=False, num_devices=1)
    build(nc)
    arrays = {f"in_{k}": v for k, v in lay_out(inputs).items()}
    r = run_bass_kernel_spmd(nc, [arrays], core_ids=[0])
    return np.ascontiguousarray(r.results[0]["outT"].reshape(C, BATCH, T).transpose(1, 2, 0))
```

```python
from contextlib import ExitStack

import numpy as np
import concourse.bass as bass
from concourse import mybir

F32, F32R, BF16, I32 = mybir.dt.float32, mybir.dt.float32r, mybir.dt.bfloat16, mybir.dt.int32
ALU, ACT, AX = mybir.AluOpType, mybir.ActivationFunctionType, mybir.AxisListType

P = 128
BATCH, T, C = 4, 512, 512
KC = C // P
TB = T // P
N_GATES = 4
TILES = BATCH * KC
EXP30 = float(np.exp(np.float32(30.0)))
HEADS_M, HD, D_IN = 16, 64, 1024
XC = D_IN // P
N_CONV = XC + 2
IN_COLS = 2 * D_IN + 2 * P + HEADS_M
DT_COL = 2 * D_IN + 2 * P
PAIRS = HEADS_M // 2
EPS = 1e-5
E, I_MOE = 8, 512
M_PIECES, M_PIECE = 3, KC * I_MOE
MOE_W = M_PIECES * M_PIECE
TOKENS = BATCH * T
NT = TOKENS // P
NBLK = (2 * TOKENS + E * (P - 1)) // P
ROUND = 1.5 * 2 ** 23
RC = {}
_at = 0
for _name, _n in (("iota", P), ("before", P), ("rst", NT * E), ("rst2", NT * E), ("full", NT), ("blk", 2 * NT), ("place", 1), ("row", 1)):
    RC[_name] = _at
    _at += _n
N_RC = _at
GROUPS, HPG, DH = 4, 4, 128
SCALE = DH ** -0.5
NI = GROUPS * BATCH
A_K, A_V, A_Q = 0, C, 2 * C
A_D = A_Q + HPG * C
ATT_W = A_D + HPG * C
PART = [(0, A_D - C), (A_D, ATT_W), (A_D - C, A_D)]
FS = 11
FFN_UP, FFN_W = KC * 256, KC * 256 + C
NEG = -1e30

COLS = {}
_at = 0
for _name, _n in (("u", 16), ("w", 16), ("conv_w", 4 * N_CONV), ("conv_b", N_CONV), ("norm_w", XC), ("d_skip", XC),
                  ("gate_s", FS), ("up_s", FS), ("down_s", KC)):
    COLS[_name] = _at
    _at += _n
N_COLS = _at
N_ROWS = 2 * HEADS_M + E
G_VEC, G_PRE, G_MAMBA = KC, 2, 8
G_MOE = G_VEC + G_PRE + G_MAMBA * BATCH
G_ATT = G_MOE + NBLK // 3
A_GATE = 2
V_CLAMPED, V_FUTURE, V_SUMS, V_INVERSE = 2, 4, 6, 8
P_PRODUCTS, P_DEN, P_DONE = 1, 2, 3


def network(nc, xT, fT, condT, cols_d, rows_d, w_in_d, w_out_d, moe_d, gw_d, bias_d, rc_d, att_d, ffn_d, outT):
    g_dram = nc.dram_tensor("gates", (N_GATES * TILES, P, T), F32, kind="Internal").ap()
    u_dram = nc.dram_tensor("u_tok", (TOKENS, C), F32, kind="Internal").ap()
    y_dram = nc.dram_tensor("y_slot", (NBLK * P, C), F32, kind="Internal").ap()
    x_view = xT.rearrange("(k p) n -> p k n", p=P)
    o_view = outT.rearrange("(k p) n -> p k n", p=P)
    ctx = ExitStack()
    with ctx:
        def sem(name):
            return ctx.enter_context(nc.semaphore(name))

        def sb(name, shape, dt=F32, stack=ctx):
            return stack.enter_context(nc.sbuf_tensor(name, shape, dt))

        XT = sb("XT", [P, KC, BATCH * T])
        cols = sb("cols", [P, N_COLS])
        rows = sb("rows", [P, N_ROWS])
        u_all = sb("u_all", [P, N_GATES * TILES])
        decay = sb("decay", [P, N_GATES * TILES])
        oscale = sb("oscale", [P, N_GATES * TILES])
        gw = sb("gw", [P, KC, E])
        ident = sb("ident", [P, P])
        ident_b = sb("ident_b", [P, P], BF16)
        ones = sb("ones", [P, P])
        sel_h = sb("sel_h", [64, HEADS_M], F32R)
        causal_b = sb("causal_b", [P, P], BF16)
        gsh = sb("gsh", [P, FS])
        ush = sb("ush", [P, FS])
        pos_i = sb("pos_i", [P, 2, NT], I32)
        we = sb("we", [P, 2, NT])
        f_sc = sb("f_sc", [P, 2])
        nmx = sb("nmx", [P, 2, TB])
        rsum = sb("rsum", [P, 2, TB])
        rinv = sb("rinv", [P, 2, TB])
        g_v = sb("g_v", [P, 2, T])
        bank = [ctx.enter_context(nc.psum_tensor(f"bank{i}", [P, 512], F32)) for i in range(8)]

        def col(name, i):
            return cols[:, COLS[name] + i:COLS[name] + i + 1]

        with ExitStack() as s:
            condT_s = sb("condT_s", [P, BATCH], F32, s)
            tf = sb("tf", [P, BATCH], F32, s)
            fac = sb("fac", [P, BATCH], F32, s)
            osc = sb("osc", [P, BATCH], F32, s)
            dec0 = sb("dec0", [P, 16], F32, s)
        gs_ = ctx.enter_context(ExitStack())
        g_ek = sb("g_ek", [P, 2, T], F32, gs_)
        g_eu = sb("g_eu", [P, 2, T], F32, gs_)
        g_e, g_r1, g_r2 = (sb(f"g_{n}", [P, T], F32, gs_) for n in ("e", "r1", "r2"))
        with ExitStack() as s:
            w_out = sb("w_out", [P, XC, C], F32, s)
            um = sb("um", [P, KC, T], F32, s)
            txm = sb("txm", [P, KC, T], F32, s)
            xa = sb("xa", [P, XC, T], F32, s)
            xdt = sb("xdt", [P, TB, D_IN], F32, s)
            state = sb("state", [P, TB - 1, D_IN], F32, s)
            w_in = sb("w_in", [P, KC, IN_COLS], F32, s)
            tri = sb("tri", [P, P], F32, s)
            neg4 = sb("neg4", [P, TB, P], BF16, s)
            sel_p = sb("sel_p", [64, PAIRS, P], F32R, s)
            bT = sb("bT", [P, T], F32, s)
            cT = sb("cT", [P, T], F32, s)
            b_tok = sb("b_tok", [P, TB, P], F32, s)
            cb = sb("cb", [P, TB, P], F32, s)
            xdt2 = sb("xdt2", [P, D_IN], F32, s)
            csT = sb("csT", [64, T], F32R, s)
            lm = sb("lm", [P, 2, 2, T], F32, s)
            e2 = sb("e2", [P, T], F32, s)
            tz = sb("tz", [P, 2, T], F32, s)
            sq = sb("sq", [P, 2, T], F32, s)
            NB = TB * HEADS_M
            d_x, d_a, d_e, d_s, d_p, d_q, dt_t, d_A, csn, w2, w2e, dts, cdec = (
                sb(f"dt{i}", [P, NB], F32, s) for i in range(13))
            a_neg = sb("a_neg", [P, HEADS_M], F32, s)
            eps_c = sb("eps_c", [P, 1], F32, s)
        acc = [lm[:, 0, 0, :], lm[:, 0, 1, :]]
        cth = [e2[:, :], tz[:, 0, :]]
        rms_inv = lm[:, 0, 0, :]
        with ExitStack() as s:
            m_stage = sb("m_stage", [P, MOE_W], F32, s)
            mw = sb("mw", [P, 2, 2, MOE_W], F32R, s)
            ug = sb("ug", [P, 3, C], F32, s)
            bu_hi = sb("bu_hi", [P, KC, P], F32R, s)
            bu_lo = sb("bu_lo", [P, KC, P], F32R, s)
            m_t = sb("m_t", [P, I_MOE], F32, s)
            m_y = sb("m_y", [P, I_MOE], F32, s)
            by_hi = sb("by_hi", [P, KC, P], F32R, s)
            by_lo = sb("by_lo", [P, KC, P], F32R, s)
            m_o = sb("m_o", [P, 3, C], F32, s)
            bias_r = sb("bias_r", [64, 2 * I_MOE + C], F32R, s)
            sel_e = sb("sel_e", [64, 3, P], F32R, s)
            row_e = sb("row_e", [64, 1], F32, s)
            exp_of = sb("exp_of", [64, NBLK + 1], F32, s)
            idx = sb("idx", [P, NBLK], I32, s)
            idx_now = sb("idx_now", [P, 3], I32, s)
            tab = sb("tab", [P, 3, NBLK + 1], I32, s)
        with ExitStack() as s:
            sb("pad_m", [P, 3, MOE_W], F32, s)
            lgT = sb("lgT", [E, 2, T], F32, s)
            uf1 = sb("uf1", [P, BATCH, KC, T], F32, s)
            rc = sb("rc", [P, N_RC], F32, s)
            bias_f = sb("bias_f", [64, 2 * I_MOE + C], F32, s)
            lg, ex, gt, eq, pre, wx, sel1, sel2, posm, incl, excl, rtmp = (sb(f"rt{i}", [P, NT, E], F32, s) for i in range(12))
            mx8 = sb("mx8", [P, NT, 8], F32, s)
            r4 = sb("r4", [P, 2, NT], F32, s)
            nb = sb("nb", [P, 3, E], F32, s)
            posf = sb("posf", [P, 3, 2, NT], F32, s)
            etab = sb("etab", [P, 3, NBLK + 1], F32, s)
            ecmp = sb("ecmp", [P, NBLK + 1, E], F32, s)
            idx_f = sb("idx_f", [P, NBLK], F32, s)
            with ExitStack() as s2:
                ut = sb("ut", [P, 4, C], F32, s2)
            with ExitStack() as s2:
                oh_r = sb("oh_r", [P, 2 * NT, P], BF16, s2)
                oh_j = sb("oh_j", [P, 2 * NT, NBLK], F32, s2)
                oh_v = sb("oh_v", [P, 2 * NT, 2, NBLK], BF16, s2)
        gs_.close()
        with ExitStack() as s:
            probs = sb("probs", [P, 2, 1280], F32, s)
            vT = sb("vT", [P, T], F32, s)
            k_hi = sb("k_hi", [P, T], F32R, s)
            with ExitStack() as s2:
                u_g = sb("u_g", [P, KC, BATCH * T], F32, s2)
                u_in = sb("u_in", [P, KC, BATCH * T], F32, s2)
                sb("pad_a", [P, ATT_W], F32, s2)
                aw_in = sb("aw_in", [P, ATT_W], F32, s2)
            u_hi = sb("u_hi", [P, KC, BATCH * T], F32R, s)
            u_lo = sb("u_lo", [P, KC, BATCH * T], F32R, s)
            with ExitStack() as s2:
                aw_hi = sb("aw_hi", [P, ATT_W], F32R, s2)
                aw_lo = sb("aw_lo", [P, ATT_W], F32R, s2)
                with ExitStack() as s3:
                    og = sb("og", [P, 2, 2, C], F32, s3)
                a_ek, a_eu, a_e, a_r1, a_r2 = (sb(f"a_{n}", [P, T], F32, s2) for n in ("ek", "eu", "e", "r1", "r2"))
                k_lo = sb("k_lo", [P, T], F32R, s2)
                v_hi = sb("v_hi", [P, TB, P], F32R, s2)
                v_lo = sb("v_lo", [P, TB, P], F32R, s2)
                q_hi = sb("q_hi", [P, 2, T], F32R, s2)
                q_lo = sb("q_lo", [P, 2, T], F32R, s2)
                pt_hi = sb("pt_hi", [P, 1280], F32R, s2)
                pt_lo = sb("pt_lo", [P, 1280], F32R, s2)
                with ExitStack() as s3:
                    og2 = sb("og2", [P, 2, 2, C], F32, s3)
                cx_hi = sb("cx_hi", [P, HPG, T], F32R, s2)
                cx_lo = sb("cx_lo", [P, HPG, T], F32R, s2)
            with ExitStack() as s2:
                fw_hi = sb("fw_hi", [P, 2, FFN_W], F32R, s2)
                f_hi = sb("f_hi", [P, 2, T], F32R, s2)
                f_lo = sb("f_lo", [P, 2, T], F32R, s2)
                fw_lo = sb("fw_lo", [P, 2, FFN_W], F32R, s2)
                f_t = sb("f_t", [P, T], F32, s2)
                f_u = sb("f_u", [P, T], F32, s2)
                f_y = sb("f_y", [P, T], F32, s2)
                sb("pad_f", [P, 2 * ATT_W - 2 * 2 * FFN_W - 7 * T], F32, s2)
                f_stage = sb("f_stage", [P, 2, FFN_W], F32, s2)

        loaded, x_loaded, w_loaded, wo_loaded, wo_scaled = sem("loaded"), sem("x_loaded"), sem("w_loaded"), sem("wo_loaded"), sem("wo_scaled")
        masks_ready, setup_step, setup_mm, setup_act = sem("masks_ready"), sem("setup_step"), sem("setup_mm"), sem("setup_act")
        g_in = [sem(f"g_in{i}") for i in range(2)]
        g_out = [sem(f"g_out{i}") for i in range(2)]
        g_exp, g_vec, g_pool, pre_in = sem("g_exp"), sem("g_vec"), sem("g_pool"), sem("pre_in")
        gm_fetched, x_tanh, u_ready = sem("gm_fetched"), sem("x_tanh"), sem("u_ready")
        g_fetched = [sem(f"g_fetched{b}") for b in range(BATCH)]
        u_hi_ready, u_split = sem("u_hi_ready"), sem("u_split")
        dve_step = sem("dve_step")
        dt_raw, dt_abs, dt_exp, dA_ready = sem("dt_raw"), sem("dt_abs"), sem("dt_exp"), sem("dA_ready")
        proj_done, tap0, conv_tapped, conv_tanh, act_ready = (
            sem("proj_done"), sem("tap0"), sem("conv_tapped"), sem("conv_tanh"), sem("act_ready"))
        cs_done, cs_neg, w_exp, ct_hi, ct_ready = sem("cs_done"), sem("cs_neg"), sem("w_exp"), sem("ct_hi"), sem("ct_ready")
        x_transposed, xdt_done, bc_done, bc_copied = sem("x_transposed"), sem("xdt_done"), sem("bc_done"), sem("bc_copied")
        s_done, state_done = sem("s_done"), sem("state_done")
        z_done, z_tanh, zs_done = sem("z_done"), sem("z_tanh"), sem("zs_done")
        r_done, l_done, m_ready, yy_done, y_done = sem("r_done"), sem("l_done"), sem("m_ready"), sem("yy_done"), sem("y_done")
        sq_added = sem("sq_added")
        sq_done, ssq_done, rms_done = (
            sem("sq_done"), sem("ssq_done"), sem("rms_done"))
        out_done, x_added = sem("out_done"), sem("x_added")
        moe_loaded = sem("moe_loaded")
        lgt_done, lgt_copied, lgt_used, ut_T = sem("lgt_done"), sem("lgt_copied"), sem("lgt_used"), sem("ut_T")
        ut_copied = [sem(f"ut_copied{i}") for i in range(2)]
        ut_stored = [sem(f"ut_stored{i}") for i in range(4)]
        route_mm, route_vec, lg_exp = sem("route_mm"), sem("route_vec"), sem("lg_exp")
        LGP_DONE, U_DONE, PREFIX_DONE, IDX_DONE = 1, 2, 3, 4
        LG_SUB, MASK_READY, ONEHOT_READY, TAB_READY, IDX_READY = 1, 2, 3, 4, 5
        m_staged = [sem(f"m_staged{i}") for i in range(M_PIECES)]
        mw_hi_ready, w_split, sel_ready = sem("mw_hi_ready"), sem("w_split"), sem("sel_ready")
        gathered = [sem(f"gathered{i}") for i in range(3)]
        y_stored = [sem(f"y_stored{i}") for i in range(3)]
        tu_done, bu_hi_ready, bu_split, g_done, l2_done, m_tanh, m_act, y_ready, ty_done, by_hi_ready, y_split, dn_done, out_copied = (
            sem("tu_done"), sem("bu_hi_ready"), sem("bu_split"), sem("g_done"), sem("l2_done"), sem("m_tanh"), sem("m_act"),
            sem("y_ready"), sem("ty_done"), sem("by_hi_ready"), sem("y_split"), sem("dn_done"), sem("out_copied"))
        og_in = [sem(f"og_in{i}") for i in range(2)]
        cb_first, cb_sum, cb_T, cb_done = sem("cb_first"), sem("cb_sum"), sem("cb_T"), sem("cb_done")
        a_staged, aw_hi_ready, aw_split = ([sem(f"{n}{i}") for i in range(3)] for n in ("a_staged", "aw_hi_ready", "aw_split"))
        k_done, k_hi_ready, k_split = sem("k_done"), sem("k_hi_ready"), sem("k_split")
        v_done, vt_copied, vt_done, v_hi_ready, v_split = (
            sem("v_done"), sem("vt_copied"), sem("vt_done"), sem("v_hi_ready"), sem("v_split"))
        q_done, q_hi_ready, q_split = sem("q_done"), sem("q_hi_ready"), sem("q_split")
        scores_done, max_ready, exp_done, p_ready = sem("scores_done"), sem("max_ready"), sem("exp_done"), sem("p_ready")
        t_done, pt_hi_ready, pt_split = sem("t_done"), sem("pt_hi_ready"), sem("pt_split")
        c_done, c_hi_ready, c_split = sem("c_done"), sem("c_hi_ready"), sem("c_split")
        dense_done, ax_acc = sem("dense_done"), sem("ax_acc")
        max_part, r_inv, f_scaled = sem("max_part"), sem("r_inv"), sem("f_scaled")
        f_staged = [sem(f"f_staged{i}") for i in range(2)]
        fw_hi_ready, fw_split = sem("fw_hi_ready"), sem("fw_split")
        f_up, f_tanh, f_lin, f_used, f_yready, f_hi_ready, f_split, f_down, fx_acc = (
            sem("f_up"), sem("f_tanh"), sem("f_lin"), sem("f_used"), sem("f_yready"), sem("f_hi_ready"), sem("f_split"),
            sem("f_down"), sem("fx_acc"))
        stored = sem("stored")

        FIRST, FIRST_DMA = 1, 16
        PJ, R0, R1, EB, YD, YO, SM = bank[0:2], bank[2], bank[3], bank[4], bank[5], bank[6], bank[7]
        OB = (*PJ, R0, R1)
        XB = (R0, R1), (YD, YO)
        LGT, UT, LGP = bank[0:2], bank[2:6], bank[6]
        UG, UL, DN, TP = bank[0:3], bank[3:6], bank[6], bank[7]
        CB = bank[4]
        S_, TT_, PP = bank[0:3], bank[3:5], bank[5:8]
        FG, FU, FD = bank[0:2], bank[2:4], bank[4:8]
        S_AT = [(2, 256, 256), (2, 0, 256), (1, 0, 384), (0, 0, 512)]
        PR_AT = [0, 128, 384, 768]

        def tok(b):
            return bass.ds(b * T, T)

        def three(out, hi_w, lo_w, hi_x, lo_x, start, stop):
            nc.tensor.matmul(out, hi_w, hi_x, start=start, stop=False)
            nc.tensor.matmul(out, hi_w, lo_x, start=False, stop=False)
            return nc.tensor.matmul(out, lo_w, hi_x, start=False, stop=stop)

        class Steps:
            def __init__(self, eng, s):
                self.eng, self.s, self.base, self.n = eng, s, 0, 0

            def inc(self, ins):
                ins.then_inc(self.s, 1)
                self.n += 1

            def wait(self):
                self.eng.wait_ge(self.s, self.base + self.n)

        CONV_ORDER = [XC, XC + 1] + list(range(XC))
        Q_BANK, C_BANK, D_BANK, KV_BANK = [1, 0, 1, 1], [0, 2, 2, 2], [2, 0, 1, 2], 0
        T_GROUP = [(0, 512, 0), (1, 512, 512), (0, 256, 1024)]
        PT_AT = [(0, 512), (512, 384), (1024, 256), (896, 128)]

        N_MASKS = 10 + 5 + 4
        DVE_MAMBA = 84
        SETUP_STEPS = 19
        GATE_CONV = [1, 3, 5, 6, 8]
        def finish(sp, s, count, per):
            n = 0
            for b in range(BATCH):
                sp.wait_ge(s, count - per * (BATCH - 1 - b))
                sp.dma_start(o_view[:, :, b * T:(b + 1) * T], XT[:, :, b * T:(b + 1) * T]).then_inc(stored, 16)
                n += 16
            sp.wait_ge(stored, n)

        A_SLOT = G_ATT % 2
        SLOT_USES = [(G_ATT - G_VEC + 1 - i) // 2 for i in range(2)]

        def g_load(eng, n, slot, use):
            eng.wait_ge(g_out[slot], FIRST_DMA + 16 * use)
            src = fT[bass.ds(n % TILES, 1)].rearrange("o p t -> (o p) t")
            eng.dma_start(g_v[:, slot, :], src).then_inc(g_in[slot], 16)

        def g_store(eng, n, slot):
            eng.wait_ge(g_pool, P_DONE * (n - G_VEC + 1))
            dst = g_dram[bass.ds(n, 1)].rearrange("o p t -> (o p) t")
            eng.dma_start(dst, g_v[:, slot, :]).then_inc(g_out[slot], 16)

        def gate_sums(eng, st, d, o, v, ek, eu, e, f):
            d_t = d.to_broadcast([P, T])
            combined, scan = eng.scalar_tensor_tensor, eng.tensor_tensor_scan
            st.inc(combined(ek, ek, EXP30, ek, ALU.min, ALU.min))
            st.wait()
            st.inc(combined(e, ek, 1.0, v, ALU.mult, ALU.mult))
            st.inc(scan(f, d_t, ek, 0.0, ALU.mult, ALU.add))
            st.wait()
            st.inc(combined(v, eu, EXP30, v, ALU.min, ALU.mult))
            st.inc(scan(ek[:, ::-1], d_t, ek[:, ::-1], 0.0, ALU.mult, ALU.add))
            st.wait()
            st.inc(combined(ek[:, 1:T], f[:, 0:T - 1], d, ek[:, 1:T], ALU.mult, ALU.add))
            st.wait()
            st.inc(scan(f, d_t, e, 0.0, ALU.mult, ALU.add))
            st.inc(combined(eu, eu, EXP30, ek, ALU.min, ALU.add))
            st.wait()
            st.inc(scan(e[:, ::-1], d_t, e[:, ::-1], 0.0, ALU.mult, ALU.add))
            st.inc(eng.tensor_scalar(eu, eu, 1e-8, o, ALU.max, ALU.mult))
            st.wait()
            st.inc(combined(e[:, 1:T], f[:, 0:T - 1], d, e[:, 1:T], ALU.mult, ALU.add))
            st.wait()
            st.inc(combined(v, v, 1.0, e, ALU.mult, ALU.add))

        def out_slot(b, tb):
            return og2 if b == 0 and tb >= 2 else og

        def att_lo(eng, ops, n, part):
            eng.wait_ge(aw_hi_ready[part], n)
            o = slice(*PART[part])
            ops.tensor_tensor(aw_lo[:, o], aw_in[:, o], aw_hi[:, o].bitcast(F32), ALU.subtract).then_inc(aw_split[part], 1)

        def gate_exps(eng, n, slot, use, ek, eu):
            eng.wait_ge(g_in[slot], 16 * (use + 1))
            A = nc.scalar.activation
            A(ek, g_v[:, slot, :], ACT.Exp).then_inc(g_exp, 1)
            A(eu, g_v[:, slot, :], ACT.Exp, bias=u_all[:, bass.ds(n, 1)]).then_inc(g_exp, 1)

        def gate_clamp(eng, n, ek, eu):
            eng.wait_ge(g_exp, 2 * (n - G_VEC + 1))
            for t_ in (ek, eu):
                nc.vector.tensor_scalar(t_, t_, EXP30, None, ALU.min).then_inc(g_vec, 1)

        def gate_scans(eng, n, ek, e, r1, r2):
            k = n - G_VEC
            d = decay[:, bass.ds(n, 1)]
            eng.wait_ge(g_pool, P_DONE * k + P_PRODUCTS)
            for src, r in ((e, r1), (ek, r2)):
                nc.vector.tensor_tensor_scan(r[:, 0:T - 1][:, ::-1], src[:, 1:T][:, ::-1], d.to_broadcast([P, T - 1]), 0.0,
                                             ALU.add, ALU.mult).then_inc(g_vec, 1)
            eng.wait_ge(g_vec, V_INVERSE * k + V_FUTURE)
            for src in (e, ek):
                nc.vector.tensor_tensor_scan(src, d.to_broadcast([P, T]), src, 0.0, ALU.mult, ALU.add).then_inc(g_vec, 1)

        def gate_inverse(eng, n, ek, eu):
            k = n - G_VEC
            eng.wait_ge(g_pool, P_DONE * k + P_DEN)
            nc.vector.tensor_scalar(eu, eu, 1e-8, oscale[:, bass.ds(n, 1)], ALU.max, ALU.mult).then_inc(g_vec, 1)
            eng.wait_ge(g_vec, V_INVERSE * (k + 1) - 1)
            nc.vector.reciprocal(ek, eu).then_inc(g_vec, 1)

        def gate_products(eng, n, v, ek, eu, e):
            eng.wait_ge(g_vec, V_INVERSE * (n - G_VEC) + V_CLAMPED)
            nc.gpsimd.tensor_tensor(e, ek, v, ALU.mult)
            eng.drain()
            nc.gpsimd.tensor_tensor(v, eu, v, ALU.mult).then_inc(g_pool, 1)

        def gate_add(eng, n, v, ek, eu, e, r1, r2):
            eng.wait_ge(g_vec, V_INVERSE * (n - G_VEC) + V_SUMS)
            last = slice(0, T - 1)
            add = nc.gpsimd.tensor_tensor
            add(ek[:, last], ek[:, last], r2[:, last], ALU.add)
            add(e[:, last], e[:, last], r1[:, last], ALU.add)
            eng.drain()
            add(eu, eu, ek, ALU.add).then_inc(g_pool, 1)
            add(v, v, e, ALU.add)
            eng.drain()

        def gate_result(eng, n, v, ek):
            eng.wait_ge(g_vec, V_INVERSE * (n - G_VEC + 1))
            nc.gpsimd.tensor_tensor(v, v, ek, ALU.mult).then_inc(g_pool, 1)

        def token_copies(eng, b):
            odd = eng is nc.vector
            if not odd:
                eng.wait_ge(lgt_done, b + 1)
                if b >= 2:
                    eng.wait_ge(lgt_used, b - 1)
                nc.scalar.activation(lgT[:, b % 2, :], LGT[b % 2][0:E, :], ACT.Copy).then_inc(lgt_copied, 1)
            for tb in range(1 if odd else 0, TB, 2):
                a = b * TB + tb
                eng.wait_ge(ut_T, a + 1)
                if b:
                    eng.wait_ge(ut_stored[tb], 16 * b)
                if odd:
                    nc.vector.tensor_copy(ut[:, tb, :], UT[tb][:]).then_inc(ut_copied[1], 1)
                else:
                    nc.scalar.activation(ut[:, tb, :], UT[tb][:], ACT.Copy).then_inc(ut_copied[0], 1)

        def mamba_tile(b, t):
            return b * G_MAMBA + (G_VEC + G_PRE + t), t % 2, b * (G_MAMBA // 2) + (G_PRE + t) // 2

        def moe_tile(pair, h):
            return pair * 2 + (G_MOE + h), (G_MOE + h) % 2, pair + (G_MOE + h - G_VEC) // 2

        def pre_buf(i):
            return xdt[:, i // 2, (i % 2) * T:(i % 2 + 1) * T]

        pre_v, pre_ek = ([pre_buf(i + o) for i in range(KC)] for o in (0, KC))
        pre_eu = [state[:, i // 2, (i % 2) * T:(i % 2 + 1) * T] for i in range(KC)]

        block = ctx.enter_context(nc.Block())
        @block.sync
        def _(sp):
            for counted in (*g_out, gm_fetched):
                sp.sem_inc(counted, FIRST_DMA)
            sp.dma_start(cols[:], cols_d).then_inc(loaded, 16)
            sp.dma_start(rows[:], rows_d).then_inc(loaded, 16)
            sp.dma_start(condT_s[:], condT).then_inc(loaded, 16)
            sp.dma_start(gw[:], gw_d).then_inc(loaded, 16)

            for i in range(KC):
                sp.dma_start(pre_v[i], fT[i]).then_inc(pre_in, 16)
            for i in range(G_PRE):
                g_load(sp, G_VEC + i, i, 0)
            for b in range(BATCH):
                sp.dma_start(XT[:, :, b * T:(b + 1) * T], x_view[:, :, b * T:(b + 1) * T]).then_inc(x_loaded, 16)
            g_store(sp, G_VEC, 0)

            def gates(b, last):
                for t in range(G_MAMBA):
                    n, slot, use = mamba_tile(b, t)
                    g_load(sp, n, slot, use)
                    if t == G_MAMBA - 1:
                        sp.wait_ge(z_done, FIRST + PAIRS * (b + 1))
                        if not last:
                            fetch_gate(0, b + 1, um[:], gm_fetched)
                        else:
                            for nxt in range(BATCH):
                                fetch_gate(1, nxt, uf1[:, nxt], g_fetched[nxt])
                    g_store(sp, n - 1, 1 - slot)

            def fetch_gate(layer, b, dst, fetched):
                first = TILES * layer + b * KC
                for i in range(2):
                    if layer < N_GATES - 1:
                        sp.wait_ge(g_out[i], FIRST_DMA + 16 * ((first + KC - G_VEC) // 2))
                    elif i == A_SLOT:
                        sp.wait_ge(g_out[i], FIRST_DMA + 16 * (SLOT_USES[i] + first + KC - G_ATT))
                    else:
                        sp.wait_ge(g_out[i], FIRST_DMA + 16 * SLOT_USES[i])
                src = g_dram[bass.ds(first, KC)].rearrange("k p t -> p k t")
                sp.dma_start(dst, src).then_inc(fetched, 16)

            with sp.Fori(0, BATCH - 1) as b:
                gates(b, False)
            gates(BATCH - 1, True)
            sp.wait_ge(x_added, KC * BATCH)
            sp.wait_ge(masks_ready, N_MASKS + 1)
            sp.dma_start(rc[:], rc_d).then_inc(moe_loaded, 16)
            for h in range(2):
                sp.dma_start(bias_f[32 * h:32 * h + E, :], bias_d).then_inc(moe_loaded, 16)

            def stage(e):
                for p in range(M_PIECES):
                    if not isinstance(e, int):
                        sp.wait_ge(w_split, M_PIECES * (e - 1) + p + 1)
                    src = moe_d[e] if isinstance(e, int) else moe_d[bass.ds(e, 1)].rearrange("o p w -> (o p) w")
                    o = slice(p * M_PIECE, (p + 1) * M_PIECE)
                    sp.dma_start(m_stage[:, o], src[:, o]).then_inc(m_staged[p], 16)

            for a in range(NT):
                if a == KC:
                    stage(0)
                sp.wait_ge(ut_copied[a % 2], a // 2 + 1)
                sp.dma_start(u_dram[a * P:(a + 1) * P, :], ut[:, a % 4, :]).then_inc(ut_stored[a % 4], 16)
            with sp.Fori(1, E) as e:
                stage(e)
            sp.wait_ge(dn_done, FIRST + NBLK)
            for i in range(3):
                sp.wait_ge(y_stored[i], FIRST_DMA + 16 * (NBLK // 3))
            def att_load(g, part):
                src = att_d[g] if isinstance(g, int) else att_d[bass.ds(g, 1)].rearrange("o p w -> (o p) w")
                o = slice(*PART[part])
                sp.dma_start(aw_in[:, o], src[:, o]).then_inc(a_staged[part], 16)

            for b in range(BATCH):
                fetch_gate(2, b, u_g[:, :, b * T:(b + 1) * T], g_fetched[b])
                if b == 0:
                    att_load(0, 0)
                    sp.wait_ge(cb_sum, TB)
                    att_load(0, 2)
                    att_load(0, 1)
            with sp.Fori(1, GROUPS) as g:
                sp.wait_ge(v_done, BATCH * g)
                att_load(g, 0)
                sp.wait_ge(q_done, HPG * BATCH * g)
                att_load(g, 2)
                sp.wait_ge(dense_done, KC * BATCH * g)
                att_load(g, 1)
            def ffn_stage(s, before, par):
                if before is not None:
                    sp.wait_ge(fw_split, FIRST + before)
                src = ffn_d[s] if isinstance(s, int) else ffn_d[bass.ds(s, 1)].rearrange("o p w -> (o p) w")
                sp.dma_start(f_stage[:, par, :], src).then_inc(f_staged[par], 16)

            for b in range(BATCH):
                i = NI - BATCH + b
                sp.wait_ge(v_done, i + 1)
                sp.wait_ge(q_done, HPG * (i + 1))
                fetch_gate(3, b, u_g[:, :, b * T:(b + 1) * T], g_fetched[b])
                if b == BATCH - 2:
                    sp.wait_ge(g_out[A_SLOT], FIRST_DMA + 16 * (SLOT_USES[A_SLOT] + N_GATES * TILES - G_ATT))
                    ffn_stage(0, None, 0)
            sp.wait_ge(scores_done, HPG * NI)
            with sp.Fori(0, FS // 2) as it:
                ffn_stage(it * 2 + 1, it * 2, 1)
                ffn_stage(it * 2 + 2, it * 2 + 1, 0)
            finish(sp, fx_acc, FIRST + KC * BATCH * FS, KC)

        @block.gpsimd
        def _(pool):
            n = [0]

            def done(ins):
                ins.then_inc(masks_ready, 1)
                n[0] += 1

            def fill(dst, src, op, val, base, pattern, mult):
                pool.wait_ge(masks_ready, n[0])
                done(nc.gpsimd.affine_select(out=dst, in_=src, compare_op=op, fill=val, base=base, pattern=pattern,
                                             channel_multiplier=mult))

            for t_, v_ in ((ident[:], 0.0), (ident_b[:], 0.0), (ones[:], 1.0), (sel_h[:].bitcast(F32), 0.0),
                           (causal_b[:], 0.0), (tri[:], 1.0), (neg4[:], 0.0), (sel_p[:].bitcast(F32), 0.0),
                           (csT[:].bitcast(F32), 0.0), (eps_c[:], EPS)):
                done(nc.gpsimd.memset(t_, v_))
            fill(ident[:], ident[:], ALU.not_equal, 1.0, 0, [[-1, P]], 1)
            fill(ident_b[:], ident_b[:], ALU.not_equal, 1.0, 0, [[-1, P]], 1)
            fill(causal_b[:], causal_b[:], ALU.is_ge, NEG, 0, [[-1, P]], 1)
            fill(tri[:], tri[:], ALU.is_ge, 0.0, 0, [[1, P]], -1)
            fill(neg4[:], neg4[:], ALU.is_ge, NEG, 0, [[0, TB], [1, P]], -1)
            for h in range(2):
                fill(sel_h[:], sel_h[:], ALU.not_equal, 1.0, -32 * h, [[-1, HEADS_M]], 1)
                fill(sel_p[:], sel_p[:], ALU.not_equal, 1.0, -32 * h, [[-2, PAIRS], [-1, 2], [0, HD]], 1)
            def slot_gate(n, slot, first=(), second=(), between=None):
                v, ek, eu = g_v[:, slot, :], g_ek[:, slot, :], g_eu[:, slot, :]
                gate_products(pool, n, v, ek, eu, g_e[:])
                for j, q in first:
                    gather(j, q)
                gate_add(pool, n, v, ek, eu, g_e[:], g_r1[:], g_r2[:])
                for j, q in second:
                    gather(j, q)
                if between is not None:
                    between()
                gate_result(pool, n, v, ek)

            with pool.Fori(0, (G_PRE + G_MAMBA * BATCH) // 2) as two:
                for slot in range(2):
                    slot_gate(two * 2 + (G_VEC + slot), slot)
            pool.wait_ge(x_added, KC * BATCH)
            done(nc.gpsimd.memset(bias_f[:], 0.0))

            for p in range(M_PIECES):
                pool.wait_ge(mw_hi_ready, p + 1)
                o = slice(p * M_PIECE, (p + 1) * M_PIECE)
                nc.gpsimd.tensor_tensor(mw[:, 0, 1, o], m_stage[:, o], mw[:, 0, 0, o].bitcast(F32), ALU.subtract).then_inc(w_split, 1)

            def gather(j, q):
                if not (isinstance(j, int) and j < 3):
                    pool.wait_ge(tu_done, j - 2)
                nc.gpsimd.tensor_copy(idx_now[:, q:q + 1], idx[:, bass.ds(j, 1)])
                pool.drain()
                nc.gpsimd.indirect_dma_start(ug[:, q, :], None, u_dram, bass.IndirectOffsetOnAxis(
                    ap=idx_now[:, q:q + 1], axis=0)).then_inc(gathered[q], 16)

            pool.wait_ge(route_vec, IDX_READY)
            for i in range(4):
                pool.wait_ge(ut_stored[i], 16 * (NT // 4))
            for j in range(3):
                gather(j, j)
            with pool.Fori(0, NBLK // 6) as pair:
                for h in range(2):
                    n, slot, _ = moe_tile(pair, h)
                    j = pair * 6 + 3 * (h + 1)
                    slot_gate(n, slot, [(j, 0), (j + 1, 1)], [(j + 2, 2)])

            def gather_out(a):
                if a >= TB:
                    pool.wait_ge(cb_T, a - 3 if a < TB + 2 else a - 1)
                dst = og2 if 2 <= a < TB else og
                for k in range(2):
                    nc.gpsimd.indirect_dma_start(
                        dst[:, a % 2, k, :], None, y_dram,
                        bass.IndirectOffsetOnAxis(ap=pos_i[:, k, a:a + 1], axis=0)).then_inc(og_in[a % 2], 16)

            def first_outputs():
                pool.wait_ge(dn_done, FIRST + NBLK)
                for i in range(3):
                    pool.wait_ge(y_stored[i], FIRST_DMA + 16 * (NBLK // 3))
                for a in range(TB):
                    gather_out(a)

            slot_gate(*moe_tile(NBLK // 6, 0)[:2], between=first_outputs)
            for a in range(TB, NT):
                gather_out(a)
            pool.wait_ge(cb_T, NT)

            def att_gate(n, between=None):
                v = g_v[:, A_SLOT, :]
                gate_products(pool, n, v, a_ek[:], a_eu[:], a_e[:])
                if between is not None:
                    between()
                gate_add(pool, n, v, a_ek[:], a_eu[:], a_e[:], a_r1[:], a_r2[:])
                gate_result(pool, n, v, a_ek[:])

            att_gate(G_ATT)
            with pool.Fori(1, GROUPS) as g:
                n = g * BATCH + (G_ATT - A_GATE - 1)
                att_lo(pool, nc.gpsimd, g + 1, 0)
                att_gate(n, lambda: att_lo(pool, nc.gpsimd, g + 1, 2))
                att_lo(pool, nc.gpsimd, g + 1, 1)
                for k in range(1, BATCH):
                    att_gate(n + k)

        @block.scalar
        def _(act):
            for counted in (*y_stored,):
                act.sem_inc(counted, FIRST_DMA)
            for counted in (out_copied, exp_done):
                act.sem_inc(counted, FIRST)
            A = nc.scalar.activation
            act.wait_ge(loaded, 64)
            act.wait_ge(masks_ready, N_MASKS)
            A(dec0[:], cols[:, COLS["w"]:COLS["w"] + 16], ACT.Exp).then_inc(setup_act, 1)
            act.wait_ge(setup_act, 1)
            A(dec0[:], dec0[:], ACT.Exp, scale=-1.0).then_inc(setup_act, 1)
            A(a_neg[:], rows[:, HEADS_M:2 * HEADS_M], ACT.Exp).then_inc(setup_act, 1)
            act.wait_ge(setup_mm, 1)
            A(tf[:], bank[0][:, 0:BATCH], ACT.Tanh, scale=0.5).then_inc(setup_act, 1)

            def gate(n, slot, use):
                gate_exps(act, n, slot, use, g_ek[:, slot, :], g_eu[:, slot, :])

            act.wait_ge(setup_step, SETUP_STEPS)
            act.wait_ge(pre_in, 16 * KC)
            act.dma_start(w_in[:], w_in_d).then_inc(w_loaded, 16)
            act.dma_start(w_out[:], w_out_d).then_inc(wo_loaded, 16)
            for i in range(KC):
                A(pre_ek[i], pre_v[i], ACT.Exp).then_inc(setup_act, 1)
                A(pre_eu[i], pre_v[i], ACT.Exp, bias=u_all[:, i:i + 1]).then_inc(setup_act, 1)
                if i < G_PRE:
                    gate(G_VEC + i, i, 0)

            def tanh_x(k, b, dst, reused):
                if reused is not None:
                    act.wait_ge(u_ready, FIRST + reused)
                A(dst, XT[:, :, tok(b)], ACT.Tanh, scale=0.5).then_inc(x_tanh, 1)

            act.wait_ge(wo_loaded, 16)
            for j in range(XC):
                A(w_out[:, j, :], w_out[:, j, :], ACT.Copy, scale=col("norm_w", j)).then_inc(wo_scaled, 1)

            act.wait_ge(x_loaded, 16 * BATCH)
            tanh_x(0, 0, txm[:], None)
            with act.Fori(0, BATCH) as b:
                act.wait_ge(dt_abs, b + 1)
                A(d_e[:], d_a[:], ACT.Exp, scale=-1.0).then_inc(dt_exp, 1)

                def first_tap(q, ch):
                    act.wait_ge(proj_done, N_CONV * b + q + 1)
                    if q >= 2:
                        act.wait_ge(act_ready, N_CONV * b + q - 1)
                    A(acc[q % 2], PJ[q % 2][:], ACT.Identity, bias=col("conv_b", ch),
                      scale=col("conv_w", 4 * ch + 3)).then_inc(tap0, 1)

                def conv_sig(q):
                    act.wait_ge(conv_tapped, N_CONV * b + q + 1)
                    if q >= 2:
                        act.wait_ge(act_ready, N_CONV * b + q - 1)
                    A(cth[q % 2], acc[q % 2], ACT.Tanh).then_inc(conv_tanh, 1)

                for q, ch in enumerate(CONV_ORDER):
                    first_tap(q, ch)
                    if q in (0, 4, 9):
                        gate(*mamba_tile(b, (0, 4, 9).index(q)))
                    if q:
                        conv_sig(q - 1)
                    if q == 5:
                        act.wait_ge(cs_neg, b + 1)
                        A(w2e[:], w2[:], ACT.Exp).then_inc(w_exp, 1)
                        A(cdec[:], SM[:, 128:128 + NB], ACT.Exp).then_inc(w_exp, 1)
                        A(csT[0:HEADS_M, :], EB[0:HEADS_M, :], ACT.Copy).then_inc(ct_hi, 1)
                conv_sig(N_CONV - 1)
                for tb in range(TB):
                    act.wait_ge(bc_done, TB * b + tb + 1)
                    A(b_tok[:, tb, :], SM[:, 192:320], ACT.Copy).then_inc(bc_copied, 1)
                    A(cb[:, tb, :], SM[:, 320:448], ACT.Copy).then_inc(bc_copied, 1)
                    if tb == 2:
                        gate(*mamba_tile(b, 3))
                act.wait_ge(act_ready, N_CONV * (b + 1))

                def square(j):
                    act.wait_ge(y_done, PAIRS * b + j + 1)
                    if j > 1:
                        act.wait_ge(sq_added, (PAIRS - 1) * b + j - 1)
                    A(sq[:, j % 2, :], xa[:, j, :], ACT.Square).then_inc(sq_done, 1)

                for j in range(PAIRS):
                    act.wait_ge(r_done, PAIRS * b + j + 1)
                    if j >= 2:
                        act.wait_ge(yy_done, PAIRS * b + j - 1)
                    for hh in range(2):
                        for tb in range(TB):
                            i = tb * HEADS_M + 2 * j + hh
                            A(lm[:, j % 2, hh, tb * P:(tb + 1) * P], (R0, R1)[hh][:, tb * P:(tb + 1) * P], ACT.Exp,
                              bias=csn[:, i:i + 1]).then_inc(l_done, 1)
                    act.wait_ge(z_done, FIRST + PAIRS * b + j + 1)
                    if j >= 2:
                        act.wait_ge(y_done, PAIRS * b + j - 1)
                    A(tz[:, j % 2, :], PJ[j % 2][:], ACT.Tanh, scale=0.5).then_inc(z_tanh, 1)
                    if j:
                        act.wait_ge(y_done, PAIRS * b + j)
                    A(e2[:], EB[:], ACT.Exp).then_inc(l_done, 1)
                    if j % 2:
                        gate(*mamba_tile(b, 4 + j // 2))
                    if j:
                        square(j - 1)
                square(PAIRS - 1)
                act.wait_ge(ssq_done, b + 1)
                A(e2[:], SM[:], ACT.Sqrt, scale=1.0 / D_IN, bias=eps_c[:]).then_inc(rms_done, 1)
                with act.If(b < BATCH - 1):
                    tanh_x(b + 1, (b + 1) % BATCH, txm[:], b + 1)
                with act.If(b == BATCH - 1):
                    act.wait_ge(x_added, KC * (BATCH - 1))
                    for nxt in range(BATCH - 1):
                        tanh_x(BATCH + nxt, nxt, txm[:], BATCH + nxt)

            act.wait_ge(x_added, KC * BATCH)
            tanh_x(2 * BATCH - 1, BATCH - 1, txm[:], 2 * BATCH - 1)
            for b in range(BATCH):
                token_copies(act, b)
            act.wait_ge(route_vec, LG_SUB)
            A(ex[:], lg[:], ACT.Exp).then_inc(lg_exp, 1)

            def up_tanh(j, q):
                act.wait_ge(g_done, j + 1)
                if not (isinstance(j, int) and j == 0):
                    act.wait_ge(y_ready, j)
                A(m_t[:], UG[q][:], ACT.Tanh, scale=0.851).then_inc(m_tanh, 1)

            def u_hi_copy(j):
                act.wait_ge(tu_done, j + 1)
                A(bu_hi[:].rearrange("p k t -> p (k t)"), TP[:], ACT.Copy).then_inc(bu_hi_ready, 1)

            def split_hi(e, slot):
                for p in range(M_PIECES):
                    act.wait_ge(m_staged[p], 16 * (e + 1))
                    o = slice(p * M_PIECE, (p + 1) * M_PIECE)
                    act.wait_ge(masks_ready, N_MASKS)
                    dst = mw[:, slot, 0, o] if isinstance(slot, int) else mw[:, bass.ds(slot, 1), 0, o].rearrange("p o w -> p (o w)")
                    A(dst, m_stage[:, o], ACT.Copy).then_inc(mw_hi_ready, 1)

            def block_act(pair, h, q, flags, last):
                it = pair * 2 + h
                j = it * 3 + q
                n, slot, use = moe_tile(pair, h)
                if q == 0:
                    gate(n, slot, use)
                if not (last and q == 2):
                    with act.If(flags[q] != 0):
                        e = act.value_load(tab[0:1, 1, j + 1:j + 2] if last else tab[0:1, 1, bass.ds(j + 1, 1)], min_val=1, max_val=E - 1)
                        act.wait_ge(dn_done, FIRST + j)
                        split_hi(e, e % 2)
                    up_tanh(j + 1, (q + 1) % 3)
                act.wait_ge(ty_done, j + 1)
                A(by_hi[:].rearrange("p k t -> p (k t)"), TP[:], ACT.Copy).then_inc(by_hi_ready, 1)
                if not (last and q >= 1):
                    u_hi_copy(j + 2)
                act.wait_ge(dn_done, FIRST + j + 1)
                act.wait_ge(y_stored[q], FIRST_DMA + 16 * it)
                A(m_o[:, q, :], DN[:], ACT.Copy, scale=0.5).then_inc(out_copied, 1)
                if q == 1:
                    g_store(act, n - 1, 1 - slot)
                if q == 2 and not last:
                    g_load(act, n + 1, 1 - slot, moe_tile(pair, h + 1)[2])
                act.wait_ge(out_copied, FIRST + j + 1)
                dst = y_dram[j * P:(j + 1) * P, :] if last else y_dram[bass.ds(j * P, P), :]
                act.dma_start(dst, m_o[:, q, :]).then_inc(y_stored[q], 16)

            split_hi(0, 0)
            act.wait_ge(route_vec, IDX_READY)
            act.wait_ge(route_vec, TAB_READY)
            g_load(act, *moe_tile(0, 0))
            u_hi_copy(0)
            up_tanh(0, 0)
            u_hi_copy(1)
            with act.Fori(0, NBLK // 6) as pair:
                for h in range(2):
                    flags = [act.value_load(tab[0:1, 2, bass.ds(pair * 6 + (3 * h + q), 1)], min_val=0, max_val=1) for q in range(3)]
                    for q in range(3):
                        block_act(pair, h, q, flags, False)
            flags = [act.value_load(tab[0:1, 2, NBLK - 3 + q:NBLK - 2 + q], min_val=0, max_val=1) for q in range(2)]
            for q in range(3):
                block_act(NBLK // 6, 0, q, flags, True)
            g_store(act, G_ATT - 1, 1 - A_SLOT)
            def gated_input(b, ffn=False):
                k = (3 if ffn else 2) * BATCH + b
                if ffn:
                    act.wait_ge(ax_acc, FIRST + KC * (NI - BATCH + b + 1))
                else:
                    act.wait_ge(cb_done, TB * (b + 1))
                A(u_in[:, :, tok(b % BATCH)], XT[:, :, tok(b % BATCH)], ACT.Tanh, scale=0.5).then_inc(x_tanh, 1)
                act.wait_ge(u_ready, FIRST + k + 1)
                act.wait_ge(masks_ready, N_MASKS)
                A(u_hi[:, :, tok(b % BATCH)], u_in[:, :, tok(b % BATCH)], ACT.Copy).then_inc(u_hi_ready, 1)

            def att_hi(n, part):
                act.wait_ge(a_staged[part], 16 * n)
                o = slice(*PART[part])
                A(aw_hi[:, o], aw_in[:, o], ACT.Copy).then_inc(aw_hi_ready[part], 1)

            def k_hi_copy(i):
                act.wait_ge(k_done, i + 1)
                if not (isinstance(i, int) and i == 0):
                    act.wait_ge(scores_done, HPG * i)
                A(k_hi[:], PP[KV_BANK][:], ACT.Copy).then_inc(k_hi_ready, 1)

            def vt_copy(i):
                act.wait_ge(v_done, i + 1)
                A(vT[:], PP[KV_BANK][:], ACT.Copy).then_inc(vt_copied, 1)

            def v_hi_copy(i):
                act.wait_ge(vt_done, i + 1)
                A(v_hi[:], TT_[0][:].rearrange("p (a d) -> p a d", a=TB), ACT.Copy).then_inc(v_hi_ready, 1)

            def q_hi_copy(i, h):
                act.wait_ge(q_done, HPG * i + h + 1)
                A(q_hi[:, h % 2, :], PP[Q_BANK[h]][:], ACT.Copy).then_inc(q_hi_ready, 1)

            def probs_exp(i, h):
                act.wait_ge(max_ready, HPG * i + h + 1)
                if not (isinstance(i, int) and i == 0 and h < 2):
                    act.wait_ge(t_done, 3 * (HPG * i + h - 1))
                for qb in range(TB):
                    bk, c0, _ = S_AT[qb]
                    w = (qb + 1) * P
                    A(probs[:, h % 2, PR_AT[qb]:PR_AT[qb] + w], S_[bk][:, c0:c0 + w], ACT.Exp,
                      bias=nmx[:, h % 2, qb:qb + 1], scale=SCALE,
                      accum_out=rsum[:, h % 2, qb:qb + 1]).then_inc(exp_done, 1)

            def pt_hi_copy(i, h):
                for r, (bk, w, c0) in enumerate(T_GROUP):
                    act.wait_ge(t_done, 3 * (HPG * i + h) + r + 1)
                    A(pt_hi[:, c0:c0 + w], TT_[bk][:, 0:w], ACT.Copy).then_inc(pt_hi_ready, 1)

            def ctx_hi(i, h):
                act.wait_ge(c_done, FIRST + HPG * i + h + 1)
                A(cx_hi[:, h, :], PP[C_BANK[h]][:], ACT.Copy).then_inc(c_hi_ready, 1)

            att_hi(1, 0)
            gated_input(0)
            k_hi_copy(0)
            q_hi_copy(0, 0)
            q_hi_copy(0, 1)
            probs_exp(0, 0)
            q_hi_copy(0, 2)
            att_hi(1, 2)
            att_hi(1, 1)

            def att_act(i, first, last):
                vt_copy(i)
                pt_hi_copy(i, 0)
                probs_exp(i, 1)
                v_hi_copy(i)
                n, use = i + (G_ATT - A_GATE), i + (SLOT_USES[A_SLOT] - A_GATE)
                ctx_hi(i, 0)
                if last:
                    g_store(act, n - 1, A_SLOT)
                elif not first:
                    with act.If(i > A_GATE):
                        g_store(act, n - 1, A_SLOT)
                if first:
                    gated_input(1)
                elif not last:
                    with act.If(i % BATCH == BATCH - 1):
                        att_hi(i // BATCH + 2, 0)
                pt_hi_copy(i, 1)
                probs_exp(i, 2)
                q_hi_copy(i, 3)
                ctx_hi(i, 1)
                if not (first or last):
                    with act.If(i >= A_GATE):
                        g_load(act, n, A_SLOT, use)
                pt_hi_copy(i, 2)
                if not last:
                    k_hi_copy(i + 1)
                probs_exp(i, 3)
                if not last:
                    q_hi_copy(i + 1, 0)
                ctx_hi(i, 2)
                if not (first or last):
                    with act.If(i >= A_GATE):
                        gate_exps(act, n, A_SLOT, use, a_ek[:], a_eu[:])
                if not last:
                    q_hi_copy(i + 1, 1)
                    if not first:
                        with act.If(i % BATCH == 0):
                            att_hi(i // BATCH + 1, 1)
                pt_hi_copy(i, 3)
                if not last:
                    probs_exp(i + 1, 0)
                    q_hi_copy(i + 1, 2)
                ctx_hi(i, 3)
                if first:
                    gated_input(2)
                elif not last:
                    with act.If(i == 1):
                        gated_input(3)
                    for b in range(2):
                        with act.If(i == NI - BATCH + 1 + b):
                            gated_input(b, True)
                    with act.If(i % BATCH == BATCH - 1):
                        att_hi(i // BATCH + 2, 2)

            att_act(0, True, False)
            with act.Fori(1, NI - 1) as i:
                att_act(i, False, False)
            att_act(NI - 1, False, True)
            gated_input(2, True)

            def ffn_hi(s, par, uses, free):
                act.wait_ge(f_staged[par], 16 * uses)
                if free is not None:
                    act.wait_ge(f_down, FIRST + free)
                A(fw_hi[:, par, :], f_stage[:, par, :], ACT.Copy).then_inc(fw_hi_ready, 1)

            def ffn_y(s, b):
                k = s * BATCH + b
                act.wait_ge(f_split, FIRST + k)
                act.wait_ge(f_up, k + 1)
                if b == 0:
                    act.wait_ge(f_scaled, 2 * (s + 1))
                A(f_t[:], FG[b % 2][:], ACT.Tanh, scale=f_sc[:, 0:1]).then_inc(f_tanh, 1)
                A(f_u[:], FU[b % 2][:], ACT.Copy, scale=f_sc[:, 1:2]).then_inc(f_lin, 1)
                act.wait_ge(f_yready, FIRST + k + 1)
                A(f_hi[:, b % 2, :], f_y[:], ACT.Copy).then_inc(f_hi_ready, 1)

            ffn_hi(0, 0, 1, None)
            gated_input(3, True)
            ffn_y(0, 0)

            def ffn_act(it, par, last):
                s = it * 2 + par
                for b in range(BATCH):
                    if b < BATCH - 1:
                        ffn_y(s, b + 1)
                    elif not last:
                        ffn_y(s + 1, 0)
                    if b == 1 and not last:
                        ffn_hi(s + 1, 1 - par, it + 1 + par, KC * BATCH * s)

            with act.Fori(0, FS // 2) as it:
                ffn_act(it, 0, False)
                ffn_act(it, 1, False)
            ffn_act(FS // 2, 0, True)

        @block.vector
        def _(dve):
            for counted in (u_ready, fw_split, f_split, pt_split, ax_acc, f_yready, fx_acc):
                dve.sem_inc(counted, FIRST)
            V = nc.vector
            setup = Steps(dve, setup_step)
            dve.wait_ge(loaded, 64)

            def spread(name, i):
                return cols[:, COLS[name] + 4 * i:COLS[name] + 4 * i + 4].unsqueeze(1).to_broadcast([P, BATCH, KC])

            def gate_cols(t_, i):
                return t_[:, TILES * i:TILES * (i + 1)].rearrange("p (b c) -> p b c", b=BATCH)

            for i in range(N_GATES):
                setup.inc(V.tensor_copy(gate_cols(u_all, i), spread("u", i)))
            setup.inc(V.tensor_scalar(gsh[:], cols[:, COLS["gate_s"]:COLS["gate_s"] + FS], 0.5, None, ALU.mult))
            cw = cols[:, COLS["conv_w"]:COLS["conv_w"] + 5 * N_CONV]
            setup.inc(V.tensor_scalar(cw, cw, 0.5, None, ALU.mult))
            setup.wait()
            setup.inc(V.tensor_tensor(ush[:], gsh[:], cols[:, COLS["up_s"]:COLS["up_s"] + FS], ALU.mult))
            dve.wait_ge(setup_act, 4)
            setup.inc(V.tensor_scalar(a_neg[:], a_neg[:], -1.0, None, ALU.mult))
            setup.inc(V.tensor_scalar(fac[:], tf[:], 0.25, 0.75, ALU.mult, ALU.add))
            setup.inc(V.tensor_scalar(osc[:], tf[:], 0.05, 0.45, ALU.mult, ALU.add))
            setup.wait()
            setup.inc(V.reciprocal(osc[:], osc[:]))
            setup.wait()
            for i in range(N_GATES):
                d0 = dec0[:, 4 * i:4 * i + 4].unsqueeze(1).to_broadcast([P, BATCH, KC])
                setup.inc(V.tensor_tensor(gate_cols(decay, i), d0, fac[:].unsqueeze(2).to_broadcast([P, BATCH, KC]), ALU.mult))
                setup.inc(V.tensor_copy(gate_cols(oscale, i), osc[:].unsqueeze(2).to_broadcast([P, BATCH, KC])))
            setup.wait()
            assert setup.n == SETUP_STEPS
            dve.wait_ge(masks_ready, N_MASKS)

            def gate(tile, part):
                n, slot, _ = tile
                ek, eu = g_ek[:, slot, :], g_eu[:, slot, :]
                if part == 0:
                    gate_clamp(dve, n, ek, eu)
                elif part == 1:
                    gate_scans(dve, n, ek, g_e[:], g_r1[:], g_r2[:])
                else:
                    gate_inverse(dve, n, ek, eu)

            for i in range(KC):
                dve.wait_ge(setup_act, 4 + 2 * (i + 1))
                gate_sums(V, setup, decay[:, i:i + 1], oscale[:, i:i + 1], pre_v[i], pre_ek[i], pre_eu[i], *acc)
                setup.wait()
                setup.inc(V.reciprocal(pre_ek[i], pre_eu[i]))
                setup.wait()
                setup.inc(V.tensor_tensor(um[:, i, :], pre_v[i], pre_ek[i], ALU.mult))
                for slot, part in (((0, 0),), ((0, 1),), ((0, 2), (1, 0)), ((1, 1),))[i]:
                    gate((G_VEC + slot, slot, 0), part)
            setup.wait()

            def gated(k, u, tx, fetched, n):
                dve.wait_ge(x_tanh, k + 1)
                dve.wait_ge(fetched, 16 * n)
                V.scalar_tensor_tensor(u, tx, 1.0, u, ALU.add, ALU.mult).then_inc(u_ready, 1)

            step = Steps(dve, dve_step)
            def mamba_input(b):
                gated(b, um[:].rearrange("p k t -> p (k t)"), txm[:].rearrange("p k t -> p (k t)"), gm_fetched, b + 1)

            def moe_input(b):
                gated(BATCH + b, uf1[:, b].rearrange("p k t -> p (k t)"), txm[:].rearrange("p k t -> p (k t)"), g_fetched[b], 1)

            mamba_input(0)
            gate((G_VEC + 1, 1, 0), 2)
            with dve.Fori(0, BATCH) as b:
                step.base = b * DVE_MAMBA
                dve.wait_ge(dt_raw, b + 1)
                dtb = rows[:, 0:HEADS_M].unsqueeze(1).to_broadcast([P, TB, HEADS_M])

                def th(t_):
                    return t_[:].rearrange("p (a h) -> p a h", a=TB)

                step.inc(V.tensor_tensor(th(d_x), SM[:, 0:NB].rearrange("p (a h) -> p a h", a=TB), dtb, ALU.add))
                step.wait()
                V.scalar_tensor_tensor(d_a[:], d_x[:], -1.0, d_x[:], ALU.mult, ALU.max).then_inc(dt_abs, 1)
                dve.wait_ge(dt_exp, b + 1)
                step.inc(V.tensor_scalar(d_s[:], d_e[:], 2.0, None, ALU.add))
                step.wait()
                step.inc(V.reciprocal(d_p[:], d_s[:]))
                step.wait()
                step.inc(V.tensor_tensor(d_s[:], d_e[:], d_p[:], ALU.mult))
                step.wait()
                step.inc(V.tensor_tensor(d_q[:], d_s[:], d_s[:], ALU.mult))
                step.wait()
                step.inc(V.tensor_scalar(d_p[:], d_q[:], 1.0 / 17, None, ALU.mult))
                for i in range(7, 0, -1):
                    step.wait()
                    step.inc(V.scalar_tensor_tensor(d_p[:], d_p[:], 1.0 / (2 * i + 1), d_q[:], ALU.add, ALU.mult))
                step.wait()
                step.inc(V.scalar_tensor_tensor(d_p[:], d_p[:], 1.0, d_s[:], ALU.add, ALU.mult))
                step.inc(V.tensor_scalar(d_x[:], d_x[:], 0.0, None, ALU.max))
                step.wait()
                step.inc(V.scalar_tensor_tensor(dt_t[:], d_p[:], 2.0, d_x[:], ALU.mult, ALU.add))
                step.wait()
                V.tensor_tensor(th(d_A), th(dt_t), a_neg[:].unsqueeze(1).to_broadcast([P, TB, HEADS_M]),
                                ALU.mult).then_inc(dA_ready, 1)

                def taps(q, ch):
                    dve.wait_ge(tap0, N_CONV * b + q + 1)
                    for k in range(1, 4):
                        if k > 1:
                            step.wait()
                        ins = V.scalar_tensor_tensor(acc[q % 2][:, k:T], PJ[q % 2][:, 0:T - k], col("conv_w", 4 * ch + 3 - k),
                                                     acc[q % 2][:, k:T], ALU.mult, ALU.add)
                        if k < 3:
                            step.inc(ins)
                        else:
                            ins.then_inc(conv_tapped, 1)

                def conv_out(q, ch):
                    dve.wait_ge(conv_tanh, N_CONV * b + q + 1)
                    dst = xa[:, ch, :] if ch < XC else (bT, cT)[ch - XC][:]
                    V.scalar_tensor_tensor(dst, cth[q % 2], 1.0, acc[q % 2], ALU.add, ALU.mult).then_inc(act_ready, 1)

                for q, ch in enumerate(CONV_ORDER):
                    taps(q, ch)
                    if q:
                        conv_out(q - 1, CONV_ORDER[q - 1])
                    if q == 4:
                        dve.wait_ge(cs_done, b + 1)
                        step.inc(V.tensor_scalar(csn[:], SM[:, 64:64 + NB], -1.0, None, ALU.mult))
                        step.wait()
                        V.tensor_tensor(w2[:], SM[:, 128:128 + NB], csn[:], ALU.add).then_inc(cs_neg, 1)
                    if q == 6:
                        dve.wait_ge(w_exp, 2 * (b + 1))
                        step.inc(V.tensor_tensor(dts[:], w2e[:], dt_t[:], ALU.mult))
                        dve.wait_ge(ct_hi, b + 1)
                        V.tensor_tensor(csT[32:32 + HEADS_M, :], EB[0:HEADS_M, :], csT[0:HEADS_M, :].bitcast(F32),
                                        ALU.subtract).then_inc(ct_ready, 1)
                    if q in GATE_CONV:
                        gate(mamba_tile(b, GATE_CONV.index(q) // 3), GATE_CONV.index(q) % 3)
                conv_out(N_CONV - 1, CONV_ORDER[-1])
                step.wait()

                def per_head(t_, tb, half):
                    h0 = tb * HEADS_M + 8 * half
                    return t_[:, h0:h0 + 8].unsqueeze(2).to_broadcast([P, 8, HD])

                def state_sum(tb):
                    dve.wait_ge(s_done, (TB - 1) * b + tb + 1)
                    for half in range(2):
                        o = slice(half * 512, half * 512 + 512)
                        if tb:
                            if half == 0:
                                dve.wait_ge(state_done, (TB - 1) * b + tb)
                            step.inc(V.tensor_tensor(state[:, tb, o].rearrange("p (h d) -> p h d", h=8),
                                                     state[:, tb - 1, o].rearrange("p (h d) -> p h d", h=8),
                                                     per_head(cdec, tb, half), ALU.mult))
                            step.wait()
                            ins = V.tensor_tensor(state[:, tb, o], state[:, tb, o], PJ[half][:], ALU.add)
                        else:
                            ins = V.tensor_copy(state[:, tb, o], PJ[half][:])
                        if half:
                            ins.then_inc(state_done, 1)
                        else:
                            step.inc(ins)

                for tb in range(TB):
                    dve.wait_ge(x_transposed, TB * b + tb + 1)
                    if tb:
                        dve.wait_ge(s_done, (TB - 1) * b + tb)
                    for dst, factor in ((xdt2[:, :], dts), (xdt[:, tb, :], dt_t)):
                        if factor is dts and tb == TB - 1:
                            continue
                        for half in range(2):
                            o = slice(half * 512, half * 512 + 512)
                            xt = XB[tb % 2][half][:].rearrange("p (h d) -> p h d", h=8)
                            ins = V.tensor_tensor(dst[:, o].rearrange("p (h d) -> p h d", h=8), xt,
                                                  per_head(factor, tb, half), ALU.mult)
                            if factor is dt_t and half:
                                ins.then_inc(xdt_done, 1)
                            else:
                                step.inc(ins)
                    if tb:
                        state_sum(tb - 1)
                    gate(mamba_tile(b, 2 if tb else 1), tb - 1 if tb else 2)

                def masked(j):
                    dve.wait_ge(l_done, 9 * (PAIRS * b + j) + 8)
                    for hh in range(2):
                        V.tensor_tensor(lm[:, j % 2, hh, :], lm[:, j % 2, hh, :], cb[:].rearrange("p a l -> p (a l)"),
                                        ALU.mult).then_inc(m_ready, 1)
                    dve.wait_ge(z_tanh, PAIRS * b + j + 1)
                    V.scalar_tensor_tensor(tz[:, j % 2, :], tz[:, j % 2, :], 1.0, PJ[j % 2][:], ALU.add, ALU.mult).then_inc(zs_done, 1)

                masked(0)
                gate(mamba_tile(b, 3), 0)
                for j in range(PAIRS):
                    if j < PAIRS - 1:
                        masked(j + 1)
                    dve.wait_ge(yy_done, PAIRS * b + j + 1)
                    dve.wait_ge(l_done, 9 * (PAIRS * b + j + 1))
                    xj = xa[:, j, :]
                    step.inc(V.scalar_tensor_tensor(xj, xj, col("d_skip", j), YD[:], ALU.mult, ALU.add))
                    step.inc(V.tensor_tensor(e2[:, P:T], YO[:, P:T], e2[:, P:T], ALU.mult))
                    step.wait()
                    step.inc(V.tensor_tensor(xj[:, P:T], xj[:, P:T], e2[:, P:T], ALU.add))
                    step.wait()
                    V.scalar_tensor_tensor(xj, xj, 0.5, tz[:, j % 2, :], ALU.mult, ALU.mult).then_inc(y_done, 1)
                    if j % 2 == 0:
                        gate(mamba_tile(b, 3 + j // 2), 1)
                    else:
                        gate(mamba_tile(b, 3 + j // 2), 2)
                        gate(mamba_tile(b, 4 + j // 2), 0)
                gate(mamba_tile(b, 7), 1)
                dve.wait_ge(rms_done, b + 1)
                step.inc(V.reciprocal(rms_inv, e2[:]))
                with dve.If(b < BATCH - 1):
                    mamba_input(b + 1)
                with dve.If(b == BATCH - 1):
                    for nxt in range(BATCH - 1):
                        moe_input(nxt)
                step.wait()
                for m in range(KC):
                    if m == 1:
                        gate(mamba_tile(b, 7), 2)
                    dve.wait_ge(out_done, KC * b + m + 1)
                    step.inc(V.tensor_tensor(tz[:, m % 2, :], OB[m][:], rms_inv, ALU.mult))
                    step.wait()
                    V.tensor_tensor(XT[:, m, tok(b)], XT[:, m, tok(b)], tz[:, m % 2, :], ALU.add).then_inc(x_added, 1)
                assert step.n == DVE_MAMBA, step.n
            def flat(t_):
                return t_.rearrange("p k t -> p (k t)")

            route = Steps(dve, dve_step)
            route.base = DVE_MAMBA * BATCH

            def rconst(name, n, at=0):
                return rc[:, RC[name] + at:RC[name] + at + n]

            def each(ins):
                route.inc(ins)
                route.wait()

            moe_input(BATCH - 1)
            for b in range(BATCH):
                token_copies(dve, b)
                if b == 1:
                    dve.wait_ge(moe_loaded, 48)
                    each(V.tensor_scalar(bias_f[:, 2 * I_MOE:], bias_f[:, 2 * I_MOE:], 2.0, None, ALU.mult))
                    each(V.tensor_copy(bias_r[:], bias_f[:]))
                    route.inc(V.tensor_tensor(bias_r[32:32 + E, :], bias_f[32:32 + E, :], bias_r[32:32 + E, :].bitcast(F32), ALU.subtract))
            wide = [P, NT, E]
            dve.wait_ge(route_mm, LGP_DONE)
            gb = rows[:, 2 * HEADS_M:2 * HEADS_M + E].unsqueeze(1).to_broadcast(wide)
            each(V.tensor_tensor(lg[:], LGP[:, 0:NT * E].rearrange("p (a e) -> p a e", a=NT), gb, ALU.add))
            for a in range(NT):
                route.inc(V.max(mx8[:, a, :], lg[:, a, :]))
            route.wait()
            m2 = mx8[:, :, 1:2].to_broadcast(wide)
            route.inc(V.tensor_tensor(gt[:], lg[:], m2, ALU.is_gt))
            each(V.tensor_tensor(eq[:], lg[:], m2, ALU.is_equal))
            V.tensor_tensor(lg[:], lg[:], mx8[:, :, 0:1].to_broadcast(wide), ALU.subtract).then_inc(route_vec, 1)
            rst = rconst("rst", NT * E)
            route.inc(V.tensor_reduce(r4[:, 0, :], gt[:], AX.X, ALU.add))
            each(V.tensor_tensor_scan(pre[:].rearrange("p a e -> p (a e)"), rst, eq[:].rearrange("p a e -> p (a e)"), 0.0,
                                      ALU.mult, ALU.add))
            each(V.tensor_scalar(r4[:, 0, :], r4[:, 0, :], -1.0, 2.0, ALU.mult, ALU.add))
            each(V.tensor_tensor(pre[:], pre[:], r4[:, 0, :].unsqueeze(2).to_broadcast(wide), ALU.is_le))
            each(V.tensor_tensor(eq[:], eq[:], pre[:], ALU.mult))
            V.tensor_tensor(gt[:], gt[:], eq[:], ALU.add).then_inc(route_vec, 1)
            dve.wait_ge(route_vec, MASK_READY)
            route.inc(V.tensor_tensor_scan(pre[:].rearrange("p a e -> p (a e)"), rst, gt[:].rearrange("p a e -> p (a e)"), 0.0,
                                           ALU.mult, ALU.add))
            dve.wait_ge(lg_exp, 1)
            each(V.tensor_tensor(wx[:], ex[:], gt[:], ALU.mult))
            route.inc(V.scalar_tensor_tensor(sel1[:], pre[:], 1.5, gt[:], ALU.is_lt, ALU.mult))
            each(V.tensor_reduce(r4[:, 0, :], wx[:], AX.X, ALU.add))
            route.inc(V.tensor_tensor(sel2[:], gt[:], sel1[:], ALU.subtract))
            each(V.reciprocal(r4[:, 1, :], r4[:, 0, :]))
            dve.wait_ge(route_mm, PREFIX_DONE)
            each(V.tensor_copy(excl[:].rearrange("p a e -> p (a e)").rearrange("p (e a) -> p e a", e=E),
                               LGP[:, 256:384].rearrange("p (a e) -> p e a", a=NT)))
            each(V.tensor_tensor_scan(incl[:].rearrange("p a e -> p (a e)"), rconst("rst2", NT * E),
                                      excl[:].rearrange("p a e -> p (a e)"), 0.0, ALU.mult, ALU.add))
            by_e = incl[:].rearrange("p a e -> p (a e)").rearrange("p (e a) -> p e a", e=E)
            ex_e = excl[:].rearrange("p a e -> p (a e)").rearrange("p (e a) -> p e a", e=E)
            route.inc(V.tensor_tensor(excl[:], incl[:], excl[:], ALU.subtract))
            cmp_ = rtmp[:].rearrange("p a e -> p (a e)").rearrange("p (e a) -> p e a", e=E)
            each(V.tensor_tensor(cmp_, by_e[:, :, NT - 1:NT].to_broadcast([P, E, NT]),
                                 rconst("full", NT).unsqueeze(1).to_broadcast([P, E, NT]), ALU.is_gt))
            each(V.tensor_reduce(nb[:, 0, :], cmp_, AX.X, ALU.add))
            each(V.tensor_tensor_scan(nb[:, 1, :], ones[:, 0:E], nb[:, 0, :], 0.0, ALU.mult, ALU.add))
            each(V.tensor_tensor(nb[:, 2, :], nb[:, 1, :], nb[:, 0, :], ALU.subtract))
            route.inc(V.tensor_tensor(posm[:], LGP[:, 128:256].rearrange("p (a e) -> p a e", a=NT),
                                      ex_e.rearrange("p e a -> p a e"), ALU.add))
            each(V.tensor_scalar(nb[:, 2, :], nb[:, 2, :], float(P), None, ALU.mult))
            each(V.tensor_tensor(posm[:], posm[:], nb[:, 2, :].unsqueeze(1).to_broadcast(wide), ALU.add))
            for k, sel in enumerate((sel1, sel2)):
                each(V.tensor_tensor(rtmp[:], sel[:], posm[:], ALU.mult))
                each(V.tensor_reduce(posf[:, 0, k, :], rtmp[:], AX.X, ALU.add))
            each(V.tensor_scalar(posf[:, 1], posf[:, 0], 63.5, 1.0 / P, ALU.subtract, ALU.mult))
            each(V.tensor_scalar(posf[:, 1], posf[:, 1], ROUND, ROUND, ALU.add, ALU.subtract))
            each(V.scalar_tensor_tensor(posf[:, 2], posf[:, 1], -float(P), posf[:, 0], ALU.mult, ALU.add))

            def choices(i, n):
                return posf[:, i].rearrange("p k a -> p (k a)").unsqueeze(2).to_broadcast([P, 2 * NT, n])

            dve.wait_ge(route_mm, U_DONE)
            for i in range(4):
                dve.wait_ge(ut_stored[i], 16 * (NT // 4))
            route.inc(V.tensor_tensor(oh_r[:], choices(2, P), rconst("iota", P).unsqueeze(1).to_broadcast([P, 2 * NT, P]),
                                      ALU.is_equal))
            each(V.tensor_tensor(oh_j[:], choices(1, NBLK), rconst("iota", NBLK).unsqueeze(1).to_broadcast([P, 2 * NT, NBLK]),
                                 ALU.is_equal))
            route.inc(V.tensor_tensor(oh_v[:, :, 0, :], oh_j[:], rconst("blk", 2 * NT).unsqueeze(2).to_broadcast([P, 2 * NT, NBLK]),
                                      ALU.mult))
            V.tensor_scalar(oh_v[:, :, 1, :], oh_j[:], rconst("place", 1), None, ALU.mult).then_inc(route_vec, 1)
            each(V.tensor_tensor(ecmp[:], nb[:, 1, :].unsqueeze(1).to_broadcast([P, NBLK + 1, E]),
                                 rconst("iota", NBLK + 1).unsqueeze(2).to_broadcast([P, NBLK + 1, E]), ALU.is_le))
            each(V.tensor_reduce(etab[:, 0, :], ecmp[:], AX.X, ALU.add))
            route.inc(V.memset(etab[:, 1, 0:1], 0.0))
            route.inc(V.memset(etab[:, 2, NBLK:NBLK + 1], 0.0))
            each(V.tensor_scalar(etab[:, 0, :], etab[:, 0, :], E - 1.0, None, ALU.min))
            each(V.tensor_scalar(etab[:, 1, 1:NBLK + 1], etab[:, 0, 0:NBLK], 1.0, E - 1.0, ALU.add, ALU.min))
            each(V.tensor_tensor(etab[:, 2, 0:NBLK], etab[:, 1, 1:NBLK + 1], etab[:, 1, 0:NBLK], ALU.subtract))
            route.inc(V.tensor_copy(exp_of[:], etab[0:64, 0, :]))
            route.inc(V.tensor_copy(row_e[:], rconst("row", 1)[0:64]))
            V.tensor_copy(tab[:], etab[:]).then_inc(route_vec, 1)
            route.inc(V.tensor_copy(pos_i[:], posf[:, 0]))
            each(V.tensor_tensor(wx[:], wx[:], r4[:, 1, :].unsqueeze(2).to_broadcast(wide), ALU.mult))
            for k, sel in enumerate((sel1, sel2)):
                each(V.tensor_tensor(rtmp[:], sel[:], wx[:], ALU.mult))
                each(V.tensor_reduce(we[:, k, :], rtmp[:], AX.X, ALU.add))
            dve.wait_ge(route_mm, IDX_DONE)
            each(V.tensor_copy(idx_f[:], LGP[:, NBLK:2 * NBLK]))
            each(V.scalar_tensor_tensor(idx_f[:], LGP[:, 0:NBLK], float(P), idx_f[:], ALU.mult, ALU.add))
            V.tensor_copy(idx[:], idx_f[:]).then_inc(route_vec, 1)
            dve.wait_ge(route_vec, IDX_READY)
            dve.wait_ge(route_vec, TAB_READY)

            def split_lo(e, slot):
                for p in range(M_PIECES):
                    dve.wait_ge(mw_hi_ready, M_PIECES * e + p + 1)
                    o = slice(p * M_PIECE, (p + 1) * M_PIECE)
                    hi, lo = ((mw[:, slot, i, o] if isinstance(slot, int) else mw[:, bass.ds(slot, 1), i, o].rearrange("p o w -> p (o w)"))
                              for i in range(2))
                    V.tensor_tensor(lo, m_stage[:, o], hi.bitcast(F32), ALU.subtract).then_inc(w_split, 1)

            def select(j, q):
                if not (isinstance(j, int) and j < 3):
                    dve.wait_ge(dn_done, FIRST + j - 2)
                V.tensor_scalar(sel_e[:, q, :], row_e[:].to_broadcast([64, P]), exp_of[:, bass.ds(j, 1)], None,
                                ALU.is_equal).then_inc(sel_ready, 1)

            def glu(j, q):
                dve.wait_ge(m_tanh, j + 1)
                V.scalar_tensor_tensor(m_t[:], m_t[:], 1.0, UG[q][:], ALU.add, ALU.mult).then_inc(m_act, 1)

            def inner(j, q):
                dve.wait_ge(l2_done, j + 1)
                dve.wait_ge(m_act, j + 1)
                V.scalar_tensor_tensor(m_y[:], UL[q][:], 1.0, m_t[:], ALU.add, ALU.mult).then_inc(y_ready, 1)

            def u_lo_split(j):
                dve.wait_ge(bu_hi_ready, j + 1)
                V.tensor_tensor(flat(bu_lo[:]), TP[:], flat(bu_hi[:]).bitcast(F32), ALU.subtract).then_inc(bu_split, 1)

            def block_dve(pair, h, q, flags, last):
                j = pair * 6 + (3 * h + q)
                if not (last and q == 2):
                    with dve.If(flags[q] != 0):
                        e = dve.value_load(tab[0:1, 1, j + 1:j + 2] if last else tab[0:1, 1, bass.ds(j + 1, 1)], min_val=1, max_val=E - 1)
                        split_lo(e, e % 2)
                    glu(j + 1, (q + 1) % 3)
                dve.wait_ge(by_hi_ready, j + 1)
                V.tensor_tensor(flat(by_lo[:]), TP[:], flat(by_hi[:]).bitcast(F32), ALU.subtract).then_inc(y_split, 1)
                if not (last and q == 2):
                    inner(j + 1, (q + 1) % 3)
                if not (last and q >= 1):
                    select(j + 2, (q + 2) % 3)
                    u_lo_split(j + 2)
                gate(moe_tile(pair, h), q)

            select(0, 0)
            select(1, 1)
            u_lo_split(0)
            glu(0, 0)
            inner(0, 0)
            u_lo_split(1)
            with dve.Fori(0, NBLK // 6) as pair:
                for h in range(2):
                    flags = [dve.value_load(tab[0:1, 2, bass.ds(pair * 6 + (3 * h + q), 1)], min_val=0, max_val=1) for q in range(3)]
                    for q in range(3):
                        block_dve(pair, h, q, flags, False)
            flags = [dve.value_load(tab[0:1, 2, NBLK - 3 + q:NBLK - 2 + q], min_val=0, max_val=1) for q in range(2)]
            for q in range(3):
                block_dve(NBLK // 6, 0, q, flags, True)

            def weighted(b, tb):
                a, s_ = b * TB + tb, tb % 2
                og = out_slot(b, tb)
                dve.wait_ge(og_in[s_], 64 if b == 0 else 32 * (b * 2 + tb // 2 + 1))
                V.tensor_scalar(og[:, s_, 0, :], og[:, s_, 0, :], we[:, 0, bass.ds(a % NT, 1)], None, ALU.mult).then_inc(cb_first, 1)
                dve.wait_ge(cb_first, a + 1)
                V.scalar_tensor_tensor(og[:, s_, 0, :], og[:, s_, 1, :], we[:, 1, bass.ds(a % NT, 1)], og[:, s_, 0, :], ALU.mult,
                                       ALU.add).then_inc(cb_sum, 1)

            def combine(b, tb):
                a = b * TB + tb
                dve.wait_ge(cb_T, a + 1)
                xa_ = XT[:, :, bass.ds(a % NT * P, P)]
                V.tensor_tensor(xa_, xa_, CB[:].rearrange("p (k t) -> p k t", k=KC), ALU.add).then_inc(cb_done, 1)

            def gated_input(b, ffn=False):
                layer = 3 if ffn else 2
                k = layer * BATCH + b
                u = u_in[:, :, tok(b % BATCH)]
                dve.wait_ge(x_tanh, k + 1)
                dve.wait_ge(g_fetched[b], 16 * layer)
                V.scalar_tensor_tensor(u, u, 1.0, u_g[:, :, tok(b % BATCH)], ALU.add, ALU.mult).then_inc(u_ready, 1)
                dve.wait_ge(u_hi_ready, k - 2 * BATCH + 1)
                V.tensor_tensor(u_lo[:, :, tok(b % BATCH)], u, u_hi[:, :, tok(b % BATCH)].bitcast(F32), ALU.subtract).then_inc(u_split, 1)

            def k_lo_split(i):
                dve.wait_ge(k_hi_ready, i + 1)
                V.tensor_tensor(k_lo[:], PP[KV_BANK][:], k_hi[:].bitcast(F32), ALU.subtract).then_inc(k_split, 1)

            def v_lo_split(i):
                dve.wait_ge(v_hi_ready, i + 1)
                V.tensor_tensor(v_lo[:], TT_[0][:].rearrange("p (a d) -> p a d", a=TB), v_hi[:].bitcast(F32),
                                ALU.subtract).then_inc(v_split, 1)

            def q_lo_split(i, h):
                dve.wait_ge(q_hi_ready, HPG * i + h + 1)
                V.tensor_tensor(q_lo[:, h % 2, :], PP[Q_BANK[h]][:], q_hi[:, h % 2, :].bitcast(F32),
                                ALU.subtract).then_inc(q_split, 1)

            def row_max(i, h):
                dve.wait_ge(scores_done, HPG * i + h + 1)
                for qb in range(TB):
                    bk, c0, _ = S_AT[qb]
                    V.tensor_reduce(rinv[:, h % 2, qb:qb + 1], S_[bk][:, c0:c0 + (qb + 1) * P], AX.X,
                                    ALU.max).then_inc(max_part, 1)
                dve.wait_ge(max_part, TB * (HPG * i + h + 1))
                V.tensor_scalar(nmx[:, h % 2, :], rinv[:, h % 2, :], -SCALE, None, ALU.mult).then_inc(max_ready, 1)

            def normalise(i, h):
                dve.wait_ge(exp_done, FIRST + TB * (HPG * i + h + 1))
                dve.wait_ge(max_ready, HPG * i + h + 1)
                V.reciprocal(rinv[:, h % 2, :], rsum[:, h % 2, :]).then_inc(r_inv, 1)
                dve.wait_ge(r_inv, HPG * i + h + 1)
                for qb in range(TB):
                    pr = probs[:, h % 2, PR_AT[qb]:PR_AT[qb] + (qb + 1) * P]
                    V.tensor_scalar(pr, pr, rinv[:, h % 2, qb:qb + 1], None, ALU.mult).then_inc(p_ready, 1)

            def pt_lo_split(i, h, groups):
                for r in groups:
                    bk, w, c0 = T_GROUP[r]
                    dve.wait_ge(pt_hi_ready, 3 * (HPG * i + h) + r + 1)
                    V.tensor_tensor(pt_lo[:, c0:c0 + w], TT_[bk][:, 0:w], pt_hi[:, c0:c0 + w].bitcast(F32),
                                    ALU.subtract).then_inc(pt_split, 1)

            def ctx_lo(i, h):
                dve.wait_ge(c_hi_ready, HPG * i + h + 1)
                V.tensor_tensor(cx_lo[:, h, :], PP[C_BANK[h]][:], cx_hi[:, h, :].bitcast(F32),
                                ALU.subtract).then_inc(c_split, 1)

            def dense_add(i, m):
                dve.wait_ge(dense_done, KC * i + m + 1)
                xm = XT[:, m, tok(i % BATCH)]
                V.tensor_tensor(xm, xm, PP[D_BANK[m]][:], ALU.add).then_inc(ax_acc, 1)

            def batch_input(b):
                weighted(b, 0)
                for tb in range(TB):
                    if tb < TB - 1:
                        weighted(b, tb + 1)
                    combine(b, tb)
                gated_input(b)

            att_lo(dve, V, 1, 0)
            batch_input(0)
            k_lo_split(0)
            q_lo_split(0, 0)
            q_lo_split(0, 1)
            row_max(0, 0)
            normalise(0, 0)
            q_lo_split(0, 2)
            att_lo(dve, V, 1, 2)
            att_lo(dve, V, 1, 1)

            def att_dve(i, first, last):
                n = i + (G_ATT - A_GATE)

                def gate_before():
                    gate_inverse(dve, n - 1, a_ek[:], a_eu[:])

                def with_gate(part):
                    if not (first or last):
                        with dve.If(i >= A_GATE):
                            part()

                pt_lo_split(i, 0, (0, 1))
                row_max(i, 1)
                pt_lo_split(i, 0, (2,))
                if not first:
                    dense_add(i - 1, 0)
                normalise(i, 1)
                if last:
                    gate_before()
                elif not first:
                    with dve.If(i > A_GATE):
                        gate_before()
                if not first:
                    dense_add(i - 1, 1)
                v_lo_split(i)
                if not first:
                    dense_add(i - 1, 2)
                    dense_add(i - 1, 3)
                ctx_lo(i, 0)
                if first:
                    batch_input(1)
                pt_lo_split(i, 1, (0, 1))
                row_max(i, 2)
                pt_lo_split(i, 1, (2,))
                q_lo_split(i, 3)
                normalise(i, 2)
                ctx_lo(i, 1)
                pt_lo_split(i, 2, (0, 1))
                row_max(i, 3)
                pt_lo_split(i, 2, (2,))
                if not last:
                    k_lo_split(i + 1)
                    q_lo_split(i + 1, 0)
                normalise(i, 3)
                ctx_lo(i, 2)
                with_gate(lambda: gate_clamp(dve, n, a_ek[:], a_eu[:]))
                if not last:
                    q_lo_split(i + 1, 1)
                pt_lo_split(i, 3, (0, 1))
                with_gate(lambda: gate_scans(dve, n, a_ek[:], a_e[:], a_r1[:], a_r2[:]))
                if not last:
                    row_max(i + 1, 0)
                pt_lo_split(i, 3, (2,))
                if not last:
                    q_lo_split(i + 1, 2)
                    normalise(i + 1, 0)
                ctx_lo(i, 3)
                if first:
                    batch_input(2)
                elif not last:
                    with dve.If(i == 1):
                        batch_input(3)
                    for b in range(2):
                        with dve.If(i == NI - BATCH + 1 + b):
                            gated_input(b, True)

            att_dve(0, True, False)
            with dve.Fori(1, NI - 1) as i:
                att_dve(i, False, False)
            att_dve(NI - 1, False, True)
            def ffn_lo(s, par):
                dve.wait_ge(fw_hi_ready, s + 1)
                V.tensor_tensor(fw_lo[:, par, :], f_stage[:, par, :], fw_hi[:, par, :].bitcast(F32),
                                ALU.subtract).then_inc(fw_split, 1)

            def ffn_y(s, b):
                k = s * BATCH + b
                dve.wait_ge(f_tanh, k + 1)
                V.scalar_tensor_tensor(f_t[:], f_t[:], 1.0, FG[b % 2][:], ALU.add, ALU.mult).then_inc(f_used, 1)
                dve.wait_ge(f_lin, k + 1)
                dve.wait_ge(f_used, k + 1)
                V.tensor_tensor(f_y[:], f_t[:], f_u[:], ALU.mult).then_inc(f_yready, 1)
                dve.wait_ge(f_hi_ready, k + 1)
                V.tensor_tensor(f_lo[:, b % 2, :], f_y[:], f_hi[:, b % 2, :].bitcast(F32), ALU.subtract).then_inc(f_split, 1)

            def ffn_add(s, b):
                for m in range(KC):
                    dve.wait_ge(f_down, FIRST + KC * (s * BATCH + b) + m + 1)
                    xm = XT[:, m, b * T:(b + 1) * T]
                    V.scalar_tensor_tensor(xm, FD[m][:], col("down_s", m), xm, ALU.mult, ALU.add).then_inc(fx_acc, 1)

            def scales(s):
                V.tensor_scalar(f_sc[:, 0:1], gsh[:, bass.ds(s, 1)], 1.0, None, ALU.mult).then_inc(f_scaled, 1)
                V.tensor_scalar(f_sc[:, 1:2], ush[:, bass.ds(s, 1)], 1.0, None, ALU.mult).then_inc(f_scaled, 1)

            gated_input(2, True)
            scales(0)
            ffn_lo(0, 0)
            for m in range(KC):
                dense_add(NI - 1, m)
            gated_input(3, True)
            ffn_y(0, 0)

            def ffn_dve(s, par, last):
                for b in range(BATCH):
                    if b < BATCH - 1:
                        ffn_y(s, b + 1)
                        if b == BATCH - 2 and not last:
                            scales(s + 1)
                    elif not last:
                        ffn_y(s + 1, 0)
                    ffn_add(s, b)
                    if b == 1 and not last:
                        ffn_lo(s + 1, 1 - par)

            with dve.Fori(0, FS // 2) as it:
                ffn_dve(it * 2, 0, False)
                ffn_dve(it * 2 + 1, 1, False)
            ffn_dve(FS - 1, 0, True)

        @block.tensor
        def _(pe):
            for counted in (z_done, dn_done, c_done, f_down):
                pe.sem_inc(counted, FIRST)
            M = nc.tensor.matmul
            pe.wait_ge(masks_ready, N_MASKS)
            pe.wait_ge(loaded, 64)
            M(bank[0][:, 0:BATCH], ones[:], condT_s[:], start=True, stop=True).then_inc(setup_mm, 1)
            pe.wait_ge(w_loaded, 16)
            with pe.Fori(0, BATCH) as b:
                pe.wait_ge(u_ready, FIRST + b + 1)
                for tb in range(TB):
                    for k in range(KC):
                        mm = M(SM[:, tb * HEADS_M:(tb + 1) * HEADS_M], um[:, k, tb * P:(tb + 1) * P], w_in[:, k, DT_COL:IN_COLS],
                               start=(k == 0), stop=(k == KC - 1))
                mm.then_inc(dt_raw, 1)

                def project(dst, c0):
                    for k in range(KC):
                        mm = M(dst[:], w_in[:, k, c0:c0 + P], um[:, k, :], start=(k == 0), stop=(k == KC - 1))
                    return mm

                pe.wait_ge(dt_abs, b + 1)
                for q, ch in enumerate(CONV_ORDER):
                    if q >= 2:
                        pe.wait_ge(conv_tapped, N_CONV * b + q - 1)
                    project(PJ[q % 2], D_IN + ch * P).then_inc(proj_done, 1)
                    if q == 3:
                        pe.wait_ge(dA_ready, b + 1)
                        M(SM[:, 64:64 + NB], tri[:], d_A[:], start=True, stop=True)
                        M(SM[:, 128:128 + NB], ones[:], d_A[:], start=True, stop=True)
                        for tb in range(TB):
                            mm = M(EB[0:HEADS_M, tb * P:(tb + 1) * P], d_A[:, tb * HEADS_M:(tb + 1) * HEADS_M], tri[:],
                                   start=True, stop=True)
                        mm.then_inc(cs_done, 1)
                def sums(j):
                    if j:
                        pe.wait_ge(l_done, 9 * (PAIRS * b + j))
                    for hh in range(2):
                        M((R0, R1)[hh][:], ident_b[:], neg4[:].rearrange("p a l -> p (a l)"), start=True, stop=False)
                        M((R0, R1)[hh][:], sel_h[:, 2 * j + hh:2 * j + hh + 1].to_broadcast([64, P]), csT[:], start=False, stop=True)
                    M(EB[:], sel_p[:, j, :], csT[:], start=True, stop=True).then_inc(r_done, 1)

                def block_state(tb):
                    pe.wait_ge(xdt_done, TB * b + tb + 1)
                    pe.wait_ge(bc_copied, 2 * (TB * b + tb + 1))
                    if tb:
                        pe.wait_ge(state_done, (TB - 1) * b + tb)
                    for half in range(2):
                        mm = M(PJ[half][:], b_tok[:, tb, :], xdt2[:, half * 512:(half + 1) * 512], start=True, stop=True)
                    mm.then_inc(s_done, 1)

                for tb in range(TB):
                    o = slice(tb * P, (tb + 1) * P)
                    if tb >= 2:
                        pe.wait_ge(xdt_done, TB * b + tb - 1)
                    for ch in range(XC):
                        if tb == 0:
                            pe.wait_ge(act_ready, N_CONV * b + 2 + ch + 1)
                        mm = nc.tensor.transpose(XB[tb % 2][ch // 4][:, (ch % 4) * P:(ch % 4 + 1) * P], xa[:, ch, o], ident[:])
                    mm.then_inc(x_transposed, 1)
                    if tb:
                        pe.wait_ge(bc_copied, 2 * (TB * b + tb))
                    nc.tensor.transpose(SM[:, 192:320], bT[:, o], ident[:])
                    M(SM[:, 320:448], bT[:, o], cT[:, o], start=True, stop=True).then_inc(bc_done, 1)
                    if tb == TB - 1:
                        pe.wait_ge(ct_ready, b + 1)
                        pe.wait_ge(xdt_done, TB * b + TB - 1)
                        sums(0)
                    if tb:
                        block_state(tb - 1)

                def z_chunk(j):
                    if j >= 2:
                        pe.wait_ge(zs_done, PAIRS * b + j - 1)
                    else:
                        pe.wait_ge(state_done, (TB - 1) * (b + 1))
                    project(PJ[j % 2], j * P).then_inc(z_done, 1)

                z_chunk(0)
                z_chunk(1)
                pe.wait_ge(xdt_done, TB * (b + 1))
                sums(1)
                pe.wait_ge(bc_copied, 2 * TB * (b + 1))
                for j in range(PAIRS):
                    pe.wait_ge(m_ready, 2 * (PAIRS * b + j + 1))
                    if j:
                        pe.wait_ge(y_done, PAIRS * b + j)
                    for hh in range(2):
                        for tb in range(TB):
                            M(YD[hh * HD:(hh + 1) * HD, tb * P:(tb + 1) * P], xdt[:, tb, (2 * j + hh) * HD:(2 * j + hh + 1) * HD],
                              lm[:, j % 2, hh, tb * P:(tb + 1) * P], start=True, stop=True)
                    for tb in range(1, TB):
                        mm = M(YO[:, tb * P:(tb + 1) * P], state[:, tb - 1, j * P:(j + 1) * P], cT[:, tb * P:(tb + 1) * P],
                               start=True, stop=True)
                    mm.then_inc(yy_done, 1)
                    if j < PAIRS - 2:
                        z_chunk(j + 2)
                        sums(j + 2)
                    if j:
                        pe.wait_ge(sq_done, PAIRS * b + j)
                        M(SM[:], ones[:], sq[:, (j - 1) % 2, :], start=(j == 1), stop=False).then_inc(sq_added, 1)
                pe.wait_ge(wo_scaled, XC)
                pe.wait_ge(zs_done, PAIRS * (b + 1))
                pe.wait_ge(l_done, 9 * PAIRS * (b + 1))
                for m in range(KC):
                    for j in range(XC):
                        if m == 0:
                            pe.wait_ge(y_done, PAIRS * b + j + 1)
                        if m == 1 and j == XC // 2:
                            pe.wait_ge(sq_done, PAIRS * (b + 1))
                            M(SM[:], ones[:], sq[:, 1, :], start=False, stop=True).then_inc(ssq_done, 1)
                        mm = M(OB[m][:], w_out[:, j, m * P:(m + 1) * P], xa[:, j, :], start=(j == 0), stop=(j == XC - 1))
                    mm.then_inc(out_done, 1)
            def transposed(out, src, dim=P):
                return nc.tensor.transpose(out, src, ident[0:dim, 0:dim])

            pe.wait_ge(x_added, KC * BATCH)
            for b in range(BATCH):
                pe.wait_ge(u_ready, FIRST + BATCH + b + 1)
                for kc in range(KC):
                    mm = M(LGT[b % 2][0:E, :], gw[:, kc, :], uf1[:, b, kc, :], start=(kc == 0), stop=(kc == KC - 1))
                mm.then_inc(lgt_done, 1)
                for tb in range(TB):
                    a = b * TB + tb
                    if a >= 4:
                        pe.wait_ge(ut_copied[a % 2], (a - 4) // 2 + 1)
                    for kc in range(KC):
                        mm = transposed(UT[tb][:, kc * P:(kc + 1) * P], uf1[:, b, kc, tb * P:(tb + 1) * P])
                    mm.then_inc(ut_T, 1)
                pe.wait_ge(lgt_copied, b + 1)
                for tb in range(TB):
                    a = b * TB + tb
                    mm = transposed(LGP[:, a * E:(a + 1) * E], lgT[:, b % 2, tb * P:(tb + 1) * P], E)
                if b == BATCH - 1:
                    mm.then_inc(route_mm, 1)
                else:
                    mm.then_inc(lgt_used, 1)
            pe.wait_ge(moe_loaded, 48)
            pe.wait_ge(route_vec, MASK_READY)
            gt2 = gt[:].rearrange("p a e -> p (a e)")
            M(LGP[:, 128:256], rc[:, RC["before"]:RC["before"] + P], gt2, start=True, stop=True).then_inc(route_mm, 1)
            M(LGP[:, 256:384], ones[:], gt2, start=True, stop=True).then_inc(route_mm, 1)
            pe.wait_ge(route_vec, ONEHOT_READY)
            for c in range(2 * NT):
                mm = M(LGP[:, 0:2 * NBLK], oh_r[:, c, :], oh_v[:, c].rearrange("p v j -> p (v j)"), start=(c == 0), stop=(c == 2 * NT - 1))
            mm.then_inc(route_mm, 1)

            def product(out, x_hi, x_lo, slot, c0, q, bias):
                M(out, sel_e[:, q, :], bias_r[:, bias:bias + C], start=True, stop=False)
                for kc in range(KC):
                    o = slice(c0 + kc * C, c0 + (kc + 1) * C)
                    hi, lo = ((mw[:, slot, i, o] if isinstance(slot, int) else mw[:, bass.ds(slot, 1), i, o].rearrange("p o w -> p (o w)"))
                              for i in range(2))
                    M(out, x_hi[:, kc, :], hi, start=False, stop=False)
                    M(out, x_hi[:, kc, :], lo, start=False, stop=False)
                    mm = M(out, x_lo[:, kc, :], hi, start=False, stop=(kc == KC - 1))
                return mm

            def up_glu(j, q, e, slot):
                pe.wait_ge(bu_split, j + 1)
                pe.wait_ge(sel_ready, j + 1)
                pe.wait_ge(w_split, M_PIECES * e + 1)
                product(UG[q][:], bu_hi, bu_lo, slot, 0, q, 0).then_inc(g_done, 1)

            def up_lin(j, q, e, slot):
                pe.wait_ge(w_split, M_PIECES * e + 2)
                product(UL[q][:], bu_hi, bu_lo, slot, M_PIECE, q, I_MOE).then_inc(l2_done, 1)

            def inputs_T(j, q, it):
                pe.wait_ge(gathered[q], 16 * (it + 1))
                for kc in range(KC):
                    mm = transposed(TP[:, kc * P:(kc + 1) * P], ug[:, q, kc * P:(kc + 1) * P])
                mm.then_inc(tu_done, 1)

            def block_pe(it, q, last):
                j = it * 3 + q
                e0 = pe.value_load(tab[0:1, 0, j:j + 1] if last else tab[0:1, 0, bass.ds(j, 1)], min_val=0, max_val=E - 1)
                if not (last and q == 2):
                    e1 = pe.value_load(tab[0:1, 0, j + 1:j + 2] if last else tab[0:1, 0, bass.ds(j + 1, 1)], min_val=0, max_val=E - 1)
                    up_glu(j + 1, (q + 1) % 3, e1, e1 % 2)
                pe.wait_ge(y_ready, j + 1)
                for kc in range(KC):
                    mm = transposed(TP[:, kc * P:(kc + 1) * P], m_y[:, kc * P:(kc + 1) * P])
                mm.then_inc(ty_done, 1)
                if not (last and q == 2):
                    up_lin(j + 1, (q + 1) % 3, e1, e1 % 2)
                pe.wait_ge(y_split, j + 1)
                if not (last and q >= 1):
                    inputs_T(j + 2, (q + 2) % 3, it + (q + 2) // 3)
                pe.wait_ge(w_split, M_PIECES * (e0 + 1))
                pe.wait_ge(out_copied, FIRST + j)
                product(DN[:], by_hi, by_lo, e0 % 2, 2 * M_PIECE, q, 2 * I_MOE).then_inc(dn_done, 1)

            pe.wait_ge(route_vec, TAB_READY)
            inputs_T(0, 0, 0)
            up_glu(0, 0, 0, 0)
            up_lin(0, 0, 0, 0)
            pe.wait_ge(bu_split, 1)
            inputs_T(1, 1, 0)
            with pe.Fori(0, NBLK // 3 - 1) as it:
                for q in range(3):
                    block_pe(it, q, False)
            for q in range(3):
                block_pe(NBLK // 3 - 1, q, True)

            def combine_T(b, tb):
                a, s_ = b * TB + tb, tb % 2
                pe.wait_ge(cb_sum, a + 1)
                if not (isinstance(a, int) and a == 0):
                    pe.wait_ge(cb_done, a)
                for kc in range(KC):
                    mm = transposed(CB[:, kc * P:(kc + 1) * P], out_slot(b, tb)[:, s_, 0, kc * P:(kc + 1) * P])
                mm.then_inc(cb_T, 1)

            def project(dst, at, b):
                for kc in range(KC):
                    o = slice(at + kc * P, at + (kc + 1) * P)
                    mm = three(dst[:], aw_hi[:, o], aw_lo[:, o], u_hi[:, kc, tok(b)], u_lo[:, kc, tok(b)], kc == 0, kc == KC - 1)
                return mm

            def keys(i):
                pe.wait_ge(aw_split[0], i // BATCH + 1)
                project(PP[KV_BANK], A_K, i % BATCH).then_inc(k_done, 1)

            def values(i):
                pe.wait_ge(q_split, HPG * i + 2)
                project(PP[KV_BANK], A_V, i % BATCH).then_inc(v_done, 1)

            def query(i, h):
                if h == 3:
                    pe.wait_ge(aw_split[2], i // BATCH + 1)
                project(PP[Q_BANK[h]], A_Q + h * C, i % BATCH).then_inc(q_done, 1)

            def values_T(i):
                pe.wait_ge(vt_copied, i + 1)
                pe.wait_ge(pt_split, FIRST + 3 * (HPG * i + 1))
                for tb in range(TB):
                    mm = transposed(TT_[0][:, tb * P:(tb + 1) * P], vT[:, tb * P:(tb + 1) * P])
                mm.then_inc(vt_done, 1)

            def scores(i, h):
                if h == 0:
                    pe.wait_ge(k_split, i + 1)
                pe.wait_ge(q_split, HPG * i + h + 1)
                pe.wait_ge(exp_done, FIRST + TB * (HPG * i + h))
                for qb in range(TB - 1, -1, -1):
                    bk, c0, w = S_AT[qb]
                    qs = slice(qb * P, (qb + 1) * P)
                    three(S_[bk][:, c0:c0 + w], q_hi[:, h % 2, qs], q_lo[:, h % 2, qs], k_hi[:, 0:w], k_lo[:, 0:w], True, False)
                    mm = M(S_[bk][:, c0 + qb * P:c0 + (qb + 1) * P], ident_b[:], causal_b[:], start=False, stop=True)
                mm.then_inc(scores_done, 1)

            def transposes(i, h, groups):
                pe.wait_ge(p_ready, TB * (HPG * i + h + 1))
                for r in groups:
                    if r == 2:
                        pe.wait_ge(pt_split, FIRST + 3 * (HPG * i + h) + 1)
                    for kb, c0 in (((0, 0),), ((1, 0), (3, 384)), ((2, 0),))[r]:
                        for qb in range(kb, TB):
                            o = PR_AT[qb] + kb * P
                            mm = transposed(TT_[T_GROUP[r][0]][:, c0 + (qb - kb) * P:c0 + (qb - kb + 1) * P], probs[:, h % 2, o:o + P])
                    mm.then_inc(t_done, 1)

            def context(i, h):
                if h == 0:
                    pe.wait_ge(v_split, i + 1)
                pe.wait_ge(pt_split, FIRST + 3 * (HPG * i + h + 1))
                for kb in range(TB):
                    o, w = PT_AT[kb]
                    mm = three(PP[C_BANK[h]][:, kb * P:T], v_hi[:, kb, :], v_lo[:, kb, :], pt_hi[:, o:o + w], pt_lo[:, o:o + w],
                               kb == 0, kb == TB - 1)
                mm.then_inc(c_done, 1)

            def dense(i, m):
                for h in range(HPG):
                    o = slice(A_D + h * C + m * P, A_D + h * C + (m + 1) * P)
                    mm = three(PP[D_BANK[m]][:], aw_hi[:, o], aw_lo[:, o], cx_hi[:, h, :], cx_lo[:, h, :], h == 0, h == HPG - 1)
                mm.then_inc(dense_done, 1)

            def batch_T(b):
                for tb in range(TB):
                    combine_T(b, tb)
                pe.wait_ge(cb_done, TB * (b + 1))

            batch_T(0)
            pe.wait_ge(u_split, 1)
            keys(0)
            query(0, 0)
            pe.wait_ge(k_split, 1)
            query(0, 1)
            scores(0, 0)
            query(0, 2)
            values(0)
            transposes(0, 0, (0, 1))

            def att_pe(i, first, last):
                scores(i, 1)
                transposes(i, 0, (2,))
                if not first:
                    pe.wait_ge(aw_split[1], (i - 1) // BATCH + 1)
                    pe.wait_ge(c_split, HPG * i)
                    dense(i - 1, 0)
                    pe.wait_ge(vt_copied, i + 1)
                    dense(i - 1, 1)
                values_T(i)
                if not first:
                    pe.wait_ge(q_split, HPG * i + 3)
                    dense(i - 1, 2)
                    pe.wait_ge(ax_acc, FIRST + KC * (i - 1) + 1)
                    dense(i - 1, 3)
                    pe.wait_ge(ax_acc, FIRST + KC * (i - 1) + 2)
                context(i, 0)
                if first:
                    batch_T(1)
                transposes(i, 1, (0, 1))
                scores(i, 2)
                transposes(i, 1, (2,))
                if first:
                    pe.wait_ge(q_split, 3)
                else:
                    pe.wait_ge(ax_acc, FIRST + KC * (i - 1) + 3)
                query(i, 3)
                if not first:
                    pe.wait_ge(ax_acc, FIRST + KC * i)
                context(i, 1)
                if not last:
                    if first:
                        pe.wait_ge(u_split, 2)
                    else:
                        with pe.If(i < BATCH - 1):
                            pe.wait_ge(u_split, i + 2)
                    pe.wait_ge(c_split, HPG * i + 1)
                    keys(i + 1)
                transposes(i, 2, (0, 1))
                scores(i, 3)
                transposes(i, 2, (2,))
                if not last:
                    pe.wait_ge(q_split, HPG * i + 4)
                    query(i + 1, 0)
                pe.wait_ge(c_split, HPG * i + 2)
                context(i, 2)
                if not last:
                    pe.wait_ge(k_split, i + 2)
                    query(i + 1, 1)
                transposes(i, 3, (0, 1))
                if not last:
                    scores(i + 1, 0)
                transposes(i, 3, (2,))
                if not last:
                    query(i + 1, 2)
                pe.wait_ge(c_split, HPG * i + 3)
                context(i, 3)
                if not last:
                    values(i + 1)
                    if first:
                        batch_T(2)
                    else:
                        with pe.If(i == 1):
                            batch_T(3)
                    transposes(i + 1, 0, (0, 1))

            att_pe(0, True, False)
            with pe.Fori(1, NI - 1) as i:
                att_pe(i, False, False)
            att_pe(NI - 1, False, True)
            pe.wait_ge(c_split, HPG * NI)
            dense(NI - 1, 0)
            dense(NI - 1, 1)
            dense(NI - 1, 2)
            pe.wait_ge(ax_acc, FIRST + KC * (NI - 1) + 1)
            dense(NI - 1, 3)
            pe.wait_ge(exp_done, FIRST + TB * HPG * NI)
            pe.wait_ge(pt_split, FIRST + 3 * HPG * NI)

            def ffn_up(s, par, b):
                k = s * BATCH + b
                if b == 0:
                    pe.wait_ge(fw_split, FIRST + s + 1)
                if par == 0:
                    pe.wait_ge(u_split, BATCH + b + 1)
                if not (isinstance(s, int) and s == 0 and b < 2):
                    pe.wait_ge(f_yready, FIRST + k - 1)
                x = slice(b * T, (b + 1) * T)
                for dst, gu in ((FG[b % 2], 0), (FU[b % 2], 1)):
                    for kc in range(KC):
                        o = slice(kc * 256 + gu * P, kc * 256 + (gu + 1) * P)
                        mm = three(dst[:], fw_hi[:, par, o], fw_lo[:, par, o], u_hi[:, kc, x], u_lo[:, kc, x], kc == 0, kc == KC - 1)
                mm.then_inc(f_up, 1)

            def ffn_down(s, par, b):
                k = s * BATCH + b
                if par == 0 and b == 0:
                    pe.wait_ge(ax_acc, FIRST + KC * NI)
                pe.wait_ge(f_split, FIRST + k + 1)
                pe.wait_ge(fx_acc, FIRST + KC * k)
                for m in range(KC):
                    o = slice(FFN_UP + m * P, FFN_UP + (m + 1) * P)
                    three(FD[m][:], fw_hi[:, par, o], fw_lo[:, par, o], f_hi[:, b % 2, :], f_lo[:, b % 2, :], True, True).then_inc(f_down, 1)

            ffn_up(0, 0, 0)

            def ffn_pe(s, par, last):
                for b in range(BATCH):
                    if b < BATCH - 1:
                        ffn_up(s, par, b + 1)
                    elif not last:
                        ffn_up(s + 1, 1 - par, 0)
                    ffn_down(s, par, b)

            with pe.Fori(0, FS // 2) as it:
                ffn_pe(it * 2, 0, False)
                ffn_pe(it * 2 + 1, 1, False)
            ffn_pe(FS - 1, 0, True)


_SHAPES = dict(xT=(C, BATCH * T), fT=(TILES, P, T), condT=(P, BATCH), cols=(P, N_COLS), rows=(P, N_ROWS),
               w_in=(P, KC, IN_COLS), w_out=(P, XC, C), moe=(E, P, MOE_W), gw=(P, KC, E), bias=(E, 2 * I_MOE + C), rc=(P, N_RC),
               att=(GROUPS, P, ATT_W), ffn=(FS, P, FFN_W))


def routing_constants():
    one = np.ones((P, 1), np.float32)
    n = np.arange(P)
    parts = dict(iota=one * n, before=n[:, None] < n[None, :], rst=one * (np.arange(NT * E) % E > 0),
                 rst2=one * (np.arange(NT * E) % NT > 0), full=one * np.where(np.arange(NT) == 0, -1, P * np.arange(NT)),
                 blk=one * (np.arange(2 * NT) % NT), place=n[:, None], row=n[:, None] % 32)
    return np.concatenate([parts[k] for k in RC], axis=1).astype(np.float32)


def lay_out(i):
    i = {k: np.asarray(v) for k, v in i.items()}
    chunks = lambda v: v.reshape(-1, P).T
    b1 = i["L0_ffn_b1"].reshape(E, I_MOE, 2)
    gates = ("L0_cond", "L0_cond2", "L1_cond", "L1_cond2")
    conv = i["L0_attn_conv_w"].reshape(N_CONV, P, 4).transpose(1, 0, 2).reshape(P, -1)
    d_skip = np.repeat(i["L0_attn_D_skip"], HD)
    cols = np.concatenate(
        [chunks(i[g + "_u"]) for g in gates] + [chunks(i[g + "_w"]) for g in gates]
        + [conv, chunks(i["L0_attn_conv_b"]), chunks(i["L0_attn_norm_w"]), chunks(d_skip),
           chunks(i["L1_ffn_gate_s"]), chunks(i["L1_ffn_up_s"]), chunks(i["L1_ffn_down_s"])], axis=1)
    row = np.concatenate([i["L0_attn_dt_bias"], i["L0_attn_A_log"], i["L0_ffn_gate_b"]])
    w1 = i["L0_ffn_w1"].reshape(E, I_MOE, 2, KC, P).transpose(0, 4, 2, 3, 1).reshape(E, P, 2 * M_PIECE)
    w2 = i["L0_ffn_w2"].reshape(E, C, I_MOE // P, P).transpose(0, 3, 2, 1).reshape(E, P, M_PIECE)
    wq = i["L1_attn_w_q"].reshape(KC, P, GROUPS, HPG, DH).transpose(2, 1, 3, 0, 4).reshape(GROUPS, P, -1)
    wkv = i["L1_attn_w_kv"].reshape(KC, P, 2, GROUPS, DH).transpose(2, 3, 1, 0, 4).reshape(2, GROUPS, P, -1)
    wd = i["L1_attn_w_dense"].reshape(GROUPS, HPG, DH, C).transpose(0, 2, 1, 3).reshape(GROUPS, P, -1)
    up = np.stack([i["L1_ffn_gate_w"], i["L1_ffn_up_w"]]).reshape(2, FS, P, KC, P).transpose(1, 4, 3, 0, 2).reshape(FS, P, -1)
    down = i["L1_ffn_down_w"].reshape(C, FS, P).transpose(1, 2, 0)
    out = dict(
        xT=i["x"].transpose(2, 0, 1).reshape(C, -1),
        fT=i["fside_BxSxS_0"].transpose(0, 2, 1).reshape(TILES, P, T),
        condT=i["cond_512"].T, cols=cols, rows=np.broadcast_to(row, (P, N_ROWS)),
        w_in=i["L0_attn_in_proj_w"].T.reshape(KC, P, IN_COLS).transpose(1, 0, 2),
        w_out=i["L0_attn_out_proj_w"].T.reshape(XC, P, C).transpose(1, 0, 2),
        moe=np.concatenate([w1, w2], axis=2), gw=i["L0_ffn_gate_w"].T.reshape(KC, P, E).transpose(1, 0, 2),
        bias=np.concatenate([b1[..., 0], b1[..., 1], i["L0_ffn_b2"]], axis=1), rc=routing_constants(), att=np.concatenate([wkv[0], wkv[1], wq, wd], axis=2), ffn=np.concatenate([up, down], axis=2))
    return {k: np.ascontiguousarray(v) for k, v in out.items()}


def build(nc):
    aps = [nc.dram_tensor(f"in_{n}", s, F32, kind="ExternalInput").ap() for n, s in _SHAPES.items()]
    out = nc.dram_tensor("outT", (C, BATCH * T), F32, kind="ExternalOutput").ap()
    network(nc, *aps, out)


def kernel(**inputs):
    import concourse.bacc as bacc
    from concourse.bass_utils import run_bass_kernel_spmd

    nc = bacc.Bacc("TRN2", target_bir_lowering=False, num_devices=1)
    build(nc)
    arrays = {f"in_{k}": v for k, v in lay_out(inputs).items()}
    r = run_bass_kernel_spmd(nc, [arrays], core_ids=[0])
    return np.ascontiguousarray(r.results[0]["outT"].reshape(C, BATCH, T).transpose(1, 2, 0))
```
